# Optimizing a Trainium2 kernel written in Bass

```python
import numpy as np
import jax
import jax.numpy as jnp

def _softmax(x, axis=-1):
    return jax.nn.softmax(x, axis=axis)

def _gelu(x):
    return jax.nn.gelu(x, approximate=True)

def _silu(x):
    return jax.nn.silu(x)

def _sigmoid(x):
    return jax.nn.sigmoid(x)

def _layernorm(x, axis=-1, eps=1e-05):
    m = jnp.mean(x, axis=axis, keepdims=True)
    v = jnp.var(x, axis=axis, keepdims=True)
    return (x - m) / jnp.sqrt(v + eps)

def _scatter_add(tgt, idx, src, axis=0):
    return tgt.at[idx].add(src)

def _segment_sum(src, seg, n):
    return jax.ops.segment_sum(src, seg, n)
kernel_name = 'mk_adaln_attn_ffn_d2_seqx_r4_f44188'

def setup_inputs(seed: int=0):
    np.random.seed(seed)
    _w = jnp.asarray

    def _rec_inputs():
        import jax
        import jax.numpy as jnp
        _rk = jax.random.key(seed)
        x = -0.0002071 + 1 * jax.random.normal(jax.random.fold_in(_rk, 1), (2, 1024, 256), jnp.float32)
        _lenS = 1024 - jax.random.randint(jax.random.fold_in(_rk, 7), (2,), 0, max(1, 1024 // 4) + 1, jnp.int32)
        _lenS2 = 1024 - jax.random.randint(jax.random.fold_in(_rk, 8), (2,), 0, max(1, 1024 // 4) + 1, jnp.int32)
        cond_8 = jax.random.uniform(jax.random.fold_in(_rk, 11), (2, 8), jnp.float32, 0.0, 0.983423)
        return (x, cond_8)
    x, cond_8 = _rec_inputs()

    def _L0_cond_setup():
        import jax, jax.numpy as jnp
        import numpy as np
        R = 16
        ALPHA = 32.0
        SCALING = ALPHA / R
        key = jax.random.key(seed)
        ks = jax.random.split(key, 6)
        B, T, C, O, E = (16, 375, 256, 256, 8)
        x = jax.random.normal(ks[0], (B, T, C), dtype=jnp.float32)
        w = jax.random.uniform(ks[1], (B, E), dtype=jnp.float32)
        W_base = jax.random.normal(ks[2], (O, C), dtype=jnp.float32) * 0.02
        b_base = jax.random.normal(ks[3], (O,), dtype=jnp.float32) * 0.02
        As = jax.random.normal(ks[4], (E, R, C), dtype=jnp.float32) * 0.02
        Bs = jax.random.normal(ks[5], (E, O, R), dtype=jnp.float32) * 0.02
        return {'x': x, 'w': w, 'W_base': W_base, 'b_base': b_base, 'As': As, 'Bs': Bs}
    _L0_cond_all = _L0_cond_setup()
    _L0_cond_in = {k: v for k, v in _L0_cond_all.items() if k in ('W_base', 'b_base', 'As', 'Bs')}
    del _L0_cond_all

    def _L0_attn_setup():
        import jax, jax.numpy as jnp
        import numpy as np
        D_MODEL = 256
        N_HEADS = 16
        HEAD_DIM = D_MODEL // N_HEADS
        key = jax.random.key(seed)
        kx, kq, kk, kv, ko = jax.random.split(key, 5)
        s = 1.0 / np.sqrt(D_MODEL)
        return {'x': jax.random.normal(kx, (4, 512, D_MODEL), dtype=jnp.float32), 'Wq': jax.random.normal(kq, (D_MODEL, D_MODEL), dtype=jnp.float32) * s, 'Wk': jax.random.normal(kk, (D_MODEL, D_MODEL), dtype=jnp.float32) * s, 'Wv': jax.random.normal(kv, (D_MODEL, D_MODEL), dtype=jnp.float32) * s, 'Wo': jax.random.normal(ko, (D_MODEL, D_MODEL), dtype=jnp.float32) * s}
    _L0_attn_all = _L0_attn_setup()
    _L0_attn_in = {k: v for k, v in _L0_attn_all.items() if k in ('Wq', 'Wk', 'Wv', 'Wo')}
    del _L0_attn_all

    def _L0_cond2_setup():
        import jax, jax.numpy as jnp
        import numpy as np
        TOP_K = 2
        NUM_MOE_LAYERS = 12

        def _gemma_mlp(x, gate_w, up_w, down_w):
            g = jnp.einsum('bsh,hi->bsi', x, gate_w)
            u = jnp.einsum('bsh,hi->bsi', x, up_w)
            return jnp.einsum('bsi,ih->bsh', jax.nn.gelu(g, approximate=True) * u, down_w)
        key = jax.random.key(seed)
        ks = jax.random.split(key, 8)
        B, S, H, I, E = (32, 64, 256, 1024, 8)
        std = 0.02
        return {'x': jax.random.normal(ks[0], (B, S, H), jnp.float32), 'router_logits': jax.random.normal(ks[1], (B, E), jnp.float32), 'skill_gate': jax.random.normal(ks[2], (E, H, I), jnp.float32) * std, 'skill_up': jax.random.normal(ks[3], (E, H, I), jnp.float32) * std, 'skill_down': jax.random.normal(ks[4], (E, I, H), jnp.float32) * std, 'shared_gate': jax.random.normal(ks[5], (H, I), jnp.float32) * std, 'shared_up': jax.random.normal(ks[6], (H, I), jnp.float32) * std, 'shared_down': jax.random.normal(ks[7], (I, H), jnp.float32) * std}
    _L0_cond2_all = _L0_cond2_setup()
    _L0_cond2_in = {k: v for k, v in _L0_cond2_all.items() if k in ('skill_gate', 'skill_up', 'skill_down', 'shared_gate', 'shared_up', 'shared_down')}
    del _L0_cond2_all

    def _L0_ffn_setup():
        import jax, jax.numpy as jnp
        import numpy as np
        B, N, D = (4, 512, 256)
        SPARSITY = 0.01
        key = jax.random.key(seed)
        k1, k2, k3 = jax.random.split(key, 3)
        x = jax.random.normal(k1, (B, N, D), dtype=jnp.float32)
        spatial = jax.random.normal(k2, (D, D), dtype=jnp.float32) * 0.02
        freq = jnp.fft.fft(spatial, axis=-1)
        k = int(D * SPARSITY)
        mag = jnp.abs(freq)
        kth = jax.lax.top_k(mag, k)[0][:, -1:]
        w_sparse = jnp.where(mag >= kth, freq, 0.0 + 0j)
        bias = jax.random.normal(k3, (D,), dtype=jnp.float32) * 0.01
        return {'x': x, 'w_freq_real': jnp.real(w_sparse).astype(jnp.float32), 'w_freq_imag': jnp.imag(w_sparse).astype(jnp.float32), 'bias': bias}
    _L0_ffn_all = _L0_ffn_setup()
    _L0_ffn_in = {k: v for k, v in _L0_ffn_all.items() if k in ('w_freq_real', 'w_freq_imag', 'bias')}
    del _L0_ffn_all

    def _L1_cond_setup():
        import jax, jax.numpy as jnp
        import numpy as np
        B, S, D = (16, 512, 256)
        E, H = (8, 512)
        key = jax.random.key(seed)
        ks = jax.random.split(key, 8)
        scale = 0.02
        x = jax.random.normal(ks[0], (B, S, D), dtype=jnp.float32)
        opcode_onehot = jax.random.uniform(ks[1], (B, E), dtype=jnp.float32)
        W_up = jax.random.normal(ks[2], (E, H, D), dtype=jnp.float32) * scale
        b_up = jnp.zeros((E, H), dtype=jnp.float32)
        W_gate = jax.random.normal(ks[3], (E, H, D), dtype=jnp.float32) * scale
        b_gate = jnp.zeros((E, H), dtype=jnp.float32)
        W_down = jax.random.normal(ks[4], (E, D, H), dtype=jnp.float32) * scale
        b_down = jnp.zeros((E, D), dtype=jnp.float32)
        return {'x': x, 'opcode_onehot': opcode_onehot, 'W_up': W_up, 'b_up': b_up, 'W_gate': W_gate, 'b_gate': b_gate, 'W_down': W_down, 'b_down': b_down}
    _L1_cond_all = _L1_cond_setup()
    _L1_cond_in = {k: v for k, v in _L1_cond_all.items() if k in ('W_up', 'b_up', 'W_gate', 'b_gate', 'W_down', 'b_down')}
    del _L1_cond_all

    def _L1_attn_setup():
        import jax, jax.numpy as jnp
        import numpy as np
        B, S, DM, DI, H = (2, 512, 256, 512, 32)
        HD = DI // H
        G = 32

        def _forward(x, in_proj_W, in_proj_b, conv_w, conv_b, dyn_W, dyn_b, dt_c, selB_W, selC_W, seldt_W, beta_W, beta_b, rg_W, rg_b, ug_W, ug_b, Q_W, out_W, D, rms_w, gn_w, gn_b):
            b, s, _ = x.shape
            residual = x
            xn = x * jax.lax.rsqrt(jnp.mean(x * x, -1, keepdims=True) + 1e-06) * rms_w
            proj = xn @ in_proj_W.T + in_proj_b
            z = proj[..., :DI]
            K = proj[..., DI:3 * DI].reshape(b, s, DI, 2)
            V = proj[..., 3 * DI:]
            vc = jax.lax.conv_general_dilated(V.transpose(0, 2, 1), conv_w[:, None, :], (1,), [(3, 0)], feature_group_count=DI, dimension_numbers=('NCH', 'OIH', 'NCH'))
            u = jax.nn.silu(vc + conv_b[None, :, None]).transpose(0, 2, 1)
            dyn = u @ dyn_W.T + dyn_b
            alpha = jax.nn.softplus(dyn[..., :H])
            omega = dyn[..., H:2 * H] + dyn[..., 2 * H:3 * H]
            rope = 1.0 / 10000.0 ** (jnp.arange(H, dtype=jnp.float32) / H)
            omega = omega + jnp.arange(s, dtype=jnp.float32)[None, :, None] * rope
            dt = jax.nn.softplus(dt_c) / (alpha + jnp.abs(omega) + 0.0001)
            dt = dt + jax.nn.softplus(u @ seldt_W.T)
            sel_B = (u @ selB_W.T).reshape(b, s, H, 1, 2)
            sel_C = (u @ selC_W.T).reshape(b, s, H, 1, 2)
            Kh = K.reshape(b, s, H, HD, 2) * sel_B
            a = 0.5 * dt * alpha
            w = 0.5 * dt * omega
            det = (1.0 + a) ** 2 + w * w
            lam2 = ((1.0 - a) ** 2 + w * w) / det
            r_gate = jax.nn.sigmoid(u @ rg_W.T + rg_b)
            vp = jnp.sqrt(jnp.clip(1.0 - lam2 ** r_gate, 1e-06))
            u_gate = jax.nn.sigmoid(u @ ug_W.T + ug_b)
            Vg = u.reshape(b, s, H, HD) * (vp * u_gate)[..., None]
            Q = (u @ Q_W.T).reshape(b, s, H, HD, 2) * sel_C
            beta = jax.nn.sigmoid(u @ beta_W.T + beta_b)
            A11 = (1.0 - a * a - w * w) / det
            A12 = 2.0 * w / det

            def step(Sc, inp):
                a11, a12, bt, k, v = inp
                S0, S1 = (Sc[..., 0], Sc[..., 1])
                r0 = a11[..., None] * S0 + a12[..., None] * S1
                r1 = -a12[..., None] * S0 + a11[..., None] * S1
                Sr = jnp.stack([r0, r1], -1)
                err = v - jnp.sum(k * Sr, -1)
                Sn = Sr + bt[..., None, None] * err[..., None] * k
                return (Sn, Sn)
            xs = (jnp.swapaxes(A11, 0, 1), jnp.swapaxes(A12, 0, 1), jnp.swapaxes(beta, 0, 1), jnp.swapaxes(Kh, 0, 1), jnp.swapaxes(Vg, 0, 1))
            S0 = jnp.zeros((b, H, HD, 2), x.dtype)
            _, Y = jax.lax.scan(step, S0, xs)
            Y = jnp.moveaxis(Y, 0, 1)
            y = jnp.sum(Q * Y, -1).reshape(b, s, DI)
            yg = y.transpose(0, 2, 1).reshape(b, G, DI // G, s)
            mu = jnp.mean(yg, (2, 3), keepdims=True)
            var = jnp.var(yg, (2, 3), keepdims=True)
            yg = (yg - mu) * jax.lax.rsqrt(var + 1e-05)
            y = (yg.reshape(b, DI, s) * gn_w[None, :, None] + gn_b[None, :, None]).transpose(0, 2, 1)
            y = y * jax.nn.silu(z)
            y = y + D * u
            return residual + y @ out_W.T
        key = jax.random.key(seed)
        ks = list(jax.random.split(key, 12))
        r = lambda k, shp, std: jax.random.normal(k, shp, jnp.float32) * std
        sel_std = 1.0 / float(np.sqrt(DI))
        return dict(x=jax.random.normal(ks[0], (B, S, DM), jnp.float32), in_proj_W=r(ks[1], (4 * DI, DM), 0.02), in_proj_b=jnp.zeros((4 * DI,), jnp.float32), conv_w=r(ks[2], (DI, 4), 0.3), conv_b=jnp.zeros((DI,), jnp.float32), dyn_W=r(ks[3], (3 * H, DI), 0.02), dyn_b=jnp.zeros((3 * H,), jnp.float32), dt_c=jnp.full((H,), 0.5, jnp.float32), selB_W=r(ks[4], (2 * H, DI), sel_std), selC_W=r(ks[5], (2 * H, DI), sel_std), seldt_W=r(ks[6], (H, DI), sel_std), beta_W=r(ks[7], (H, DI), sel_std), beta_b=jnp.zeros((H,), jnp.float32), rg_W=r(ks[8], (H, DI), sel_std), rg_b=jnp.ones((H,), jnp.float32), ug_W=r(ks[9], (H, DI), sel_std), ug_b=jnp.full((H,), -1.0, jnp.float32), Q_W=jnp.repeat(jnp.eye(DI, dtype=jnp.float32), 2, axis=0), out_W=r(ks[10], (DM, DI), 0.02), D=jnp.zeros((DI,), jnp.float32), rms_w=jnp.ones((DM,), jnp.float32), gn_w=jnp.ones((DI,), jnp.float32), gn_b=jnp.zeros((DI,), jnp.float32))
    _L1_attn_all = _L1_attn_setup()
    _L1_attn_in = {k: v for k, v in _L1_attn_all.items() if k in ('in_proj_W', 'in_proj_b', 'conv_w', 'conv_b', 'dyn_W', 'dyn_b', 'dt_c', 'selB_W', 'selC_W', 'seldt_W', 'beta_W', 'beta_b', 'rg_W', 'rg_b', 'ug_W', 'ug_b', 'Q_W', 'out_W', 'D', 'rms_w', 'gn_w', 'gn_b')}
    del _L1_attn_all

    def _L1_cond2_setup():
        import jax, jax.numpy as jnp
        import numpy as np
        key = jax.random.key(seed)
        k1, k2, k3, k4, k5 = jax.random.split(key, 5)
        B, N, T, O, G = (32, 64, 256, 256, 8)
        x = jax.random.normal(k1, (B, N, T), dtype=jnp.float32)
        y = jax.random.uniform(k2, (B, G), dtype=jnp.float32)
        weight = jax.random.normal(k3, (G, O, T), dtype=jnp.float32) * (1.0 / np.sqrt(T))
        mask = jax.random.uniform(k4, (O, T), dtype=jnp.float32)
        bias = jax.random.normal(k5, (O,), dtype=jnp.float32)
        return {'x': x, 'y': y, 'weight': weight, 'mask': mask, 'bias': bias}
    _L1_cond2_all = _L1_cond2_setup()
    _L1_cond2_in = {k: v for k, v in _L1_cond2_all.items() if k in ('weight', 'mask', 'bias')}
    del _L1_cond2_all

    def _L1_ffn_setup():
        import jax, jax.numpy as jnp
        import numpy as np
        EMB = 256
        HID = 512
        HEADS = 16
        HEAD_DIM = EMB // HEADS
        EXPERTS = 8
        TOPK = 2
        EPS = 1e-05

        def layernorm(x, scale, shift):
            mean = jnp.mean(x, axis=-1, keepdims=True)
            var = jnp.mean((x - mean) ** 2, axis=-1, keepdims=True)
            return scale * (x - mean) / jnp.sqrt(var + EPS) + shift

        def attention(x, wq, wk, wv, wo, bo):
            b, t, _ = x.shape
            q = (x @ wq).reshape(b, t, HEADS, HEAD_DIM)
            k = (x @ wk).reshape(b, t, HEADS, HEAD_DIM)
            v = (x @ wv).reshape(b, t, HEADS, HEAD_DIM)
            scores = jnp.einsum('bqhd,bkhd->bhqk', q, k)
            mask = jnp.arange(t)[:, None] < jnp.arange(t)[None, :]
            scores = jnp.where(mask, -jnp.inf, scores)
            attn = jax.nn.softmax(scores / np.sqrt(HEAD_DIM), axis=-1)
            ctx = jnp.einsum('bhqk,bkhd->bqhd', attn, v).reshape(b, t, EMB)
            return ctx @ wo + bo

        def moe_ff(x, gate_w, w1, w2, w3):
            b, t, d = x.shape
            xf = x.reshape(b * t, d)
            scores = xf @ gate_w
            topk_scores, topk_idx = jax.lax.top_k(scores, TOPK)
            topk_probs = jax.nn.softmax(topk_scores, axis=-1)
            weight = jnp.sum(jax.nn.one_hot(topk_idx, EXPERTS, dtype=xf.dtype) * topk_probs[..., None], axis=1)
            h = jax.nn.silu(jnp.einsum('td,edh->eth', xf, w1)) * jnp.einsum('td,edh->eth', xf, w2)
            out_e = jnp.einsum('eth,ehd->etd', h, w3)
            out = jnp.einsum('etd,te->td', out_e, weight)
            return out.reshape(b, t, d)
        key = jax.random.key(seed)
        ks = jax.random.split(key, 12)
        s = lambda k, shape, fan: jax.random.normal(k, shape, jnp.float32) / np.sqrt(fan)
        return {'x': jax.random.normal(ks[0], (2, 512, EMB), jnp.float32), 'ln1_scale': jnp.ones((EMB,), jnp.float32), 'ln1_shift': jnp.zeros((EMB,), jnp.float32), 'wq': s(ks[1], (EMB, EMB), EMB), 'wk': s(ks[2], (EMB, EMB), EMB), 'wv': s(ks[3], (EMB, EMB), EMB), 'wo': s(ks[4], (EMB, EMB), EMB), 'bo': jnp.zeros((EMB,), jnp.float32), 'ln2_scale': jnp.ones((EMB,), jnp.float32), 'ln2_shift': jnp.zeros((EMB,), jnp.float32), 'gate_w': s(ks[5], (EMB, EXPERTS), EMB), 'w1': s(ks[6], (EXPERTS, EMB, HID), EMB), 'w2': s(ks[7], (EXPERTS, EMB, HID), EMB), 'w3': s(ks[8], (EXPERTS, HID, EMB), HID)}
    _L1_ffn_all = _L1_ffn_setup()
    _L1_ffn_in = {k: v for k, v in _L1_ffn_all.items() if k in ('ln1_scale', 'ln1_shift', 'wq', 'wk', 'wv', 'wo', 'bo', 'ln2_scale', 'ln2_shift', 'gate_w', 'w1', 'w2', 'w3')}
    del _L1_ffn_all
    return {'x': x, 'cond_8': cond_8, 'L0_cond_W_base': _L0_cond_in['W_base'], 'L0_cond_b_base': _L0_cond_in['b_base'], 'L0_cond_As': _L0_cond_in['As'], 'L0_cond_Bs': _L0_cond_in['Bs'], 'L0_attn_Wq': _L0_attn_in['Wq'], 'L0_attn_Wk': _L0_attn_in['Wk'], 'L0_attn_Wv': _L0_attn_in['Wv'], 'L0_attn_Wo': _L0_attn_in['Wo'], 'L0_cond2_skill_gate': _L0_cond2_in['skill_gate'], 'L0_cond2_skill_up': _L0_cond2_in['skill_up'], 'L0_cond2_skill_down': _L0_cond2_in['skill_down'], 'L0_cond2_shared_gate': _L0_cond2_in['shared_gate'], 'L0_cond2_shared_up': _L0_cond2_in['shared_up'], 'L0_cond2_shared_down': _L0_cond2_in['shared_down'], 'L0_ffn_w_freq_real': _L0_ffn_in['w_freq_real'], 'L0_ffn_w_freq_imag': _L0_ffn_in['w_freq_imag'], 'L0_ffn_bias': _L0_ffn_in['bias'], 'L1_cond_W_up': _L1_cond_in['W_up'], 'L1_cond_b_up': _L1_cond_in['b_up'], 'L1_cond_W_gate': _L1_cond_in['W_gate'], 'L1_cond_b_gate': _L1_cond_in['b_gate'], 'L1_cond_W_down': _L1_cond_in['W_down'], 'L1_cond_b_down': _L1_cond_in['b_down'], 'L1_attn_in_proj_W': _L1_attn_in['in_proj_W'], 'L1_attn_in_proj_b': _L1_attn_in['in_proj_b'], 'L1_attn_conv_w': _L1_attn_in['conv_w'], 'L1_attn_conv_b': _L1_attn_in['conv_b'], 'L1_attn_dyn_W': _L1_attn_in['dyn_W'], 'L1_attn_dyn_b': _L1_attn_in['dyn_b'], 'L1_attn_dt_c': _L1_attn_in['dt_c'], 'L1_attn_selB_W': _L1_attn_in['selB_W'], 'L1_attn_selC_W': _L1_attn_in['selC_W'], 'L1_attn_seldt_W': _L1_attn_in['seldt_W'], 'L1_attn_beta_W': _L1_attn_in['beta_W'], 'L1_attn_beta_b': _L1_attn_in['beta_b'], 'L1_attn_rg_W': _L1_attn_in['rg_W'], 'L1_attn_rg_b': _L1_attn_in['rg_b'], 'L1_attn_ug_W': _L1_attn_in['ug_W'], 'L1_attn_ug_b': _L1_attn_in['ug_b'], 'L1_attn_Q_W': _L1_attn_in['Q_W'], 'L1_attn_out_W': _L1_attn_in['out_W'], 'L1_attn_D': _L1_attn_in['D'], 'L1_attn_rms_w': _L1_attn_in['rms_w'], 'L1_attn_gn_w': _L1_attn_in['gn_w'], 'L1_attn_gn_b': _L1_attn_in['gn_b'], 'L1_cond2_weight': _L1_cond2_in['weight'], 'L1_cond2_mask': _L1_cond2_in['mask'], 'L1_cond2_bias': _L1_cond2_in['bias'], 'L1_ffn_ln1_scale': _L1_ffn_in['ln1_scale'], 'L1_ffn_ln1_shift': _L1_ffn_in['ln1_shift'], 'L1_ffn_wq': _L1_ffn_in['wq'], 'L1_ffn_wk': _L1_ffn_in['wk'], 'L1_ffn_wv': _L1_ffn_in['wv'], 'L1_ffn_wo': _L1_ffn_in['wo'], 'L1_ffn_bo': _L1_ffn_in['bo'], 'L1_ffn_ln2_scale': _L1_ffn_in['ln2_scale'], 'L1_ffn_ln2_shift': _L1_ffn_in['ln2_shift'], 'L1_ffn_gate_w': _L1_ffn_in['gate_w'], 'L1_ffn_w1': _L1_ffn_in['w1'], 'L1_ffn_w2': _L1_ffn_in['w2'], 'L1_ffn_w3': _L1_ffn_in['w3']}

def reference(x, cond_8, L0_cond_W_base, L0_cond_b_base, L0_cond_As, L0_cond_Bs, L0_attn_Wq, L0_attn_Wk, L0_attn_Wv, L0_attn_Wo, L0_cond2_skill_gate, L0_cond2_skill_up, L0_cond2_skill_down, L0_cond2_shared_gate, L0_cond2_shared_up, L0_cond2_shared_down, L0_ffn_w_freq_real, L0_ffn_w_freq_imag, L0_ffn_bias, L1_cond_W_up, L1_cond_b_up, L1_cond_W_gate, L1_cond_b_gate, L1_cond_W_down, L1_cond_b_down, L1_attn_in_proj_W, L1_attn_in_proj_b, L1_attn_conv_w, L1_attn_conv_b, L1_attn_dyn_W, L1_attn_dyn_b, L1_attn_dt_c, L1_attn_selB_W, L1_attn_selC_W, L1_attn_seldt_W, L1_attn_beta_W, L1_attn_beta_b, L1_attn_rg_W, L1_attn_rg_b, L1_attn_ug_W, L1_attn_ug_b, L1_attn_Q_W, L1_attn_out_W, L1_attn_D, L1_attn_rms_w, L1_attn_gn_w, L1_attn_gn_b, L1_cond2_weight, L1_cond2_mask, L1_cond2_bias, L1_ffn_ln1_scale, L1_ffn_ln1_shift, L1_ffn_wq, L1_ffn_wk, L1_ffn_wv, L1_ffn_wo, L1_ffn_bo, L1_ffn_ln2_scale, L1_ffn_ln2_shift, L1_ffn_gate_w, L1_ffn_w1, L1_ffn_w2, L1_ffn_w3):
    import jax
    import jax.numpy as jnp

    def _L0_cond_ref(x, w, W_base, b_base, As, Bs):
        import jax, jax.numpy as jnp
        import numpy as np
        R = 16
        ALPHA = 32.0
        SCALING = ALPHA / R
        out = jnp.einsum('btc,oc->bto', x, W_base) + b_base
        h = jnp.einsum('btc,erc->bter', x, As)
        lora = jnp.einsum('bter,eor,be->bto', h, Bs, w)
        return out + lora * SCALING

    def _L0_attn_ref(x, Wq, Wk, Wv, Wo):
        import jax, jax.numpy as jnp
        import numpy as np
        D_MODEL = 256
        N_HEADS = 16
        HEAD_DIM = D_MODEL // N_HEADS
        B, T, C = x.shape

        def proj(W):
            y = jnp.einsum('btc,dc->btd', x, W)
            return y.reshape(B, T, N_HEADS, HEAD_DIM).transpose(0, 2, 1, 3)
        q, k, v = (proj(Wq), proj(Wk), proj(Wv))
        scale = 1.0 / np.sqrt(HEAD_DIM).astype(np.float32)
        att = jnp.einsum('bhqd,bhkd->bhqk', q, k) * scale
        causal = jnp.tril(jnp.ones((T, T), dtype=bool))
        att = jnp.where(causal[None, None], att, -jnp.inf)
        att = jax.nn.softmax(att, axis=-1)
        out = jnp.einsum('bhqk,bhkd->bhqd', att, v)
        out = out.transpose(0, 2, 1, 3).reshape(B, T, C)
        return jnp.einsum('btc,dc->btd', out, Wo)

    def _L0_cond2_ref(x, router_logits, skill_gate, skill_up, skill_down, shared_gate, shared_up, shared_down):
        import jax, jax.numpy as jnp
        import numpy as np
        TOP_K = 2
        NUM_MOE_LAYERS = 12

        def _gemma_mlp(x, gate_w, up_w, down_w):
            g = jnp.einsum('bsh,hi->bsi', x, gate_w)
            u = jnp.einsum('bsh,hi->bsi', x, up_w)
            return jnp.einsum('bsi,ih->bsh', jax.nn.gelu(g, approximate=True) * u, down_w)
        B = x.shape[0]
        E = skill_gate.shape[0]
        rw = jax.nn.softmax(router_logits.astype(jnp.float32), axis=-1)
        w, sel = jax.lax.top_k(rw, TOP_K)
        w = w / w.sum(axis=-1, keepdims=True)
        w = w.astype(x.dtype)
        scale = 1.0 / NUM_MOE_LAYERS
        w = scale * w + (1.0 - scale) * jax.lax.stop_gradient(w)
        dense_w = jnp.zeros((B, E), x.dtype).at[jnp.arange(B)[:, None], sel].add(w)

        def step(acc, params):
            g, u, d, we = params
            return (acc + we[:, None, None] * _gemma_mlp(x, g, u, d), None)
        out, _ = jax.lax.scan(step, jnp.zeros_like(x), (skill_gate, skill_up, skill_down, dense_w.T))
        out = out + _gemma_mlp(x, shared_gate, shared_up, shared_down)
        return out

    def _L0_ffn_ref(x, w_freq_real, w_freq_imag, bias):
        import jax, jax.numpy as jnp
        import numpy as np
        B, N, D = (4, 512, 256)
        SPARSITY = 0.01
        w = jax.lax.complex(w_freq_real, w_freq_imag)
        x_freq = jnp.fft.fft(x, axis=-1)
        y_freq = jnp.einsum('bnd,do->bno', x_freq, w)
        y = jnp.real(jnp.fft.ifft(y_freq, axis=-1))
        return y + bias

    def _L1_cond_ref(x, opcode_onehot, W_up, b_up, W_gate, b_gate, W_down, b_down):
        import jax, jax.numpy as jnp
        import numpy as np
        B, S, D = (16, 512, 256)
        E, H = (8, 512)
        expert = jnp.argmax(opcode_onehot, axis=-1)
        wu, bu = (W_up[expert], b_up[expert])
        wg, bg = (W_gate[expert], b_gate[expert])
        wd, bd = (W_down[expert], b_down[expert])
        up = jnp.einsum('bsd,bhd->bsh', x, wu) + bu[:, None, :]
        gate = jnp.einsum('bsd,bhd->bsh', x, wg) + bg[:, None, :]
        hidden = jax.nn.silu(up) * gate
        out = jnp.einsum('bsh,bdh->bsd', hidden, wd) + bd[:, None, :]
        return out

    def _L1_attn_ref(x, in_proj_W, in_proj_b, conv_w, conv_b, dyn_W, dyn_b, dt_c, selB_W, selC_W, seldt_W, beta_W, beta_b, rg_W, rg_b, ug_W, ug_b, Q_W, out_W, D, rms_w, gn_w, gn_b):
        import jax, jax.numpy as jnp
        import numpy as np
        B, S, DM, DI, H = (2, 512, 256, 512, 32)
        HD = DI // H
        G = 32

        def _forward(x, in_proj_W, in_proj_b, conv_w, conv_b, dyn_W, dyn_b, dt_c, selB_W, selC_W, seldt_W, beta_W, beta_b, rg_W, rg_b, ug_W, ug_b, Q_W, out_W, D, rms_w, gn_w, gn_b):
            b, s, _ = x.shape
            residual = x
            xn = x * jax.lax.rsqrt(jnp.mean(x * x, -1, keepdims=True) + 1e-06) * rms_w
            proj = xn @ in_proj_W.T + in_proj_b
            z = proj[..., :DI]
            K = proj[..., DI:3 * DI].reshape(b, s, DI, 2)
            V = proj[..., 3 * DI:]
            vc = jax.lax.conv_general_dilated(V.transpose(0, 2, 1), conv_w[:, None, :], (1,), [(3, 0)], feature_group_count=DI, dimension_numbers=('NCH', 'OIH', 'NCH'))
            u = jax.nn.silu(vc + conv_b[None, :, None]).transpose(0, 2, 1)
            dyn = u @ dyn_W.T + dyn_b
            alpha = jax.nn.softplus(dyn[..., :H])
            omega = dyn[..., H:2 * H] + dyn[..., 2 * H:3 * H]
            rope = 1.0 / 10000.0 ** (jnp.arange(H, dtype=jnp.float32) / H)
            omega = omega + jnp.arange(s, dtype=jnp.float32)[None, :, None] * rope
            dt = jax.nn.softplus(dt_c) / (alpha + jnp.abs(omega) + 0.0001)
            dt = dt + jax.nn.softplus(u @ seldt_W.T)
            sel_B = (u @ selB_W.T).reshape(b, s, H, 1, 2)
            sel_C = (u @ selC_W.T).reshape(b, s, H, 1, 2)
            Kh = K.reshape(b, s, H, HD, 2) * sel_B
            a = 0.5 * dt * alpha
            w = 0.5 * dt * omega
            det = (1.0 + a) ** 2 + w * w
            lam2 = ((1.0 - a) ** 2 + w * w) / det
            r_gate = jax.nn.sigmoid(u @ rg_W.T + rg_b)
            vp = jnp.sqrt(jnp.clip(1.0 - lam2 ** r_gate, 1e-06))
            u_gate = jax.nn.sigmoid(u @ ug_W.T + ug_b)
            Vg = u.reshape(b, s, H, HD) * (vp * u_gate)[..., None]
            Q = (u @ Q_W.T).reshape(b, s, H, HD, 2) * sel_C
            beta = jax.nn.sigmoid(u @ beta_W.T + beta_b)
            A11 = (1.0 - a * a - w * w) / det
            A12 = 2.0 * w / det

            def step(Sc, inp):
                a11, a12, bt, k, v = inp
                S0, S1 = (Sc[..., 0], Sc[..., 1])
                r0 = a11[..., None] * S0 + a12[..., None] * S1
                r1 = -a12[..., None] * S0 + a11[..., None] * S1
                Sr = jnp.stack([r0, r1], -1)
                err = v - jnp.sum(k * Sr, -1)
                Sn = Sr + bt[..., None, None] * err[..., None] * k
                return (Sn, Sn)
            xs = (jnp.swapaxes(A11, 0, 1), jnp.swapaxes(A12, 0, 1), jnp.swapaxes(beta, 0, 1), jnp.swapaxes(Kh, 0, 1), jnp.swapaxes(Vg, 0, 1))
            S0 = jnp.zeros((b, H, HD, 2), x.dtype)
            _, Y = jax.lax.scan(step, S0, xs)
            Y = jnp.moveaxis(Y, 0, 1)
            y = jnp.sum(Q * Y, -1).reshape(b, s, DI)
            yg = y.transpose(0, 2, 1).reshape(b, G, DI // G, s)
            mu = jnp.mean(yg, (2, 3), keepdims=True)
            var = jnp.var(yg, (2, 3), keepdims=True)
            yg = (yg - mu) * jax.lax.rsqrt(var + 1e-05)
            y = (yg.reshape(b, DI, s) * gn_w[None, :, None] + gn_b[None, :, None]).transpose(0, 2, 1)
            y = y * jax.nn.silu(z)
            y = y + D * u
            return residual + y @ out_W.T
        return _forward(x, in_proj_W, in_proj_b, conv_w, conv_b, dyn_W, dyn_b, dt_c, selB_W, selC_W, seldt_W, beta_W, beta_b, rg_W, rg_b, ug_W, ug_b, Q_W, out_W, D, rms_w, gn_w, gn_b)

    def _L1_cond2_ref(x, y, weight, mask, bias):
        import jax, jax.numpy as jnp
        import numpy as np
        masked_w = weight * mask[None, :, :]
        w_bot = jnp.einsum('bg,got->bot', y, masked_w)
        return jnp.einsum('bnt,bot->bno', x, w_bot) + bias

    def _L1_ffn_ref(x, ln1_scale, ln1_shift, wq, wk, wv, wo, bo, ln2_scale, ln2_shift, gate_w, w1, w2, w3):
        import jax, jax.numpy as jnp
        import numpy as np
        EMB = 256
        HID = 512
        HEADS = 16
        HEAD_DIM = EMB // HEADS
        EXPERTS = 8
        TOPK = 2
        EPS = 1e-05

        def layernorm(x, scale, shift):
            mean = jnp.mean(x, axis=-1, keepdims=True)
            var = jnp.mean((x - mean) ** 2, axis=-1, keepdims=True)
            return scale * (x - mean) / jnp.sqrt(var + EPS) + shift

        def attention(x, wq, wk, wv, wo, bo):
            b, t, _ = x.shape
            q = (x @ wq).reshape(b, t, HEADS, HEAD_DIM)
            k = (x @ wk).reshape(b, t, HEADS, HEAD_DIM)
            v = (x @ wv).reshape(b, t, HEADS, HEAD_DIM)
            scores = jnp.einsum('bqhd,bkhd->bhqk', q, k)
            mask = jnp.arange(t)[:, None] < jnp.arange(t)[None, :]
            scores = jnp.where(mask, -jnp.inf, scores)
            attn = jax.nn.softmax(scores / np.sqrt(HEAD_DIM), axis=-1)
            ctx = jnp.einsum('bhqk,bkhd->bqhd', attn, v).reshape(b, t, EMB)
            return ctx @ wo + bo

        def moe_ff(x, gate_w, w1, w2, w3):
            b, t, d = x.shape
            xf = x.reshape(b * t, d)
            scores = xf @ gate_w
            topk_scores, topk_idx = jax.lax.top_k(scores, TOPK)
            topk_probs = jax.nn.softmax(topk_scores, axis=-1)
            weight = jnp.sum(jax.nn.one_hot(topk_idx, EXPERTS, dtype=xf.dtype) * topk_probs[..., None], axis=1)
            h = jax.nn.silu(jnp.einsum('td,edh->eth', xf, w1)) * jnp.einsum('td,edh->eth', xf, w2)
            out_e = jnp.einsum('eth,ehd->etd', h, w3)
            out = jnp.einsum('etd,te->td', out_e, weight)
            return out.reshape(b, t, d)
        h = layernorm(x, ln1_scale, ln1_shift)
        x = x + attention(h, wq, wk, wv, wo, bo)
        h = layernorm(x, ln2_scale, ln2_shift)
        x = x + moe_ff(h, gate_w, w1, w2, w3)
        return x
    x = x + _L0_attn_ref(_L0_cond_ref(x, cond_8, L0_cond_W_base, L0_cond_b_base, L0_cond_As, L0_cond_Bs), L0_attn_Wq, L0_attn_Wk, L0_attn_Wv, L0_attn_Wo)
    x = x + _L0_ffn_ref(_L0_cond2_ref(x, cond_8, L0_cond2_skill_gate, L0_cond2_skill_up, L0_cond2_skill_down, L0_cond2_shared_gate, L0_cond2_shared_up, L0_cond2_shared_down), L0_ffn_w_freq_real, L0_ffn_w_freq_imag, L0_ffn_bias)
    x = x + _L1_attn_ref(_L1_cond_ref(x, cond_8, L1_cond_W_up, L1_cond_b_up, L1_cond_W_gate, L1_cond_b_gate, L1_cond_W_down, L1_cond_b_down), L1_attn_in_proj_W, L1_attn_in_proj_b, L1_attn_conv_w, L1_attn_conv_b, L1_attn_dyn_W, L1_attn_dyn_b, L1_attn_dt_c, L1_attn_selB_W, L1_attn_selC_W, L1_attn_seldt_W, L1_attn_beta_W, L1_attn_beta_b, L1_attn_rg_W, L1_attn_rg_b, L1_attn_ug_W, L1_attn_ug_b, L1_attn_Q_W, L1_attn_out_W, L1_attn_D, L1_attn_rms_w, L1_attn_gn_w, L1_attn_gn_b)
    x = x + _L1_ffn_ref(_L1_cond2_ref(x, cond_8, L1_cond2_weight, L1_cond2_mask, L1_cond2_bias), L1_ffn_ln1_scale, L1_ffn_ln1_shift, L1_ffn_wq, L1_ffn_wk, L1_ffn_wv, L1_ffn_wo, L1_ffn_bo, L1_ffn_ln2_scale, L1_ffn_ln2_shift, L1_ffn_gate_w, L1_ffn_w1, L1_ffn_w2, L1_ffn_w3)
    return x

_drawn_inputs = setup_inputs


def setup_inputs(seed=0):
    import zlib

    import numpy as np

    out = dict(_drawn_inputs(seed))
    spreads = {'L1_cond_b_up': (0.0, 0.1),
     'L1_cond_b_gate': (0.0, 0.1),
     'L1_cond_b_down': (0.0, 0.1),
     'L1_attn_in_proj_b': (0.0, 0.1),
     'L1_attn_conv_b': (0.0, 0.1),
     'L1_attn_dyn_b': (0.0, 0.1),
     'L1_attn_dt_c': (0.5, 0.2),
     'L1_attn_beta_b': (0.0, 0.1),
     'L1_attn_rg_b': (1.0, 0.2),
     'L1_attn_ug_b': (-1.0, 0.2),
     'L1_attn_D': (0.0, 0.1),
     'L1_attn_rms_w': (1.0, 0.2),
     'L1_attn_gn_w': (1.0, 0.2),
     'L1_attn_gn_b': (0.0, 0.1),
     'L1_ffn_ln1_scale': (1.0, 0.2),
     'L1_ffn_ln1_shift': (0.0, 0.1),
     'L1_ffn_bo': (0.0, 0.1),
     'L1_ffn_ln2_scale': (1.0, 0.2),
     'L1_ffn_ln2_shift': (0.0, 0.1)}
    factors = {}
    for name, (base, spread) in spreads.items():
        noise = np.random.default_rng([zlib.crc32(name.encode()), seed]).standard_normal(out[name].shape)
        drawn = base * np.exp(spread * noise) if base else spread * noise
        out[name] = jnp.asarray(drawn.astype(out[name].dtype))
    for name, factor in factors.items():
        out[name] = (out[name] * factor).astype(out[name].dtype)
    return out
```

```python
import numpy as np
import concourse.bass as bass
from concourse import mybir
from contextlib import ExitStack

F32 = mybir.dt.float32
U32 = mybir.dt.uint32
F32R = mybir.dt.float32r
ALU = mybir.AluOpType
ACT = mybir.ActivationFunctionType
AX = mybir.AxisListType.X

P = 128
B, T, D = 2, 1024, 256
N = B * T
KD = D // P
TT = 512
NT = N // TT
HEADS, HD = 16, 16
SLOT = 32
GH = P // SLOT
GROUPS = HEADS // GH
E = 8
SCALE = HD ** -0.5


class Chip:

    def __init__(self, nc, ctx):
        self.nc, self.ctx, self.sems = nc, ctx, []
        self.bank = [ctx.enter_context(nc.psum_tensor(f"bank{n}", [P, 512], F32)) for n in range(4, 8)]
        self.pair = [ctx.enter_context(nc.psum_tensor(f"pair{n}", [P, 1024], F32)) for n in range(2)]
        self.quad = [self.pair[n // 2][:, 512 * (n % 2):512 * (n % 2) + 512] for n in range(4)]
        self.x = self.sb("x_stream", [P, KD, N])
        self.h = self.sb("h_stream", [P, KD, N])
        self.ident = self.sb("ident", [P, P])
        self.neg_ident = self.sb("neg_ident", [P, P])
        self.mean_ones = self.sb("mean_ones", [P, P])
        self.sum_pick = self.sb("sum_pick", [P, P])
        self.k_ones = self.sb("k_ones", [P, 1])
        self.v_ones = self.sb("v_ones", [P, 512])
        self.cond = self.sb("cond", [P, B, E])
        self.moe_w = self.sb("moe_w", [P, B, 3])
        self.moe_i = self.sb("moe_i", [P, B, 3], U32)

    def sb(self, name, shape, dt=F32, ctx=None):
        return (ctx or self.ctx).enter_context(self.nc.sbuf_tensor(name, shape, dt))

    def sem(self, name):
        self.sems.append(self.nc.alloc_semaphore(name=name))
        return self.sems[-1]

    def end_layer(self):
        self.nc.clear_and_free_semaphores(self.sems)
        self.nc.all_engine_barrier()
        self.sems = []


def setup(c, A):
    nc = c.nc
    loaded, picked, weighed = c.sem("su_loaded"), c.sem("su_picked"), c.sem("su_weighed")
    exp_done = c.sem("su_exp_done")
    with nc.Block() as block:
        @block.sync
        def _(sp):
            sp.dma_start(c.cond[:, :, :], A["cond_all"]).then_inc(loaded, 16)
            sp.dma_start(c.x[:, :, :], A["x"]).then_inc(loaded, 16)
            sp.dma_start(c.ident[:, :], A["ident"]).then_inc(loaded, 16)
            sp.dma_start(c.neg_ident[:, :], A["neg_ident"]).then_inc(loaded, 16)
            sp.dma_start(c.mean_ones[:, :], A["mean_ones"]).then_inc(loaded, 16)
            sp.dma_start(c.sum_pick[:, :], A["sum_pick"]).then_inc(loaded, 16)
            sp.dma_start(c.k_ones[:, :], A["k_ones"]).then_inc(loaded, 16)
            sp.dma_start(c.v_ones[:, :], A["v_ones"]).then_inc(loaded, 16)
            sp.wait_ge(loaded, 8 * 16)

        with ExitStack() as ctx:
            top = c.sb("su_top", [P, B, 8], ctx=ctx)
            idx = c.sb("su_idx", [P, B, 8], U32, ctx=ctx)
            gap = c.sb("su_gap", [P, B], ctx=ctx)
            den = c.sb("su_den", [P, B], ctx=ctx)

            @block.vector
            def _(dve):
                dve.wait_ge(loaded, 8 * 16)
                for b in range(B):
                    nc.vector.max(top[:, b, :], c.cond[:, b, :]).then_inc(picked, 1)
                dve.wait_ge(picked, B)
                for b in range(B):
                    nc.vector.max_index(idx[:, b, :], top[:, b, :], c.cond[:, b, :]).then_inc(picked, 1)
                nc.vector.tensor_tensor(gap[:, :], top[:, :, 1], top[:, :, 0], ALU.subtract).then_inc(picked, 1)
                nc.vector.memset(c.moe_i[:, :, 2:3], E).then_inc(weighed, 1)
                nc.vector.memset(c.moe_w[:, :, 2:3], 1.0).then_inc(weighed, 1)
                dve.wait_ge(picked, 2 * B + 1)
                nc.vector.tensor_copy(c.moe_i[:, :, 0:2], idx[:, :, 0:2]).then_inc(weighed, 1)
                dve.wait_ge(exp_done, 1)
                nc.vector.tensor_scalar(den[:, :], c.moe_w[:, :, 1], 1.0, None, ALU.add).then_inc(picked, 1)
                dve.wait_ge(picked, 2 * B + 2)
                nc.vector.reciprocal(c.moe_w[:, :, 0], den[:, :]).then_inc(picked, 1)
                dve.wait_ge(picked, 2 * B + 3)
                nc.vector.tensor_tensor(c.moe_w[:, :, 1], c.moe_w[:, :, 1], c.moe_w[:, :, 0], ALU.mult)\
                    .then_inc(weighed, 1)

            @block.scalar
            def _(act):
                act.wait_ge(picked, 2 * B + 1)
                nc.scalar.activation(c.moe_w[:, :, 1], gap[:, :], ACT.Exp).then_inc(exp_done, 1)


def merged_input(c, A):
    nc = c.nc
    loaded, scaled, merged, ready = c.sem("mi_loaded"), c.sem("mi_scaled"), c.sem("mi_merged"), c.sem("mi_ready")
    out_mm, out_ev = c.sem("mi_out_mm"), c.sem("mi_out_ev")
    with ExitStack() as ctx:
        lora_a = c.sb("mi_lora_a", [P, D], ctx=ctx)
        lora_b = c.sb("mi_lora_b", [P, D], ctx=ctx)
        cond_er = c.sb("mi_cond_er", [P, B], ctx=ctx)
        w_base = c.sb("mi_w_base", [P, KD, D], ctx=ctx)
        bias = c.sb("mi_bias", [P, KD], ctx=ctx)
        scaled_b = c.sb("mi_scaled_b", [P, B, D], ctx=ctx)
        w_eff = c.sb("mi_w_eff", [P, B, KD, D], ctx=ctx)
        with nc.Block() as block:
            @block.sync
            def _(sp):
                for dst, src in ((lora_a[:, :], "L0_cond_As"), (lora_b[:, :], "L0_cond_Bs"), (cond_er[:, :], "cond_er"),
                                 (w_base[:, :, :], "L0_cond_W_base"), (bias[:, :], "L0_cond_b_base")):
                    sp.dma_start(dst, A[src]).then_inc(loaded, 16)

            @block.vector
            def _(dve):
                dve.wait_ge(loaded, 5 * 16)
                for b in range(B):
                    nc.vector.tensor_scalar(scaled_b[:, b, :], lora_b[:, :], cond_er[:, b:b + 1], 2.0, ALU.mult, ALU.mult)\
                        .then_inc(scaled, 1)
                for b in range(B):
                    for k in range(KD):
                        dve.wait_ge(merged, b * KD + k + 1)
                        nc.vector.tensor_tensor(w_eff[:, b, k, :], c.quad[b * KD + k][:, 0:D], w_base[:, k, :], ALU.add)\
                            .then_inc(ready, 1)

            @block.tensor
            def _(pe):
                pe.wait_ge(loaded, 5 * 16)
                for b in range(B):
                    pe.wait_ge(scaled, b + 1)
                    for k in range(KD):
                        nc.tensor.matmul(c.quad[b * KD + k][:, 0:D], lora_a[:, k * P:(k + 1) * P], scaled_b[:, b, :],
                                         start=True, stop=True).then_inc(merged, 1)
                n = 0
                for b in range(B):
                    pe.wait_ge(ready, (b + 1) * KD)
                    for t in range(T // TT):
                        for m in range(KD):
                            if n >= 4:
                                pe.wait_ge(out_ev, n - 3)
                            for k in range(KD):
                                last = nc.tensor.matmul(c.bank[n % 4][:, :], w_eff[:, b, k, m * P:(m + 1) * P],
                                                        c.x[:, k, b * T + t * TT:b * T + (t + 1) * TT],
                                                        start=k == 0, stop=k == KD - 1)
                            last.then_inc(out_mm, 1)
                            n += 1

            @block.scalar
            def _(act):
                act.wait_ge(loaded, 5 * 16)
                n = 0
                for b in range(B):
                    for t in range(T // TT):
                        for m in range(KD):
                            act.wait_ge(out_mm, n + 1)
                            nc.scalar.activation(c.h[:, m, b * T + t * TT:b * T + (t + 1) * TT], c.bank[n % 4][:, :],
                                                 ACT.Identity, bias=bias[:, m:m + 1]).then_inc(out_ev, 1)
                            n += 1


def attention(c, A, tag, w_qkv, w_out, b_out, dest):
    nc = c.nc
    s = {n: c.sem(f"{tag}_{n}") for n in (
        "mask", "passed", "seen", "wg", "hc", "hc_free", "proj", "k_ev", "qm", "qm1", "vp", "v_ev", "a_mm", "a_max",
        "t_mm", "t_add", "b_mm", "b_exp", "b_cut", "pv", "o_sum", "o_cp", "o_rc", "o_done", "zero", "ow", "om", "oe")}
    QT = T // P
    HALF = T // TT
    with ExitStack() as octx:
        o_all = c.sb(f"{tag}_o_all", [P, GROUPS, N], ctx=octx)
        with ExitStack() as ctx:
            w = c.sb(f"{tag}_w", [P, 3, KD, P], ctx=ctx)
            hc = c.sb(f"{tag}_hc", [P, KD, T], ctx=ctx)
            k_sb = c.sb(f"{tag}_k", [P, T], ctx=ctx)
            qm = c.sb(f"{tag}_qm", [P, GH, T], ctx=ctx)
            v_sb = c.sb(f"{tag}_v", [P, QT, P], ctx=ctx)
            mx = c.sb(f"{tag}_mx", [P, QT, P], ctx=ctx)
            junk = c.sb(f"{tag}_junk", [P, 2, T], ctx=ctx)
            mask = c.sb(f"{tag}_mask", [P, T], ctx=ctx)
            RING = 3
            prob = c.sb(f"{tag}_prob", [P, RING, GH, TT], ctx=ctx)
            o_raw = c.sb(f"{tag}_o_raw", [P, HALF, TT], ctx=ctx)
            o_rcp = c.sb(f"{tag}_o_rcp", [P, TT], ctx=ctx)
            steps = [(h, j) for h in range(HALF) for j in range(4 * (h + 1))]
            NS = len(steps)

            def cut(h, j):
                return max(0, j * P - h * TT)

            with nc.Block() as block:
                @block.sync
                def _(sp):
                    sp.dma_start(mask[:, :], A["causal"]).then_inc(s["mask"], 16)
                    with sp.Fori(0, B) as b:
                        with sp.Fori(0, GROUPS) as g:
                            n = b * GROUPS + g
                            sp.wait_ge(s["hc_free"], n + 1)
                            sp.dma_start(w[:, :, :, :], A[w_qkv][g, :, :, :, :]).then_inc(s["wg"], 16)

                @block.gpsimd
                def _(pool):
                    for g in range(GH):
                        nc.gpsimd.memset(qm[:, g, :], 0.0).then_inc(s["zero"], 1)
                    nc.gpsimd.memset(mx[:, :, :], 0.0).then_inc(s["zero"], 1)
                    pool.wait_ge(s["zero"], GH + 1)
                    with pool.Fori(0, B) as b:
                        with pool.Fori(0, GROUPS) as g:
                            n = b * GROUPS + g
                            pool.wait_ge(s["hc_free"], n + 1)
                            pool.sem_inc(s["passed"], 1)
                            nc.gpsimd.tensor_copy(hc[:, :, :], c.h[:, :, :].rearrange("p k (b t) -> p k b t", b=B)[:, :, b, :])\
                                .then_inc(s["hc"], 1)
                            for h, j in steps:
                                if j < 4 * h:
                                    continue
                                i = steps.index((h, j))
                                pool.wait_ge(s["b_exp"], (n * NS + i + 1) * GH)
                                pool.sem_inc(s["passed"], 1)
                                q0 = cut(h, j)
                                block_ = prob[:, i % RING, :, q0:q0 + P]
                                nc.gpsimd.affine_select(out=block_, in_=block_, compare_op=ALU.is_ge, fill=0.0, base=0,
                                                        pattern=[[0, GH], [1, P]], channel_multiplier=-1)\
                                    .then_inc(s["b_cut"], 1)

                @block.tensor
                def _(pe):
                    pe.wait_ge(s["zero"], GH + 1)
                    with pe.Fori(0, B) as b:
                        with pe.Fori(0, GROUPS) as g:
                            n = b * GROUPS + g
                            pe.wait_ge(s["wg"], n * 16 + 16)
                            pe.wait_ge(s["hc"], n + 1)
                            for h in range(HALF):
                                for m in range(2):
                                    for k in range(KD):
                                        last = nc.tensor.matmul(c.quad[2 * h + m], w[:, m, k, :], hc[:, k, h * TT:(h + 1) * TT],
                                                                start=k == 0, stop=k == KD - 1)
                                    last.then_inc(s["proj"], 1)
                            for v in range(QT // 4):
                                for t in range(4):
                                    for k in range(KD):
                                        last = nc.tensor.matmul(c.bank[v][:, t * P:(t + 1) * P],
                                                                hc[:, k, (4 * v + t) * P:(4 * v + t + 1) * P], w[:, 2, k, :],
                                                                start=k == 0, stop=k == KD - 1)
                                last.then_inc(s["vp"], 1)

                            def first(lo, hi):
                                for i in range(lo, hi):
                                    for a in range(GH):
                                        t = i * GH + a
                                        if t >= 2:
                                            pe.wait_ge(s["a_max"], n * QT * GH + (t - 1))
                                        for c0 in range(0, (i + 1) * P, 512):
                                            c1 = min(c0 + 512, (i + 1) * P)
                                            last = nc.tensor.matmul(c.pair[t % 2][:, c0:c1], qm[:, a, i * P:(i + 1) * P],
                                                                    k_sb[:, c0:c1], start=True, stop=True)
                                        last.then_inc(s["a_mm"], 1)

                            def maxima(h):
                                pe.wait_ge(s["a_max"], n * QT * GH + (h + 1) * 4 * GH)
                                for i in range(4):
                                    last = nc.tensor.matmul(c.bank[0][:, i * P:(i + 1) * P], mx[:, 4 * h + i, :],
                                                            c.neg_ident[:, :], start=True, stop=True)
                                last.then_inc(s["t_mm"], 1)

                            def scores(i):
                                h, j = steps[i]
                                q0 = cut(h, j)
                                for a in range(GH):
                                    t = i * GH + a
                                    if t >= 4:
                                        pe.wait_ge(s["b_exp"], n * NS * GH + t - 3)
                                    nc.tensor.matmul(c.quad[t % 4][:, q0:TT], k_sb[:, j * P:(j + 1) * P],
                                                     qm[:, a, h * TT + q0:(h + 1) * TT], start=True, stop=True)\
                                        .then_inc(s["b_mm"], 1)

                            def values(i):
                                h, j = steps[i]
                                q0 = cut(h, j)
                                pe.wait_ge(s["b_exp"], (n * NS + i + 1) * GH)
                                if j >= 4 * h:
                                    pe.wait_ge(s["b_cut"], n * QT + j + 1)
                                for a in range(GH):
                                    r = slice(a * SLOT, (a + 1) * SLOT)
                                    last = nc.tensor.matmul(c.bank[1 + h][r, q0:TT], v_sb[:, j, r], prob[:, i % RING, a, q0:TT],
                                                            start=j == 0, stop=j == 4 * h + 3)
                                last.then_inc(s["pv"], 1)

                            def sums(h):
                                pe.wait_ge(s["o_cp"], n * HALF + h + 1)
                                pe.wait_ge(s["o_rc"], n * HALF + h + 1)
                                nc.tensor.matmul(c.bank[3][:, :], c.sum_pick[:, :], o_raw[:, h, :], start=True, stop=True)\
                                    .then_inc(s["o_sum"], 1)

                            pe.wait_ge(s["qm"], (n + 1) * GH)
                            pe.wait_ge(s["qm1"], (n + 1) * GH)
                            pe.wait_ge(s["k_ev"], (n + 1) * HALF)
                            first(0, QT)
                            pe.wait_ge(s["v_ev"], n * 2 + 2)
                            maxima(0)
                            pe.wait_ge(s["t_add"], n * HALF + 1)
                            pe.wait_ge(s["a_max"], (n + 1) * QT * GH)
                            for i in range(4):
                                scores(i)
                                if i:
                                    values(i - 1)
                            maxima(1)
                            values(3)
                            pe.wait_ge(s["t_add"], n * HALF + 2)
                            for i in range(4, NS):
                                scores(i)
                                if i == 6:
                                    sums(0)
                                if i > 4:
                                    values(i - 1)
                            values(NS - 1)
                            sums(1)

                @block.scalar
                def _(act):
                    act.wait_ge(s["zero"], GH + 1)
                    with act.Fori(0, B) as b:
                        with act.Fori(0, GROUPS) as g:
                            n = b * GROUPS + g
                            for h in range(HALF):
                                cols = slice(h * TT, (h + 1) * TT)
                                act.wait_ge(s["proj"], n * 2 * HALF + 2 * h + 1)
                                if h == 0:
                                    for a in range(GH):
                                        r = slice(a * SLOT, (a + 1) * SLOT)
                                        nc.scalar.activation(qm[r, a, cols], c.quad[0][r, :], ACT.Copy).then_inc(s["qm"], 1)
                                act.wait_ge(s["proj"], n * 2 * HALF + 2 * h + 2)
                                nc.scalar.activation(k_sb[:, cols], c.quad[2 * h + 1], ACT.Identity, bias=c.k_ones[:, 0:1])\
                                    .then_inc(s["k_ev"], 1)
                            for i, (h, j) in enumerate(steps):
                                q0 = cut(h, j)
                                if i >= RING:
                                    act.wait_ge(s["pv"], n * NS + i - RING + 1)
                                for a in range(GH):
                                    act.wait_ge(s["b_mm"], (n * NS + i) * GH + a + 1)
                                    nc.scalar.activation(prob[:, i % RING, a, q0:TT], c.quad[(i * GH + a) % 4][:, q0:TT],
                                                         ACT.Exp, scale=SCALE).then_inc(s["b_exp"], 1)

                @block.vector
                def _(dve):
                    dve.wait_ge(s["mask"], 16)
                    dve.wait_ge(s["zero"], GH + 1)
                    for free in ("hc_free", "o_rc"):
                        dve.sem_inc(s[free], 1)
                    with dve.Fori(0, B) as b:
                        with dve.Fori(0, GROUPS) as g:
                            n = b * GROUPS + g
                            dve.wait_ge(s["proj"], n * 2 * HALF + 3)
                            for a in range(GH):
                                r = slice(a * SLOT, (a + 1) * SLOT)
                                nc.vector.tensor_copy(qm[r, a, TT:2 * TT], c.quad[2][r, :]).then_inc(s["qm1"], 1)
                            for v in range(QT // 4):
                                dve.wait_ge(s["vp"], n * 2 + v + 1)
                                nc.vector.tensor_tensor(v_sb[:, 4 * v:4 * v + 4, :].rearrange("p t d -> p (t d)"), c.bank[v][:, :],
                                                        c.v_ones[:, :], ALU.add).then_inc(s["v_ev"], 1)
                            dve.wait_ge(s["v_ev"], n * 2 + 2)
                            dve.sem_inc(s["hc_free"], 1)

                            def maxima(lo, hi):
                                for i in range(lo, hi):
                                    for a in range(GH):
                                        t = i * GH + a
                                        cols = (i + 1) * P
                                        dve.wait_ge(s["a_mm"], n * QT * GH + t + 1)
                                        if t >= 2:
                                            dve.wait_ge(s["a_max"], n * QT * GH + t - 1)
                                        dve.sem_inc(s["seen"], 1)
                                        nc.vector.tensor_tensor_reduce(
                                            out=junk[:, t % 2, 0:cols], in0=c.pair[t % 2][:, 0:cols], in1=mask[:, T - cols:T],
                                            scale=1.0, scalar=-3.0e38, op0=ALU.add, op1=ALU.max,
                                            accum_out=mx[:, i, a * SLOT + HD:a * SLOT + HD + 1]).then_inc(s["a_max"], 1)

                            def add_max(h):
                                dve.wait_ge(s["t_mm"], n * HALF + h + 1)
                                for a in range(GH):
                                    r = slice(a * SLOT, (a + 1) * SLOT)
                                    cols = slice(h * TT, (h + 1) * TT)
                                    last = nc.vector.tensor_tensor(qm[r, a, cols], c.bank[0][r, :], qm[r, a, cols], ALU.add)
                                last.then_inc(s["t_add"], 1)

                            def copy_out(h):
                                dve.wait_ge(s["pv"], n * NS + (4 if h == 0 else NS))
                                nc.vector.tensor_copy(o_raw[:, h, :], c.bank[1 + h][:, :]).then_inc(s["o_cp"], 1)

                            def divide(h):
                                dve.wait_ge(s["o_sum"], n * HALF + h + 1)
                                nc.vector.reciprocal(o_rcp[:, :], c.bank[3][:, :]).then_inc(s["o_rc"], 1)
                                dve.wait_ge(s["o_rc"], n * HALF + h + 2)
                                o_b = o_all[:, :, :].rearrange("p g (b h t) -> p (g b h) t", b=B, h=HALF)
                                nc.vector.tensor_tensor(o_b[:, g * (B * HALF) + (b * HALF + h), :], o_raw[:, h, :],
                                                        o_rcp[:, :], ALU.mult).then_inc(s["o_done"], 1)

                            maxima(0, 4)
                            maxima(4, QT)
                            add_max(0)
                            add_max(1)
                            copy_out(0)
                            divide(0)
                            copy_out(1)
                            divide(1)
                            dve.wait_ge(s["o_done"], n * HALF + HALF)
                            dve.nop()

        with ExitStack() as ctx:
            wo = c.sb(f"{tag}_wo", [P, GROUPS, D], ctx=ctx)
            bo = c.sb(f"{tag}_bo", [P, KD], ctx=ctx)
            with nc.Block() as block:
                @block.sync
                def _(sp):
                    sp.dma_start(wo[:, :, :], A[w_out]).then_inc(s["ow"], 16)
                    sp.dma_start(bo[:, :], A[b_out]).then_inc(s["ow"], 16)

                @block.tensor
                def _(pe):
                    pe.wait_ge(s["ow"], 32)
                    with pe.Fori(0, NT) as t:
                        for m in range(KD):
                            pe.wait_ge(s["oe"], t * KD + m + 1)
                            for g in range(GROUPS):
                                last = nc.tensor.matmul(c.bank[m][:, :], wo[:, g, m * P:(m + 1) * P],
                                                        o_all[:, g, :].rearrange("p (n t) -> p n t", t=TT)[:, t, :],
                                                        start=g == 0, stop=g == GROUPS - 1)
                            last.then_inc(s["om"], 1)

                @block.vector
                def _(dve):
                    dve.sem_inc(s["oe"], KD)
                    dve.wait_ge(s["ow"], 32)
                    with dve.Fori(0, NT) as t:
                        for m in range(KD):
                            dve.wait_ge(s["om"], t * KD + m + 1)
                            tile = dest[:, m, :].rearrange("p (n t) -> p n t", t=TT)[:, t, :]
                            nc.vector.scalar_tensor_tensor(out=tile, in0=c.bank[m][:, :], scalar=bo[:, m:m + 1], in1=tile,
                                                           op0=ALU.add, op1=ALU.add).then_inc(s["oe"], 1)


def split(c, tag, src, hi, lo):
    nc = c.nc
    rounded, rest = c.sem(f"{tag}_sp_rounded"), c.sem(f"{tag}_sp_rest")
    with nc.Block() as block:
        @block.scalar
        def _(act):
            for k in range(KD):
                nc.scalar.activation(hi[:, k, :], src[:, k, :], ACT.Copy).then_inc(rounded, 1)

        @block.vector
        def _(dve):
            for k in range(KD):
                dve.wait_ge(rounded, k + 1)
                nc.vector.tensor_tensor(lo[:, k, :], src[:, k, :], hi[:, k, :].bitcast(F32), ALU.subtract).then_inc(rest, 1)


def product(nc, out, w_hi, w_lo, x_hi, x_lo, first, last):
    nc.tensor.matmul(out, w_lo, x_hi, start=first, stop=False)
    nc.tensor.matmul(out, w_hi, x_hi, start=False, stop=False)
    return nc.tensor.matmul(out, w_hi, x_lo, start=False, stop=last)


def gated_mlp(c, tag, hb, rounds, tiles, source, func, x_hi, x_lo, y, load_extra=None, bias=None, finish=None):
    nc = c.nc
    part = KD * hb * P
    steps = [(s, i, m) for s in range(2) for i in range(len(tiles[s])) for m in range(hb)]
    SB, TB = len(steps), len(tiles[0]) + len(tiles[1])
    LAG, RING = 3, 4
    q = {n: c.sem(f"{tag}_{n}") for n in (
        "passed", "raw0", "raw1", "raw_free", "w_hi", "w_ready", "unit_done", "up", "act", "prod", "hi", "lo",
        "down", "y_done", "y_part", "extra", "extra0", "extra1", "extra_free")}
    raw_ready = [q["raw0"], q["raw1"]]
    if bias:
        bias["sem"].append(q["extra"])
    with ExitStack() as ctx:
        raw = c.sb(f"{tag}_raw", [P, 2, part], ctx=ctx)
        w_hi = c.sb(f"{tag}_w_hi", [P, 2, 3, part], F32R, ctx=ctx)
        w_lo = c.sb(f"{tag}_w_lo", [P, 2, 3, part], F32R, ctx=ctx)
        g_sb = c.sb(f"{tag}_g", [P, 2, TT], ctx=ctx)
        h_sb = c.sb(f"{tag}_h", [P, 2, TT], ctx=ctx)
        h_hi = c.sb(f"{tag}_h_hi", [P, RING, TT], F32R, ctx=ctx)
        h_lo = c.sb(f"{tag}_h_lo", [P, RING, TT], F32R, ctx=ctx)

        def rolled(eng, body):
            if rounds == 1:
                body(0)
            else:
                with eng.Fori(0, rounds) as r:
                    body(r)

        with nc.Block() as block:
            @block.sync
            def _(sp):
                def body(r):
                    for s in range(2):
                        unit = source(sp, r, s)
                        if load_extra:
                            load_extra(sp, r, s, unit, q)
                        for p in range(3):
                            n = 3 * s + p
                            sp.wait_ge(q["raw_free"], r * 6 + n + 1)
                            sp.dma_start(raw[:, n % 2, :], unit(p)).then_inc(raw_ready[n % 2], 16)
                rolled(sp, body)

            @block.gpsimd
            def _(pool):
                pool.sem_inc(q["raw_free"], 2)

                def body(r):
                    for s in range(2):
                        for p in range(3):
                            n = 3 * s + p
                            pool.wait_ge(raw_ready[n % 2], (r * 3 + n // 2 + 1) * 16)
                            if p == 0:
                                pool.wait_ge(q["unit_done"], r * 2 + s + 1)
                            pool.sem_inc(q["passed"], 1)
                            nc.gpsimd.tensor_copy(w_hi[:, s, p, :], raw[:, n % 2, :]).then_inc(q["w_hi"], 1)
                            pool.wait_ge(q["w_hi"], r * 6 + n + 1)
                            nc.gpsimd.tensor_tensor(w_lo[:, s, p, :], raw[:, n % 2, :], w_hi[:, s, p, :].bitcast(F32),
                                                    ALU.subtract).then_inc(q["w_ready"], 1)
                            pool.wait_ge(q["w_ready"], r * 6 + n + 1)
                            pool.sem_inc(q["raw_free"], 1)
                rolled(pool, body)

            @block.tensor
            def _(pe):
                pe.sem_inc(q["unit_done"], 2)

                def body(r):
                    def w(arr, s, p, k, m):
                        wide = hb if p < 2 else KD
                        return arr[:, s, p, (k * wide + m) * P:(k * wide + m + 1) * P]

                    def up(n):
                        s, i, m = steps[n]
                        t0 = tiles[s][i]
                        if n >= 2:
                            pe.wait_ge(q["prod"], r * SB + n + 1)
                        for p in range(2):
                            if i == 0 and m == 0:
                                pe.wait_ge(q["w_ready"], r * 6 + 3 * s + p + 1)
                            for k in range(KD):
                                last = product(nc, c.quad[2 * (n % 2) + p], w(w_hi, s, p, k, m), w(w_lo, s, p, k, m),
                                               x_hi[:, k, t0:t0 + TT], x_lo[:, k, t0:t0 + TT], k == 0, k == KD - 1)
                            last.then_inc(q["up"], 1)

                    def down(n):
                        s, i, m = steps[n]
                        tile = n // hb
                        if i == 0 and m == 0:
                            pe.wait_ge(q["w_ready"], r * 6 + 3 * s + 3)
                        if m == 0:
                            pe.wait_ge(q["y_done"], r * TB + tile + 1)
                        pe.wait_ge(q["lo"], r * SB + n + 1)
                        for o in range(KD):
                            last = product(nc, c.bank[2 * (tile % 2) + o][:, :], w(w_hi, s, 2, m, o), w(w_lo, s, 2, m, o),
                                           h_hi[:, n % RING, :], h_lo[:, n % RING, :], m == 0, m == hb - 1)
                        last.then_inc(q["down"], 1)
                        if i == len(tiles[s]) - 1 and m == hb - 1:
                            pe.wait_ge(q["down"], RING + r * SB + n + 1)
                            pe.sem_inc(q["unit_done"], 1)

                    for n in range(SB):
                        up(n)
                        if n >= LAG:
                            down(n - LAG)
                    for n in range(SB - LAG, SB):
                        down(n)
                rolled(pe, body)

            @block.scalar
            def _(act):
                act.sem_inc(q["down"], RING)

                def body(r):
                    def rounded(n):
                        act.wait_ge(q["down"], r * SB + n + 1)
                        act.wait_ge(q["prod"], 2 + r * SB + n + 1)
                        nc.scalar.activation(h_hi[:, n % RING, :], h_sb[:, n % 2, :], ACT.Copy).then_inc(q["hi"], 1)

                    for n in range(SB):
                        s, i, m = steps[n]
                        act.wait_ge(q["prod"], r * SB + n + 1)
                        act.wait_ge(q["up"], 2 * (r * SB + n) + 1)
                        if bias:
                            if i == 0 and m == 0:
                                act.wait_ge(q["extra"], 16 * bias["loads"])
                            nc.scalar.activation(g_sb[:, n % 2, :], c.quad[2 * (n % 2)], func,
                                                 bias=bias["first"](s, m)).then_inc(q["act"], 1)
                        else:
                            nc.scalar.activation(g_sb[:, n % 2, :], c.quad[2 * (n % 2)], func).then_inc(q["act"], 1)
                        if n:
                            rounded(n - 1)
                    rounded(SB - 1)
                rolled(act, body)

            @block.vector
            def _(dve):
                dve.sem_inc(q["prod"], 2)
                dve.sem_inc(q["y_done"], 2)
                if load_extra:
                    dve.sem_inc(q["extra_free"], 2)
                    dve.sem_inc(q["y_part"], 1)
                if bias:
                    dve.wait_ge(q["extra"], 16 * bias["loads"])

                def body(r):
                    def rest(n):
                        dve.wait_ge(q["hi"], r * SB + n + 1)
                        nc.vector.tensor_tensor(h_lo[:, n % RING, :], h_sb[:, n % 2, :], h_hi[:, n % RING, :].bitcast(F32),
                                                ALU.subtract).then_inc(q["lo"], 1)

                    def add(tile):
                        s = tile // len(tiles[0])
                        t0 = tiles[s][tile % len(tiles[0])]
                        dve.wait_ge(q["down"], RING + r * SB + (tile + 1) * hb)
                        for o in range(KD):
                            last = finish(dve, r, s, o, t0, c.bank[2 * (tile % 2) + o][:, :], q)
                        if last is dve:
                            dve.sem_inc(q["y_done"], 1)
                        else:
                            last.then_inc(q["y_done"], 1)
                        if load_extra and (tile + 1) % len(tiles[0]) == 0:
                            dve.wait_ge(q["y_done"], 2 + r * TB + tile + 1)
                            dve.sem_inc(q["extra_free"], 1)

                    for n in range(SB):
                        s, i, m = steps[n]
                        dve.wait_ge(q["act"], r * SB + n + 1)
                        dve.wait_ge(q["up"], 2 * (r * SB + n) + 2)
                        if n >= 2:
                            dve.wait_ge(q["lo"], r * SB + n - 1)
                        if bias:
                            nc.vector.scalar_tensor_tensor(out=h_sb[:, n % 2, :], in0=c.quad[2 * (n % 2) + 1],
                                                           scalar=bias["second"](s, m), in1=g_sb[:, n % 2, :],
                                                           op0=ALU.add, op1=ALU.mult).then_inc(q["prod"], 1)
                        else:
                            nc.vector.tensor_tensor(h_sb[:, n % 2, :], c.quad[2 * (n % 2) + 1], g_sb[:, n % 2, :],
                                                    ALU.mult).then_inc(q["prod"], 1)
                        if n:
                            rest(n - 1)
                        if n >= hb + LAG and (n - LAG) % hb == 0:
                            add((n - LAG) // hb - 1)
                    rest(SB - 1)
                    add(TB - 1)
                rolled(dve, body)


def two_of_eight(c, A):
    nc = c.nc
    zeroed = c.sem("m2_zeroed")
    with ExitStack() as ctx:
        x_hi = c.sb("m2_x_hi", [P, KD, N], F32R, ctx=ctx)
        x_lo = c.sb("m2_x_lo", [P, KD, N], F32R, ctx=ctx)
        split(c, "m2", c.x, x_hi, x_lo)
        with nc.Block() as block:
            @block.vector
            def _(dve):
                for k in range(KD):
                    nc.vector.memset(c.h[:, k, :], 0.0).then_inc(zeroed, 1)

        def source(sp, r, s):
            e = sp.value_load(c.moe_i[0:1, s, :][:, bass.ds(r, 1)], min_val=0, max_val=E)
            return lambda p: A["L0_cond2_experts"][e, p, :, :]

        def finish(dve, r, s, o, t0, psum, q):
            y = c.h[:, o, t0:t0 + TT]
            return nc.vector.scalar_tensor_tensor(out=y, in0=psum, scalar=c.moe_w[:, s, :][:, bass.ds(r, 1)], in1=y,
                                                  op0=ALU.mult, op1=ALU.add)

        tiles = [[b * T + t * TT for t in range(T // TT)] for b in range(B)]
        gated_mlp(c, "m2", 8, 3, tiles, source, ACT.Gelu_apprx_tanh, x_hi, x_lo, c.h, finish=finish)


def spectral(c, A):
    nc = c.nc
    loaded, u_mm, u_ev, m_mm, m_ev = (c.sem(f"sp_{n}") for n in ("loaded", "u_mm", "u_ev", "m_mm", "m_ev"))
    mm, added = c.sem("sp_mm"), c.sem("sp_added")
    with ExitStack() as ctx:
        dft = c.sb("sp_dft", [P, 3, KD, D], ctx=ctx)
        wr = c.sb("sp_wr", [P, KD, D], ctx=ctx)
        wi = c.sb("sp_wi", [P, KD, D], ctx=ctx)
        bias = c.sb("sp_bias", [P, KD], ctx=ctx)
        u = c.sb("sp_u", [P, 2, KD, D], ctx=ctx)
        mat = c.sb("sp_mat", [P, KD, D], ctx=ctx)
        with nc.Block() as block:
            @block.sync
            def _(sp):
                for dst, src in ((dft[:, :, :, :], "dft"), (wr[:, :, :], "L0_ffn_wr"), (wi[:, :, :], "L0_ffn_wi"),
                                 (bias[:, :], "L0_ffn_bias")):
                    sp.dma_start(dst, A[src]).then_inc(loaded, 16)

            @block.tensor
            def _(pe):
                pe.wait_ge(loaded, 4 * 16)
                for part, terms in enumerate((((wr, 0), (wi, 1)), ((wi, 0), (wr, 2)))):
                    for f in range(KD):
                        n = 0
                        for w, d in terms:
                            for k in range(KD):
                                last = nc.tensor.matmul(c.quad[part * KD + f][:, 0:D], w[:, k, f * P:(f + 1) * P],
                                                        dft[:, d, k, :], start=n == 0, stop=n == 2 * KD - 1)
                                n += 1
                        last.then_inc(u_mm, 1)
                pe.wait_ge(u_ev, 2 * KD)
                for i in range(KD):
                    n = 0
                    for part, d in ((0, 0), (1, 2)):
                        for f in range(KD):
                            last = nc.tensor.matmul(c.bank[i][:, 0:D], u[:, part, f, i * P:(i + 1) * P], dft[:, d, f, :],
                                                    start=n == 0, stop=n == 2 * KD - 1)
                            n += 1
                    last.then_inc(m_mm, 1)
                pe.wait_ge(m_ev, KD)
                for t in range(NT):
                    for o in range(KD):
                        n = t * KD + o
                        if n >= 4:
                            pe.wait_ge(added, n - 3)
                        for k in range(KD):
                            last = nc.tensor.matmul(c.quad[n % 4], mat[:, k, o * P:(o + 1) * P],
                                                    c.h[:, k, t * TT:(t + 1) * TT], start=k == 0, stop=k == KD - 1)
                        last.then_inc(mm, 1)

            @block.scalar
            def _(act):
                for n in range(2 * KD):
                    act.wait_ge(u_mm, n + 1)
                    nc.scalar.activation(u[:, n // KD, n % KD, :], c.quad[n][:, 0:D], ACT.Copy).then_inc(u_ev, 1)
                for i in range(KD):
                    act.wait_ge(m_mm, i + 1)
                    nc.scalar.activation(mat[:, i, :], c.bank[i][:, 0:D], ACT.Copy, scale=1.0 / D).then_inc(m_ev, 1)

            @block.vector
            def _(dve):
                dve.wait_ge(loaded, 4 * 16)
                for t in range(NT):
                    for o in range(KD):
                        n = t * KD + o
                        dve.wait_ge(mm, n + 1)
                        x = c.x[:, o, t * TT:(t + 1) * TT]
                        nc.vector.scalar_tensor_tensor(out=x, in0=c.quad[n % 4], scalar=bias[:, o:o + 1], in1=x,
                                                       op0=ALU.add, op1=ALU.add).then_inc(added, 1)


def chosen_expert(c, A):
    nc = c.nc
    HB = 4
    with ExitStack() as ctx:
        x_hi = c.sb("m1_x_hi", [P, KD, N], F32R, ctx=ctx)
        x_lo = c.sb("m1_x_lo", [P, KD, N], F32R, ctx=ctx)
        biases = c.sb("m1_biases", [P, B, 2 * HB + KD], ctx=ctx)
        split(c, "m1", c.x, x_hi, x_lo)

        def source(sp, r, s):
            e = sp.value_load(c.moe_i[0:1, s, 0:1], min_val=0, max_val=E - 1)
            sp.dma_start(biases[:, s, :], A["L1_cond_biases"][e, :, :]).then_inc(extra[0], 16)
            return lambda p: A["L1_cond_experts"][e, p, :, :]

        extra = []

        def finish(dve, r, s, o, t0, psum, q):
            return nc.vector.tensor_scalar(c.h[:, o, t0:t0 + TT], psum, biases[:, s, 2 * HB + o:2 * HB + o + 1], None, ALU.add)

        bias = {"loads": B, "first": lambda s, m: biases[:, s, m:m + 1],
                "second": lambda s, m: biases[:, s, HB + m:HB + m + 1], "sem": extra}
        tiles = [[b * T + t * TT for t in range(T // TT)] for b in range(B)]
        gated_mlp(c, "m1", HB, 1, tiles, source, ACT.Silu, x_hi, x_lo, c.h, bias=bias, finish=finish)


H = 32
DI = 512
KI = DI // P
QW_ = T // 4
H_ALPHA, H_OMEGA1, H_OMEGA2, H_SELB0, H_SELB1, H_SELC0, H_SELC1, H_SELDT, H_BETA, H_RG, H_UG = range(11)
V_A11, V_A12, V_BETA, V_VF, V_SB0, V_SB1, V_SC0, V_SC1 = range(8)
L_STEP = 32
CHUNKS = T // L_STEP
NB = KI * CHUNKS


def recurrent(c, A):
    nc = c.nc
    names = ("rcp passed wload2 sq ms rt xn mm ev acc u hmm h1 h2 wload cb cd cp qload qmm d1 d2 d3 x1 p2 p3 "
             "g1 g2 g3 g4 g5 oload omm oadd e1 win const").split()
    s = {n: c.sem(f"r_{n}") for n in names}
    with ExitStack() as ctx:
        z = c.sb("r_z", [P, KI, T], ctx=ctx)
        u = c.sb("r_u", [P, KI, T], ctx=ctx)
        coef = c.sb("r_coef", [P, 6, KI * T], ctx=ctx)
        weights = c.sb("r_weights", [P, 4096], ctx=ctx)
        scr = c.sb("r_scratch", [P, 4096], ctx=ctx)
        spread = c.sb("r_spread", [P, 4, KI, P], ctx=ctx)
        in_bias = c.sb("r_in_bias", [P, 16], ctx=ctx)
        vecs = c.sb("r_vecs", [P, KI, 9], ctx=ctx)
        hvecs = c.sb("r_hvecs", [P, 8], ctx=ctx)
        rms_w = c.sb("r_rms_w", [P, KD], ctx=ctx)
        group = c.sb("r_group", [P, P], ctx=ctx)
        dtc = c.sb("r_dtc", [P, 4], ctx=ctx)
        stat = c.sb("r_stat", [P, KI, 8], ctx=ctx)
        eps = c.sb("r_eps", [P, 2], ctx=ctx)
        flat = coef[:, :, :].rearrange("p a n -> p (a n)")
        pos = A["r_pos"]
        HALF = T // TT

        def tok(arr, b):
            return arr[:, :, :].rearrange("p k (b t) -> p k b t", b=B)[:, :, b, :]

        with nc.Block() as block:
            @block.sync
            def _(sp):
                for dst, src in ((spread[:, :, :, :], "r_spread"), (in_bias[:, :], "r_in_bias"), (vecs[:, :, :], "r_vecs"),
                                 (hvecs[:, :], "r_hvecs"), (rms_w[:, :], "r_rms_w"), (group[:, :], "r_group"),
                                 (eps[:, :], "r_eps")):
                    sp.dma_start(dst, A[src]).then_inc(s["const"], 16)

            @block.scalar
            def _(act):
                act.wait_ge(s["const"], 7 * 16)
                nc.scalar.activation(dtc[:, 1:2], hvecs[:, 3:4], ACT.Abs).then_inc(s["e1"], 1)
                act.wait_ge(s["e1"], 1)
                nc.scalar.activation(dtc[:, 2:3], dtc[:, 1:2], ACT.Exp, scale=-1.0).then_inc(s["e1"], 1)
                act.wait_ge(s["e1"], 2)
                nc.scalar.activation(dtc[:, 3:4], dtc[:, 2:3], ACT.Ln, bias=1.0).then_inc(s["e1"], 1)

            @block.vector
            def _(dve):
                dve.wait_ge(s["e1"], 3)
                nc.vector.scalar_tensor_tensor(out=dtc[:, 0:1], in0=hvecs[:, 3:4], scalar=0.0, in1=dtc[:, 3:4],
                                               op0=ALU.max, op1=ALU.add).then_inc(s["win"], 1)

        with nc.Fori(0, B) as b:
            xn = scr[:, 0:2 * T].rearrange("p (k t) -> p k t", k=KD)
            with nc.Block() as block:
                @block.sync
                def _(sp):
                    sp.dma_start(weights[:, :], A["r_in_proj"]).then_inc(s["wload"], 16)

                @block.scalar
                def _(act):
                    for k in range(KD):
                        nc.scalar.activation(xn[:, k, :], tok(c.h, b)[:, k, :], ACT.Square).then_inc(s["sq"], 1)
                    for h in range(HALF):
                        act.wait_ge(s["ms"], b * HALF + h + 1)
                        nc.scalar.activation(scr[:, 2 * T + h * TT:2 * T + (h + 1) * TT], c.quad[h], ACT.Sqrt,
                                             bias=eps[:, 0:1]).then_inc(s["rt"], 1)

                @block.tensor
                def _(pe):
                    pe.wait_ge(s["sq"], (b + 1) * KD)
                    for h in range(HALF):
                        for k in range(KD):
                            last = nc.tensor.matmul(c.quad[h], c.mean_ones[:, :], xn[:, k, h * TT:(h + 1) * TT],
                                                    start=k == 0, stop=k == KD - 1)
                        last.then_inc(s["ms"], 1)

                @block.vector
                def _(dve):
                    for h in range(HALF):
                        dve.wait_ge(s["rt"], b * HALF + h + 1)
                        nc.vector.reciprocal(scr[:, 3 * T + h * TT:3 * T + (h + 1) * TT],
                                             scr[:, 2 * T + h * TT:2 * T + (h + 1) * TT]).then_inc(s["rcp"], 1)
                    dve.wait_ge(s["rcp"], b * 2 + 2)
                    for k in range(KD):
                        nc.vector.scalar_tensor_tensor(out=xn[:, k, :], in0=tok(c.h, b)[:, k, :], scalar=rms_w[:, k:k + 1],
                                                       in1=scr[:, 3 * T:4 * T], op0=ALU.mult, op1=ALU.mult)\
                            .then_inc(s["xn"], 1)

            PADT = T + 3
            vpad = flat[:, 0:KI * PADT].rearrange("p (m t) -> p m t", m=KI)
            conv = coef[:, 2, :].rearrange("p (m t) -> p m t", m=KI)
            w_in = weights[:, :].rearrange("p (k m) -> p k m", k=KD)
            order = list(range(16))
            with nc.Block() as block:
                @block.tensor
                def _(pe):
                    pe.wait_ge(s["wload"], b * 16 + 16)
                    pe.wait_ge(s["xn"], b * KD + KD)
                    for n, m in enumerate(order):
                        for h in range(HALF):
                            t = n * HALF + h
                            if t >= 4:
                                pe.wait_ge(s["ev"], b * 32 + t - 3)
                            for k in range(KD):
                                last = nc.tensor.matmul(c.quad[t % 4], w_in[:, k, m * P:(m + 1) * P],
                                                        xn[:, k, h * TT:(h + 1) * TT], start=k == 0, stop=k == KD - 1)
                            last.then_inc(s["mm"], 1)

                @block.scalar
                def _(act):
                    for n, m in enumerate(order):
                        for h in range(HALF):
                            t = n * HALF + h
                            act.wait_ge(s["mm"], b * 32 + t + 1)
                            cols = slice(h * TT, (h + 1) * TT)
                            if m < 4:
                                dst, f = vpad[:, m, 3 + h * TT:3 + (h + 1) * TT], ACT.Identity
                            elif m < 12:
                                dst, f = coef[:, 4 + (m - 4) // 4, :].rearrange("p (m t) -> p m t", m=KI)[:, (m - 4) % 4, cols], ACT.Identity
                            else:
                                dst, f = z[:, m - 12, cols], ACT.Silu
                            nc.scalar.activation(dst, c.quad[t % 4], f, bias=in_bias[:, m:m + 1]).then_inc(s["ev"], 1)
                    for m in range(KI):
                        act.wait_ge(s["acc"], b * 4 * KI + (m + 1) * 4)
                        nc.scalar.activation(u[:, m, :], conv[:, m, :], ACT.Silu, bias=vecs[:, m, 4:5]).then_inc(s["u"], 1)

                @block.vector
                def _(dve):
                    nc.vector.memset(vpad[:, :, 0:3], 0.0).then_inc(s["e1"], 1)
                    dve.wait_ge(s["e1"], b + 4)
                    for m in range(KI):
                        dve.wait_ge(s["ev"], b * 32 + 2 * m + 2)
                        for j in range(4):
                            n = b * 4 * KI + 4 * m + j
                            src = vpad[:, m, j:j + T]
                            if j == 0:
                                op = nc.vector.tensor_scalar(conv[:, m, :], src, vecs[:, m, 0:1], None, ALU.mult)
                            else:
                                dve.wait_ge(s["acc"], n)
                                op = nc.vector.scalar_tensor_tensor(out=conv[:, m, :], in0=src, scalar=vecs[:, m, j:j + 1],
                                                                    in1=conv[:, m, :], op0=ALU.mult, op1=ALU.add)
                            op.then_inc(s["acc"], 1)

            w_h = weights[:, 0:KI * 11 * H].rearrange("p (k q h) -> p k q h", k=KI, q=11)
            hq = weights[:, 2048:4096].rearrange("p (v t) -> p v t", v=8)
            tmp = scr[:, :].rearrange("p (v t) -> p v t", t=QW_)
            places = [H_ALPHA, H_OMEGA1, H_SELDT, H_SELB0, H_SELB1, H_SELC0, H_SELC1, H_BETA, H_RG, H_UG]

            def head_psum(q):
                i = places.index(q)
                bank = [c.quad[0], c.quad[1], c.quad[2], c.quad[3], c.bank[0][:, :]][i // 2]
                return bank[:, (i % 2) * QW_:(i % 2 + 1) * QW_]

            with nc.Block() as block:
                @block.sync
                def _(sp):
                    sp.dma_start(weights[:, 0:KI * 11 * H], A["r_head_w"]).then_inc(s["wload2"], 16)
                    sp.dma_start(tmp[:, 15, :], pos).then_inc(s["wload2"], 16)

                @block.tensor
                def _(pe):
                    pe.wait_ge(s["wload2"], b * 32 + 32)
                    for q in places:
                        rows = [q, H_OMEGA2] if q == H_OMEGA1 else [q]
                        out = head_psum(q)
                        terms = [(r, k) for r in rows for k in range(KI)]
                        for n, (r, k) in enumerate(terms):
                            for t in range(4):
                                last = nc.tensor.matmul(out[t * H:(t + 1) * H, :], w_h[:, k, r, :],
                                                        u[:, k, t * QW_:(t + 1) * QW_], start=n == 0, stop=n == len(terms) - 1)
                        last.then_inc(s["hmm"], 1)

                (T_AL, T_OM, T_E1, T_E2, T_L1, T_L2, T_R, T_UG, T_A, T_W, T_DET, T_LAM, T_X, T_Y, T_Z) = range(15)

                @block.scalar
                def _(act):
                    count = [0]

                    def step(out, in_, f, **kw):
                        nc.scalar.activation(out, in_, f, **kw).then_inc(s["h1"], 1)
                        count[0] += 1
                        return count[0]

                    def own():
                        act.wait_ge(s["h1"], b * 22 + count[0])

                    act.wait_ge(s["hmm"], b * 10 + 10)
                    step(tmp[:, T_AL, :], head_psum(H_ALPHA), ACT.Identity, bias=hvecs[:, 0:1])
                    step(hq[:, V_SB0, :], head_psum(H_SELB0), ACT.Copy)
                    step(hq[:, V_SB1, :], head_psum(H_SELB1), ACT.Copy)
                    step(hq[:, V_SC0, :], head_psum(H_SELC0), ACT.Copy)
                    step(hq[:, V_SC1, :], head_psum(H_SELC1), ACT.Copy)
                    step(hq[:, V_BETA, :], head_psum(H_BETA), ACT.Sigmoid, bias=hvecs[:, 4:5])
                    step(tmp[:, T_R, :], head_psum(H_RG), ACT.Sigmoid, bias=hvecs[:, 5:6])
                    step(tmp[:, T_UG, :], head_psum(H_UG), ACT.Sigmoid, bias=hvecs[:, 6:7])
                    own()
                    step(tmp[:, T_E1, :], tmp[:, T_AL, :], ACT.Abs)
                    step(tmp[:, T_E2, :], head_psum(H_SELDT), ACT.Abs)
                    own()
                    step(tmp[:, T_X, :], tmp[:, T_E1, :], ACT.Exp, scale=-1.0)
                    step(tmp[:, T_Y, :], tmp[:, T_E2, :], ACT.Exp, scale=-1.0)
                    own()
                    step(tmp[:, T_L1, :], tmp[:, T_X, :], ACT.Ln, bias=1.0)
                    step(tmp[:, T_L2, :], tmp[:, T_Y, :], ACT.Ln, bias=1.0)
                    act.wait_ge(s["h2"], b * 23 + 2)
                    step(tmp[:, T_Z, :], tmp[:, T_OM, :], ACT.Abs)
                    act.wait_ge(s["h2"], b * 23 + 9)
                    step(tmp[:, T_X, :], tmp[:, T_A, :], ACT.Square, bias=1.0)
                    step(tmp[:, T_Y, :], tmp[:, T_A, :], ACT.Square, bias=1.0, scale=-1.0)
                    step(tmp[:, T_Z, :], tmp[:, T_W, :], ACT.Square)
                    step(tmp[:, T_E1, :], tmp[:, T_A, :], ACT.Square)
                    act.wait_ge(s["h2"], b * 23 + 18)
                    step(tmp[:, T_L1, :], tmp[:, T_E2, :], ACT.Ln)
                    act.wait_ge(s["h2"], b * 23 + 19)
                    step(tmp[:, T_L2, :], tmp[:, T_L1, :], ACT.Exp)
                    act.wait_ge(s["h2"], b * 23 + 22)
                    step(tmp[:, T_L1, :], tmp[:, T_L2, :], ACT.Sqrt)
                    assert count[0] == 22

                @block.vector
                def _(dve):
                    count = [0]

                    def did(op):
                        op.then_inc(s["h2"], 1)
                        count[0] += 1

                    def own():
                        dve.wait_ge(s["h2"], b * 23 + count[0])

                    def acts(n):
                        dve.wait_ge(s["h1"], b * 22 + n)

                    tt, ts, stt = nc.vector.tensor_tensor, nc.vector.tensor_scalar, nc.vector.scalar_tensor_tensor
                    t_ = lambda i: tmp[:, i, :]
                    dve.wait_ge(s["hmm"], b * 10 + 10)
                    dve.wait_ge(s["wload2"], b * 32 + 32)
                    acts(10)
                    did(stt(out=t_(T_OM), in0=head_psum(H_OMEGA1), scalar=hvecs[:, 1:2], in1=t_(15), op0=ALU.add, op1=ALU.add))
                    own()
                    did(ts(t_(T_OM), t_(T_OM), hvecs[:, 2:3], None, ALU.add))
                    acts(15)
                    did(stt(out=t_(T_AL), in0=t_(T_AL), scalar=0.0, in1=t_(T_L1), op0=ALU.max, op1=ALU.add))
                    did(stt(out=t_(T_L2), in0=head_psum(H_SELDT), scalar=0.0, in1=t_(T_L2), op0=ALU.max, op1=ALU.add))
                    own()
                    did(stt(out=t_(T_Z), in0=t_(T_AL), scalar=1.0e-4, in1=t_(T_Z), op0=ALU.add, op1=ALU.add))
                    own()
                    did(nc.vector.reciprocal(t_(T_L1), t_(T_Z)))
                    own()
                    did(stt(out=t_(T_L1), in0=t_(T_L1), scalar=dtc[:, 0:1], in1=t_(T_L2), op0=ALU.mult, op1=ALU.add))
                    own()
                    did(stt(out=t_(T_A), in0=t_(T_L1), scalar=0.5, in1=t_(T_AL), op0=ALU.mult, op1=ALU.mult))
                    did(stt(out=t_(T_W), in0=t_(T_L1), scalar=0.5, in1=t_(T_OM), op0=ALU.mult, op1=ALU.mult))
                    acts(19)
                    did(tt(t_(T_DET), t_(T_X), t_(T_Z), ALU.add))
                    did(tt(t_(T_LAM), t_(T_Y), t_(T_Z), ALU.add))
                    own()
                    did(nc.vector.reciprocal(t_(T_X), t_(T_DET)))
                    did(stt(out=t_(T_E1), in0=t_(T_E1), scalar=-1.0, in1=t_(T_Z), op0=ALU.mult, op1=ALU.subtract))
                    own()
                    did(stt(out=hq[:, V_A11, :], in0=t_(T_E1), scalar=1.0, in1=t_(T_X), op0=ALU.add, op1=ALU.mult))
                    did(stt(out=hq[:, V_A12, :], in0=t_(T_W), scalar=2.0, in1=t_(T_X), op0=ALU.mult, op1=ALU.mult))
                    did(tt(t_(T_LAM), t_(T_LAM), t_(T_X), ALU.mult))
                    own()
                    did(ts(t_(T_Y), t_(T_LAM), 0.0, None, ALU.is_gt))
                    did(ts(t_(T_E2), t_(T_LAM), 2.0 ** -63, None, ALU.max))
                    acts(20)
                    did(tt(t_(T_L1), t_(T_L1), t_(T_R), ALU.mult))
                    acts(21)
                    did(tt(t_(T_L2), t_(T_L2), t_(T_Y), ALU.mult))
                    own()
                    did(ts(t_(T_L2), t_(T_L2), -1.0, 1.0, ALU.mult, ALU.add))
                    own()
                    did(ts(t_(T_L2), t_(T_L2), 1.0e-6, None, ALU.max))
                    acts(22)
                    did(tt(hq[:, V_VF, :], t_(T_L1), t_(T_UG), ALU.mult))
                    assert count[0] == 23

            units = [(m, h) for m in range(KI) for h in range(HALF)]
            NU = len(units)
            d_order = []
            D1 = ["kh0", "kh1", "t1", "t2", "t3", "t4", "bk0", "bk1", "v"]
            D2 = ["m00", "m01", "m10", "m11"]
            PO = ["c0", "c1", "e00", "e01", "e10", "e11", "b0", "b1"]
            for n in range(NU + 1):
                d_order += [(n, o) for o in D1] if n < NU else []
                d_order += [(n - 1, o) for o in D2] if n else []
            ND, NP_ = len(d_order), NU * len(PO)
            d_at = {o: i + 1 for i, o in enumerate(d_order)}

            def p_at(n, o):
                return n * len(PO) + PO.index(o) + 1

            values = [V_SB0, V_SB1, V_A11, V_A12, V_BETA, V_VF]

            def vbank(n, v):
                return {V_SB0: c.bank[0][:, :], V_SB1: c.bank[1][:, :], V_BETA: c.bank[2][:, :], V_VF: c.bank[3][:, :],
                        V_A11: c.quad[n % 2], V_A12: c.quad[2 + n % 2]}[v]

            def vlast(n, v):
                return d_at[n, {V_SB0: "kh0", V_SB1: "kh1", V_A11: "m11", V_A12: "m10", V_BETA: "bk1", V_VF: "v"}[v]]

            def part(slot, n):
                m, h = units[n]
                return coef[:, slot, m * T + h * TT:m * T + (h + 1) * TT]

            def temp(n, i):
                return scr[:, ((n % 2) * 3 + i) * TT:((n % 2) * 3 + i + 1) * TT]

            with nc.Block() as block:
                @block.tensor
                def _(pe):
                    for n, (m, h) in enumerate(units):
                        for v in values:
                            back = 2 if v in (V_A11, V_A12) else 1
                            if n >= back:
                                pe.wait_ge(s["cd"], b * ND + vlast(n - back, v))
                            for t in range(2):
                                last = nc.tensor.matmul(vbank(n, v)[:, t * QW_:(t + 1) * QW_], spread[:, 2 * h + t, m, :],
                                                        hq[:, v, :], start=True, stop=True)
                            last.then_inc(s["cb"], 1)

                @block.vector
                def _(dve):
                    def cb(n, v):
                        dve.wait_ge(s["cb"], b * NU * 6 + n * 6 + values.index(v) + 1)

                    def own(n, o):
                        dve.wait_ge(s["cd"], b * ND + d_at[n, o])

                    def pool(n, o):
                        dve.wait_ge(s["cp"], b * NP_ + p_at(n, o))

                    mul = lambda out, a, bb: nc.vector.tensor_tensor(out, a, bb, ALU.mult)
                    for n, o in d_order:
                        m, h = units[n]
                        kh0, kh1, v_ = temp(n, 0), temp(n, 1), temp(n, 2)
                        if o == "kh0":
                            cb(n, V_SB0)
                            if n >= 2:
                                pool(n - 2, "b1")
                            op = mul(kh0, part(4, n), vbank(n, V_SB0))
                        elif o == "kh1":
                            cb(n, V_SB1)
                            op = mul(kh1, part(5, n), vbank(n, V_SB1))
                        elif o == "t1":
                            cb(n, V_A11)
                            own(n, "kh0")
                            op = mul(part(0, n), kh0, vbank(n, V_A11))
                        elif o == "t2":
                            cb(n, V_A12)
                            own(n, "kh1")
                            op = mul(part(1, n), kh1, vbank(n, V_A12))
                        elif o == "t3":
                            op = mul(part(2, n), kh0, vbank(n, V_A12))
                        elif o == "t4":
                            op = mul(part(3, n), kh1, vbank(n, V_A11))
                        elif o == "bk0":
                            cb(n, V_BETA)
                            own(n, "t3")
                            op = mul(kh0, kh0, vbank(n, V_BETA))
                        elif o == "bk1":
                            own(n, "t4")
                            op = mul(kh1, kh1, vbank(n, V_BETA))
                        elif o == "v":
                            cb(n, V_VF)
                            op = mul(v_, u[:, m, h * TT:(h + 1) * TT], vbank(n, V_VF))
                        else:
                            i = D2.index(o)
                            pool(n, "e" + o[1:])
                            a = vbank(n, V_A12 if o in ("m01", "m10") else V_A11)
                            if o == "m10":
                                op = nc.vector.scalar_tensor_tensor(out=part(i, n), in0=a, scalar=-1.0, in1=part(i, n),
                                                                    op0=ALU.mult, op1=ALU.subtract)
                            else:
                                op = nc.vector.tensor_tensor(part(i, n), a, part(i, n), ALU.subtract)
                        op.then_inc(s["cd"], 1)

                @block.gpsimd
                def _(pool):
                    def dve(n, o):
                        pool.wait_ge(s["cd"], b * ND + d_at[n, o])

                    def own(n, o):
                        pool.wait_ge(s["cp"], b * NP_ + p_at(n, o))

                    tt = nc.gpsimd.tensor_tensor
                    for n in range(NU):
                        bk0, bk1, v_ = temp(n, 0), temp(n, 1), temp(n, 2)
                        dve(n, "t3")
                        tt(part(4, n), part(0, n), part(1, n), ALU.subtract).then_inc(s["cp"], 1)
                        dve(n, "t4")
                        tt(part(5, n), part(2, n), part(3, n), ALU.add).then_inc(s["cp"], 1)
                        dve(n, "bk1")
                        own(n, "c1")
                        for i, (x_, y_) in enumerate(((bk0, 4), (bk0, 5), (bk1, 4), (bk1, 5))):
                            tt(part(i, n), x_, part(y_, n), ALU.mult).then_inc(s["cp"], 1)
                        dve(n, "v")
                        own(n, "e11")
                        tt(part(4, n), bk0, v_, ALU.mult).then_inc(s["cp"], 1)
                        tt(part(5, n), bk1, v_, ALU.mult).then_inc(s["cp"], 1)

            def at(slot, l):
                return coef[:, slot, :].rearrange("p (n l) -> p l n", l=L_STEP)[:, l, :]

            four = coef[:, 0:4, :].rearrange("p (i j) (n l) -> p l i j n", i=2, l=L_STEP)
            X = scr[:, 0:6 * NB].rearrange("p (i n q) -> p i n q", i=2, q=3)
            prod = scr[:, 1024:1024 + 12 * NB].rearrange("p (i n q j) -> p i n q j", i=2, q=3, j=2)
            starts = scr[:, 3072:3072 + (CHUNKS + 1) * KI * 3].rearrange("p (s m q) -> p s m q", m=KI, q=3)
            small = scr[:, 3600:3600 + KI * 6].rearrange("p (i m q) -> p i m q", i=2, q=3)
            sums = scr[:, 3840:3840 + 2 * NB].rearrange("p (i n) -> p i n", i=2)
            prev = scr[:, 768:768 + 2 * NB].rearrange("p (j n) -> p j n", j=2)
            with nc.Block() as block:
                @block.sync
                def _(sp):
                    sp.dma_start(weights[:, 0:2048], A["r_q_w"][:, 0:2048]).then_inc(s["qload"], 16)

                @block.vector
                def _(dve):
                    tt = nc.vector.tensor_tensor
                    total = 6 + (L_STEP - 1) * 4 + 2 + CHUNKS * 2 + 2 + L_STEP * 3
                    count = [0]

                    def did(op):
                        op.then_inc(s["x1"], 1)
                        count[0] += 1

                    def own():
                        dve.wait_ge(s["x1"], b * total + count[0])

                    for i in range(2):
                        for j in range(2):
                            did(nc.vector.tensor_copy(X[:, i, :, j], at(2 * i + j, 0)))
                        did(nc.vector.tensor_copy(X[:, i, :, 2], at(4 + i, 0)))
                    for l in range(1, L_STEP):
                        own()
                        x_t = X[:, :, :, :].rearrange("p j n q -> p n q j")
                        for i in range(2):
                            m_t = four[:, l, i, :, :].rearrange("p j n -> p n j").unsqueeze(2).broadcast_to([P, NB, 3, 2])
                            did(tt(prod[:, i, :, :, :], m_t, x_t, ALU.mult))
                        own()
                        did(tt(X[:, :, :, :].rearrange("p i n q -> p (i n q)"),
                               prod[:, :, :, :, 0].rearrange("p i n q -> p (i n q)"),
                               prod[:, :, :, :, 1].rearrange("p i n q -> p (i n q)"), ALU.add))
                        own()
                        off = coef[:, 4:6, :].rearrange("p i (n l) -> p l i n", l=L_STEP)[:, l, :, :]
                        did(tt(X[:, :, :, 2], X[:, :, :, 2], off, ALU.add))
                    did(nc.vector.memset(starts[:, :, :, :], 0.0))
                    own()
                    for k in range(CHUNKS):
                        xs = X[:, :, :, :].rearrange("p i (m s) q -> p s i m q", m=KI)[:, k, :, :, :]
                        st = starts[:, k, :, :].unsqueeze(1).broadcast_to([P, 2, KI, 3])
                        if k == 0:
                            did(nc.vector.memset(starts[:, :, :, 2:3], 1.0))
                            own()
                            did(tt(small[:, :, :, :], xs, st, ALU.mult))
                        else:
                            did(tt(small[:, :, :, :], xs, st, ALU.mult))
                        own()
                        did(nc.vector.tensor_reduce(starts[:, k + 1, :, 0:2].rearrange("p m i -> p i m"), small[:, :, :, :],
                                                    AX, ALU.add))
                        own()
                    for j in range(2):
                        did(nc.vector.tensor_copy(prev[:, j, :].rearrange("p (m s) -> p m s", m=KI),
                                                  starts[:, 0:CHUNKS, :, j].rearrange("p s m -> p m s")))
                    p3 = scr[:, 1024:1024 + 4 * NB].rearrange("p (i n j) -> p i n j", i=2, j=2)
                    for l in range(L_STEP):
                        own()
                        for i in range(2):
                            before = prev[:, :, :] if l == 0 else \
                                coef[:, 4:6, :].rearrange("p j (n l) -> p l j n", l=L_STEP)[:, l - 1, :, :]
                            op = tt(p3[:, i, :, :].rearrange("p n j -> p j n"), four[:, l, i, :, :], before, ALU.mult)
                            if i:
                                did(op)
                            else:
                                op.then_inc(s["p2"], 1)
                        dve.wait_ge(s["p2"], b * L_STEP + l + 1)
                        own()
                        did(tt(sums[:, :, :], p3[:, :, :, 0], p3[:, :, :, 1], ALU.add))
                        own()
                        off = coef[:, 4:6, :].rearrange("p i (n l) -> p l i n", l=L_STEP)[:, l, :, :]
                        did(tt(off, sums[:, :, :], off, ALU.add))
                    assert count[0] == total

            w_q = weights[:, 0:2048]
            ybuf = coef[:, 0, :].rearrange("p (m t) -> p m t", m=KI)
            with nc.Block() as block:
                @block.sync
                def _(sp):
                    sp.wait_ge(s["d3"], b + 1)
                    sp.dma_start(weights[:, 0:2048], A["r_q_w"][:, 2048:4096]).then_inc(s["qload"], 16)

                @block.tensor
                def _(pe):
                    for n, (m, h) in enumerate(units):
                        if n == 0:
                            pe.wait_ge(s["qload"], b * 32 + 16)
                        if n == NU // 2:
                            pe.wait_ge(s["qload"], b * 32 + 32)
                        if n >= 2:
                            pe.wait_ge(s["d1"], b * NU * 4 + 4 * (n - 2) + 4)
                        for j in range(2):
                            bank = c.quad[2 * (n % 2) + j]
                            for k in range(KI):
                                w_ = w_q.rearrange("p (m j k o) -> p m j k o", m=2, j=2, k=KI)[:, m % 2, j, k, :]
                                last = nc.tensor.matmul(bank, w_, u[:, k, h * TT:(h + 1) * TT], start=k == 0, stop=k == KI - 1)
                            bank = c.bank[2 * (n % 2) + j]
                            for t in range(2):
                                last = nc.tensor.matmul(bank[:, t * QW_:(t + 1) * QW_], spread[:, 2 * h + t, m, :],
                                                        hq[:, V_SC0 + j, :], start=True, stop=True)
                        last.then_inc(s["qmm"], 1)
                        if n == NU // 2 - 1:
                            pe.wait_ge(s["qmm"], b * NU + n + 1)
                            pe.sem_inc(s["d3"], 1)

                @block.vector
                def _(dve):
                    for n, (m, h) in enumerate(units):
                        dve.wait_ge(s["qmm"], b * NU + n + 1)
                        for j in range(2):
                            nc.vector.tensor_tensor(part(4 + j, n), part(4 + j, n), c.bank[2 * (n % 2) + j][:, :], ALU.mult)\
                                .then_inc(s["d1"], 1)
                        for j in range(2):
                            dve.wait_ge(s["d1"], b * NU * 4 + 4 * n + j + 1)
                            nc.vector.tensor_tensor(part(4 + j, n), part(4 + j, n), c.quad[2 * (n % 2) + j], ALU.mult)\
                                .then_inc(s["d1"], 1)

                @block.gpsimd
                def _(pool):
                    for n in range(NU):
                        pool.wait_ge(s["d1"], b * NU * 4 + 4 * n + 4)
                        nc.gpsimd.tensor_tensor(part(0, n), part(4, n), part(5, n), ALU.add).then_inc(s["d2"], 1)
                        if n == 0:
                            pool.sem_inc(s["passed"], 1)

            with nc.Block() as block:
                @block.scalar
                def _(act):
                    for m in range(KI):
                        nc.scalar.activation(scr[:, 0:T], ybuf[:, m, :], ACT.Copy, accum_out=stat[:, m, 0:1]).then_inc(s["g1"], 1)
                        act.wait_ge(s["g1"], b * 2 * KI + m + 1)
                    act.wait_ge(s["g2"], b * 2 + 1)
                    for m in range(KI):
                        nc.scalar.activation(scr[:, 0:T], ybuf[:, m, :], ACT.Square, bias=stat[:, m, 1:2],
                                             accum_out=stat[:, m, 2:3]).then_inc(s["g1"], 1)
                        act.wait_ge(s["g1"], b * 2 * KI + KI + m + 1)
                    act.wait_ge(s["g3"], b * 2 + 2)
                    nc.scalar.activation(stat[:, :, 3], c.quad[1][:, 0:KI], ACT.Sqrt, bias=eps[:, 1:2]).then_inc(s["g4"], 1)
                    act.wait_ge(s["g2"], b * 2 + 2)
                    for m in range(KI):
                        nc.scalar.activation(ybuf[:, m, :], ybuf[:, m, :], ACT.Identity, bias=stat[:, m, 6:7],
                                             scale=stat[:, m, 5:6]).then_inc(s["g5"], 1)

                @block.tensor
                def _(pe):
                    for i in range(2):
                        pe.wait_ge(s["g1"], b * 2 * KI + (i + 1) * KI)
                        nc.tensor.matmul(c.quad[i][:, 0:KI], group[:, :], stat[:, :, 2 * i], start=True, stop=True)\
                            .then_inc(s["g3"], 1)

                @block.vector
                def _(dve):
                    dve.wait_ge(s["g3"], b * 2 + 1)
                    nc.vector.tensor_scalar(stat[:, :, 1], c.quad[0][:, 0:KI], -1.0, None, ALU.mult).then_inc(s["g2"], 1)
                    dve.wait_ge(s["g4"], b + 1)
                    nc.vector.reciprocal(stat[:, :, 4], stat[:, :, 3]).then_inc(s["p3"], 1)
                    dve.wait_ge(s["p3"], b * (3 + 2 * KI) + 1)
                    nc.vector.tensor_tensor(stat[:, :, 5], stat[:, :, 4], vecs[:, :, 5], ALU.mult).then_inc(s["p3"], 1)
                    dve.wait_ge(s["p3"], b * (3 + 2 * KI) + 2)
                    nc.vector.tensor_tensor(stat[:, :, 7], stat[:, :, 5], stat[:, :, 1], ALU.mult).then_inc(s["p3"], 1)
                    dve.wait_ge(s["p3"], b * (3 + 2 * KI) + 3)
                    nc.vector.tensor_tensor(stat[:, :, 6], stat[:, :, 7], vecs[:, :, 6], ALU.add).then_inc(s["g2"], 1)
                    for m in range(KI):
                        dve.wait_ge(s["g5"], b * KI + m + 1)
                        nc.vector.tensor_tensor(ybuf[:, m, :], ybuf[:, m, :], z[:, m, :], ALU.mult).then_inc(s["p3"], 1)
                        dve.wait_ge(s["p3"], b * (3 + 2 * KI) + 3 + 2 * m + 1)
                        nc.vector.scalar_tensor_tensor(out=ybuf[:, m, :], in0=u[:, m, :], scalar=vecs[:, m, 7:8], in1=ybuf[:, m, :],
                                                       op0=ALU.mult, op1=ALU.add).then_inc(s["p3"], 1)
                    dve.wait_ge(s["p3"], (b + 1) * (3 + 2 * KI))
                    dve.sem_inc(s["passed"], 1)

                @block.sync
                def _(sp):
                    sp.dma_start(weights[:, 0:KI * D], A["r_out_w"]).then_inc(s["oload"], 16)

            w_o = weights[:, 0:KI * D].rearrange("p (k m) -> p k m", k=KI)
            with nc.Block() as block:
                @block.tensor
                def _(pe):
                    pe.wait_ge(s["oload"], b * 16 + 16)
                    for m in range(KD):
                        for h in range(HALF):
                            for k in range(KI):
                                last = nc.tensor.matmul(c.quad[m * HALF + h], w_o[:, k, m * P:(m + 1) * P],
                                                        ybuf[:, k, h * TT:(h + 1) * TT], start=k == 0, stop=k == KI - 1)
                            last.then_inc(s["omm"], 1)

                @block.vector
                def _(dve):
                    for m in range(KD):
                        x = tok(c.x, b)[:, m, :]
                        nc.vector.tensor_tensor(x, x, tok(c.h, b)[:, m, :], ALU.add).then_inc(s["oadd"], 1)
                    dve.wait_ge(s["oadd"], b * (KD + KD * HALF) + KD)
                    for m in range(KD):
                        for h in range(HALF):
                            dve.wait_ge(s["omm"], b * KD * HALF + m * HALF + h + 1)
                            x = tok(c.x, b)[:, m, h * TT:(h + 1) * TT]
                            nc.vector.tensor_tensor(x, c.quad[m * HALF + h], x, ALU.add).then_inc(s["oadd"], 1)


def gated_weight(c, A, v):
    nc = c.nc
    loaded, step, made, mm, ev = (c.sem(f"gw_{n}") for n in ("loaded", "step", "made", "mm", "ev"))
    with ExitStack() as ctx:
        w = c.sb("gw_w", [P, E, KD * D], ctx=ctx)
        mask = c.sb("gw_mask", [P, KD * D], ctx=ctx)
        bias = c.sb("gw_bias", [P, KD], ctx=ctx)
        w_b = c.sb("gw_w_b", [P, B, KD * D], ctx=ctx)
        with nc.Block() as block:
            @block.sync
            def _(sp):
                for dst, src in ((w[:, :, :], "L1_cond2_weight"), (mask[:, :], "L1_cond2_mask"), (bias[:, :], "L1_cond2_bias")):
                    sp.dma_start(dst, A[src]).then_inc(loaded, 16)

            @block.vector
            def _(dve):
                dve.wait_ge(loaded, 3 * 16)
                n = 0
                for g in range(E + 1):
                    for b in range(B):
                        if g:
                            dve.wait_ge(step, n - 1)
                        if g == 0:
                            op = nc.vector.tensor_scalar(w_b[:, b, :], w[:, 0, :], c.cond[:, b, 0:1], None, ALU.mult)
                        elif g < E:
                            op = nc.vector.scalar_tensor_tensor(out=w_b[:, b, :], in0=w[:, g, :], scalar=c.cond[:, b, g:g + 1],
                                                                in1=w_b[:, b, :], op0=ALU.mult, op1=ALU.add)
                        else:
                            op = nc.vector.tensor_tensor(w_b[:, b, :], w_b[:, b, :], mask[:, :], ALU.mult)
                        op.then_inc(step, 1)
                        n += 1

            @block.tensor
            def _(pe):
                n = 0
                for b in range(B):
                    pe.wait_ge(step, B * E + b + 1)
                    for t in range(T // TT):
                        for m in range(KD):
                            if n >= 4:
                                pe.wait_ge(ev, n - 3)
                            for k in range(KD):
                                last = nc.tensor.matmul(c.quad[n % 4], w_b[:, b, k * D + m * P:k * D + (m + 1) * P],
                                                        c.x[:, k, b * T + t * TT:b * T + (t + 1) * TT],
                                                        start=k == 0, stop=k == KD - 1)
                            last.then_inc(mm, 1)
                            n += 1

            @block.scalar
            def _(act):
                n = 0
                for b in range(B):
                    for t in range(T // TT):
                        for m in range(KD):
                            act.wait_ge(mm, n + 1)
                            nc.scalar.activation(v[:, m, b * T + t * TT:b * T + (t + 1) * TT], c.quad[n % 4],
                                                 ACT.Identity, bias=bias[:, m:m + 1]).then_inc(ev, 1)
                            n += 1


def layer_norm(c, A, tag, src, dst, params):
    nc = c.nc
    s = {n: c.sem(f"{tag}_{n}") for n in "loaded mm1 cen sq mm2 root rcp mul out".split()}
    with ExitStack() as ctx:
        vec = c.sb(f"{tag}_vec", [P, 2 * KD + 1], ctx=ctx)
        cen = c.sb(f"{tag}_cen", [P, NT, KD, TT], ctx=ctx)
        sq = c.sb(f"{tag}_sq", [P, NT, KD, TT], ctx=ctx)
        root = c.sb(f"{tag}_root", [P, NT, TT], ctx=ctx)
        rcp = c.sb(f"{tag}_rcp", [P, NT, TT], ctx=ctx)
        with nc.Block() as block:
            @block.sync
            def _(sp):
                sp.dma_start(vec[:, :], A[params]).then_inc(s["loaded"], 16)

            @block.tensor
            def _(pe):
                for t in range(NT):
                    for k in range(KD):
                        last = nc.tensor.matmul(c.quad[t], c.mean_ones[:, :], src[:, k, t * TT:(t + 1) * TT],
                                                start=k == 0, stop=k == KD - 1)
                    last.then_inc(s["mm1"], 1)
                for t in range(NT):
                    for k in range(KD):
                        pe.wait_ge(s["sq"], t * KD + k + 1)
                        last = nc.tensor.matmul(c.bank[t][:, :], c.mean_ones[:, :], sq[:, t, k, :],
                                                start=k == 0, stop=k == KD - 1)
                    last.then_inc(s["mm2"], 1)

            @block.vector
            def _(dve):
                dve.wait_ge(s["loaded"], 16)
                for t in range(NT):
                    dve.wait_ge(s["mm1"], t + 1)
                    for k in range(KD):
                        nc.vector.tensor_tensor(cen[:, t, k, :], src[:, k, t * TT:(t + 1) * TT], c.quad[t], ALU.subtract)\
                            .then_inc(s["cen"], 1)
                for t in range(NT):
                    dve.wait_ge(s["root"], t + 1)
                    nc.vector.reciprocal(rcp[:, t, :], root[:, t, :]).then_inc(s["rcp"], 1)
                    dve.wait_ge(s["rcp"], t + 1)
                    for k in range(KD):
                        nc.vector.scalar_tensor_tensor(out=cen[:, t, k, :], in0=cen[:, t, k, :], scalar=vec[:, k:k + 1],
                                                       in1=rcp[:, t, :], op0=ALU.mult, op1=ALU.mult).then_inc(s["mul"], 1)

            @block.scalar
            def _(act):
                act.wait_ge(s["loaded"], 16)
                for t in range(NT):
                    for k in range(KD):
                        act.wait_ge(s["cen"], t * KD + k + 1)
                        nc.scalar.activation(sq[:, t, k, :], cen[:, t, k, :], ACT.Square).then_inc(s["sq"], 1)
                for t in range(NT):
                    act.wait_ge(s["mm2"], t + 1)
                    nc.scalar.activation(root[:, t, :], c.bank[t][:, :], ACT.Sqrt, bias=vec[:, 2 * KD:2 * KD + 1])\
                        .then_inc(s["root"], 1)
                for t in range(NT):
                    for k in range(KD):
                        act.wait_ge(s["mul"], t * KD + k + 1)
                        nc.scalar.activation(dst[:, k, t * TT:(t + 1) * TT], cen[:, t, k, :], ACT.Identity,
                                             bias=vec[:, KD + k:KD + k + 1]).then_inc(s["out"], 1)


def router(c, A, v, table):
    nc = c.nc
    TL = N // P
    s = {n: c.sem(f"ro_{n}") for n in "loaded mm sc top idx gap exp den p1 p2 oh w tr cp out add".split()}
    with ExitStack() as ctx:
        gate = c.sb("ro_gate", [P, KD, E], ctx=ctx)
        number = c.sb("ro_number", [P, TL, E], ctx=ctx)
        score = c.sb("ro_score", [P, TL, E], ctx=ctx)
        top = c.sb("ro_top", [P, TL, 8], ctx=ctx)
        idx = c.sb("ro_idx", [P, TL, 8], U32, ctx=ctx)
        idx_f = c.sb("ro_idx_f", [P, TL, 2], ctx=ctx)
        prob = c.sb("ro_prob", [P, 4, TL], ctx=ctx)
        hot = c.sb("ro_hot", [P, 2, TL, E], ctx=ctx)
        w_t = c.sb("ro_w_t", [E, N], ctx=ctx)
        with nc.Block() as block:
            @block.sync
            def _(sp):
                sp.dma_start(gate[:, :, :], A["L1_ffn_gate_w"]).then_inc(s["loaded"], 16)
                sp.dma_start(number[:, :, :], A["number"]).then_inc(s["loaded"], 16)
                sp.wait_ge(s["cp"], 4)
                sp.dma_start(table, w_t[:, :]).then_inc(s["out"], 16)
                sp.wait_ge(s["out"], 16)

            @block.tensor
            def _(pe):
                pe.wait_ge(s["loaded"], 32)
                for t in range(TL):
                    for k in range(KD):
                        last = nc.tensor.matmul(c.quad[0][:, t * E:(t + 1) * E], c.h[:, k, t * P:(t + 1) * P], gate[:, k, :],
                                                start=k == 0, stop=k == KD - 1)
                last.then_inc(s["mm"], 1)
                pe.wait_ge(s["w"], 1)
                for q in range(4):
                    for t in range(4):
                        last = nc.tensor.transpose(c.bank[q][0:E, t * P:(t + 1) * P], hot[:, 0, 4 * q + t, :], c.ident[:, :])
                    last.then_inc(s["tr"], 1)

            @block.scalar
            def _(act):
                act.wait_ge(s["gap"], 1)
                nc.scalar.activation(prob[:, 1, :], prob[:, 0, :], ACT.Exp).then_inc(s["exp"], 1)
                for q in range(4):
                    act.wait_ge(s["tr"], q + 1)
                    nc.scalar.activation(w_t[:, q * 512:(q + 1) * 512], c.bank[q][0:E, :], ACT.Copy).then_inc(s["cp"], 1)

            @block.gpsimd
            def _(pool):
                for k in range(KD):
                    nc.gpsimd.tensor_tensor(c.x[:, k, :], c.x[:, k, :], v[:, k, :], ALU.add).then_inc(s["add"], 1)

            @block.vector
            def _(dve):
                dve.wait_ge(s["mm"], 1)
                nc.vector.tensor_copy(score[:, :, :].rearrange("p t e -> p (t e)"), c.quad[0][:, 0:TL * E]).then_inc(s["sc"], 1)
                dve.wait_ge(s["sc"], 1)
                for t in range(TL):
                    nc.vector.max(top[:, t, :], score[:, t, :]).then_inc(s["top"], 1)
                for t in range(TL):
                    dve.wait_ge(s["top"], t + 1)
                    nc.vector.max_index(idx[:, t, :], top[:, t, :], score[:, t, :]).then_inc(s["idx"], 1)
                nc.vector.tensor_tensor(prob[:, 0, :], top[:, :, 1], top[:, :, 0], ALU.subtract).then_inc(s["gap"], 1)
                dve.wait_ge(s["idx"], TL)
                nc.vector.tensor_copy(idx_f[:, :, :], idx[:, :, 0:2]).then_inc(s["idx"], 1)
                dve.wait_ge(s["exp"], 1)
                nc.vector.tensor_scalar(prob[:, 3, :], prob[:, 1, :], 1.0, None, ALU.add).then_inc(s["den"], 1)
                dve.wait_ge(s["den"], 1)
                nc.vector.reciprocal(prob[:, 2, :], prob[:, 3, :]).then_inc(s["p1"], 1)
                dve.wait_ge(s["p1"], 1)
                nc.vector.tensor_tensor(prob[:, 3, :], prob[:, 1, :], prob[:, 2, :], ALU.mult).then_inc(s["p2"], 1)
                dve.wait_ge(s["idx"], TL + 1)
                for i in range(2):
                    nc.vector.tensor_tensor(hot[:, i, :, :], number[:, :, :], idx_f[:, :, i:i + 1].broadcast_to([P, TL, E]),
                                            ALU.is_equal).then_inc(s["oh"], 1)
                dve.wait_ge(s["p2"], 1)
                for i in range(2):
                    dve.wait_ge(s["oh"], i + 1)
                    nc.vector.tensor_tensor(hot[:, i, :, :], hot[:, i, :, :],
                                            prob[:, 2 + i, :].unsqueeze(2).broadcast_to([P, TL, E]), ALU.mult)\
                        .then_inc(s["oh"], 1)
                dve.wait_ge(s["oh"], 4)
                nc.vector.tensor_tensor(hot[:, 0, :, :], hot[:, 0, :, :], hot[:, 1, :, :], ALU.add).then_inc(s["w"], 1)


def mixture(c, A, table):
    nc = c.nc
    part_done = c.sem("mx_part_done")
    with ExitStack() as ctx:
        x_hi = c.sb("mx_x_hi", [P, KD, N], F32R, ctx=ctx)
        x_lo = c.sb("mx_x_lo", [P, KD, N], F32R, ctx=ctx)
        wt = c.sb("mx_wt", [P, 2, N], ctx=ctx)
        part = c.sb("mx_part", [P, KD, TT], ctx=ctx)
        split(c, "mx", c.h, x_hi, x_lo)
        tiles = [[t * TT for t in range(NT)] for _ in range(2)]

        def source(sp, r, s):
            e = r * 2 + s
            return lambda p: A["L1_ffn_experts"][e, p, :, :]

        def load_extra(sp, r, s, unit, q):
            sp.wait_ge(q["extra_free"], r * 2 + s + 1)
            sp.dma_start(wt[:, s, :], table[bass.ds(r * 2 + s, 1), :].broadcast_to([P, N])).then_inc(q[f"extra{s}"], 16)

        def finish(dve, r, s, o, t0, psum, q):
            n = s * NT + t0 // TT
            if o == 0:
                dve.wait_ge(q[f"extra{s}"], r * 16 + 16)
            dve.wait_ge(q["y_part"], r * 2 * NT * KD + n * KD + o + 1)
            nc.vector.tensor_tensor(part[:, o, :], psum, wt[:, s, t0:t0 + TT], ALU.mult).then_inc(part_done, 1)
            dve.wait_ge(part_done, r * 2 * NT * KD + n * KD + o + 1)
            y = c.x[:, o, t0:t0 + TT]
            nc.vector.tensor_tensor(y, y, part[:, o, :], ALU.add).then_inc(q["y_part"], 1)
            if o == KD - 1:
                dve.wait_ge(q["y_part"], 1 + r * 2 * NT * KD + n * KD + o + 1)
                return dve
            return None

        gated_mlp(c, "mx", 4, 4, tiles, source, ACT.Silu, x_hi, x_lo, c.x, load_extra=load_extra, finish=finish)


def build(nc, A, out):
    table = nc.dram_tensor("expert_weights", [E, N], F32, kind="Internal").ap()
    with ExitStack() as ctx:
        c = Chip(nc, ctx)
        setup(c, A)
        merged_input(c, A)
        attention(c, A, "a0", "L0_qkv", "L0_wo", "zero_bias", c.x)
        two_of_eight(c, A)
        spectral(c, A)
        c.end_layer()
        chosen_expert(c, A)
        recurrent(c, A)
        last_branch(c, A, table)
        stored = c.sem("stored")
        with nc.Block() as block:
            @block.sync
            def _(sp):
                sp.dma_start(out, c.x[:, :, :]).then_inc(stored, 16)
                sp.wait_ge(stored, 16)


def last_branch(c, A, table):
    with ExitStack() as ctx:
        v = c.sb("branch", [P, KD, N], ctx=ctx)
        gated_weight(c, A, v)
        layer_norm(c, A, "n1", v, c.h, "L1_ffn_ln1")
        attention(c, A, "a1", "L1_qkv", "L1_wo", "L1_bo", v)
        layer_norm(c, A, "n2", v, c.h, "L1_ffn_ln2")
        router(c, A, v, table)
    mixture(c, A, table)



def _rows(w):
    return w.reshape(w.shape[0] // P, P, *w.shape[1:]).swapaxes(0, 1)


def _features(x):
    return _rows(x.transpose(2, 0, 1).reshape(x.shape[2], -1))


def _column(v):
    return v.reshape(-1, P).T


def _slots(w):
    out = np.zeros((w.shape[0], GROUPS, GH, SLOT), w.dtype)
    out[..., :HD] = w.reshape(w.shape[0], GROUPS, GH, HD)
    return out


def _qkv(wq, wk, wv):
    parts = [_slots(w).reshape(KD, P, GROUPS, P).transpose(2, 1, 0, 3) for w in (wq, wk, wv)]
    return np.stack(parts, 2)


def _out_rows(w):
    out = np.zeros((GROUPS, GH, SLOT, D), w.dtype)
    out[:, :, :HD] = w.reshape(GROUPS, GH, HD, D)
    return out.reshape(GROUPS, P, D).transpose(1, 0, 2)


def _constants():
    f = np.float32
    ident = np.eye(P, dtype=f)
    row = np.arange(P)
    extra = (row % SLOT == HD)
    pick = (extra[:, None] & (row[:, None] // SLOT == row[None, :] // SLOT)).astype(f)
    causal = np.zeros((P, T), f)
    causal[:, T - P:] = np.where(row[None, :] > row[:, None], -1.0e30, 0.0)
    freq = np.arange(D)
    angle = 2 * np.pi * ((freq[:, None] * freq[None, :]) % D) / D
    return {
        "ident": ident, "neg_ident": -ident, "mean_ones": np.full((P, P), 1.0 / D, f), "sum_pick": pick,
        "k_ones": extra.astype(f)[:, None], "v_ones": np.tile(extra.astype(f)[None, :], (P, 4)), "causal": causal,
        "zero_bias": np.zeros((P, KD), f),
        "dft": np.stack([_rows(np.cos(angle).astype(f)), _rows(np.sin(angle).astype(f)), _rows(-np.sin(angle).astype(f))], 1),
    }


def _recurrent(i):
    f = np.float32
    a = {}
    w, bias = i["L1_attn_in_proj_W"], i["L1_attn_in_proj_b"]
    rows = np.concatenate([np.arange(3 * DI, 4 * DI), np.arange(DI, 3 * DI, 2), np.arange(DI + 1, 3 * DI, 2), np.arange(DI)])
    a["r_in_proj"] = _rows(w[rows].T).reshape(P, -1)
    a["r_in_bias"] = _column(bias[rows])
    cols = [*i["L1_attn_conv_w"].T, i["L1_attn_conv_b"], i["L1_attn_gn_w"], i["L1_attn_gn_b"], i["L1_attn_D"], i["L1_attn_D"]]
    a["r_vecs"] = np.stack([_column(v) for v in cols], 2)
    a["r_rms_w"] = _column(i["L1_attn_rms_w"])
    dyn, selb, selc = i["L1_attn_dyn_W"], i["L1_attn_selB_W"], i["L1_attn_selC_W"]
    heads = [dyn[:H], dyn[H:2 * H], dyn[2 * H:], selb[0::2], selb[1::2], selc[0::2], selc[1::2],
             i["L1_attn_seldt_W"], i["L1_attn_beta_W"], i["L1_attn_rg_W"], i["L1_attn_ug_W"]]
    a["r_head_w"] = _rows(np.concatenate(heads).T).reshape(P, -1)
    db = i["L1_attn_dyn_b"]
    hv = [db[:H], db[H:2 * H], db[2 * H:], i["L1_attn_dt_c"], i["L1_attn_beta_b"], i["L1_attn_rg_b"], i["L1_attn_ug_b"],
          i["L1_attn_ug_b"]]
    a["r_hvecs"] = np.tile(np.stack(hv, 1), (4, 1))
    q = i["L1_attn_Q_W"].reshape(KI, P, 2, KI, P).transpose(4, 0, 2, 3, 1)
    a["r_q_w"] = q.reshape(P, -1)
    a["r_out_w"] = _rows(i["L1_attn_out_W"].T).reshape(P, -1)
    row, ch = np.arange(P), np.arange(DI)
    spread = np.zeros((P, 4, KI, P), f)
    for t in range(4):
        for m in range(KI):
            spread[:, t, m, :] = row[:, None] == t * H + (ch[None, m * P:(m + 1) * P] // 16)
    a["r_spread"] = spread
    a["r_group"] = (row[:, None] // 16 == row[None, :] // 16).astype(f) / f(16 * T)
    rope = (f(1.0) / (f(10000.0) ** (np.arange(H, dtype=f) / f(H)))).astype(f)
    a["r_pos"] = (np.arange(T, dtype=f).reshape(4, 1, QW_) * rope[None, :, None]).reshape(P, QW_)
    a["r_eps"] = np.tile(np.array([[1e-6, 1e-5]], f), (P, 1))
    return a


def _lay_out(i):
    a = _constants()
    a["x"] = _features(i["x"])
    a["cond_all"] = np.broadcast_to(i["cond_8"][None], (P, B, E))
    a["cond_er"] = np.repeat(i["cond_8"].T, P // E, axis=0)
    a["L0_cond_As"] = i["L0_cond_As"].reshape(P, D)
    a["L0_cond_Bs"] = i["L0_cond_Bs"].transpose(0, 2, 1).reshape(P, D)
    a["L0_cond_W_base"] = _rows(i["L0_cond_W_base"].T)
    a["L0_cond_b_base"] = _column(i["L0_cond_b_base"])
    a["L0_qkv"] = _qkv(i["L0_attn_Wq"].T, i["L0_attn_Wk"].T, i["L0_attn_Wv"].T)
    a["L0_wo"] = _out_rows(i["L0_attn_Wo"].T)

    def parts(gate, up, down):
        def rows(w):
            return w.reshape(w.shape[0], -1, P, w.shape[2]).swapaxes(1, 2).reshape(w.shape[0], P, -1)
        return np.stack([rows(gate), rows(up), rows(down)], 1)

    a["L0_cond2_experts"] = np.concatenate([
        parts(i["L0_cond2_skill_gate"], i["L0_cond2_skill_up"], i["L0_cond2_skill_down"]),
        parts(i["L0_cond2_shared_gate"][None], i["L0_cond2_shared_up"][None], i["L0_cond2_shared_down"][None])])
    a["L0_ffn_wr"] = _rows(i["L0_ffn_w_freq_real"])
    a["L0_ffn_wi"] = _rows(i["L0_ffn_w_freq_imag"])
    a["L0_ffn_bias"] = _column(i["L0_ffn_bias"])
    a["L1_cond_experts"] = parts(*(i[f"L1_cond_W_{n}"].transpose(0, 2, 1) for n in ("up", "gate", "down")))
    a["L1_cond_biases"] = np.concatenate([i[f"L1_cond_b_{n}"].reshape(E, -1, P).swapaxes(1, 2)
                                          for n in ("up", "gate", "down")], 2)
    a.update(_recurrent(i))
    a["number"] = np.tile(np.arange(E, dtype=np.float32), (P, N // P, 1))
    a["L1_cond2_weight"] = _rows(i["L1_cond2_weight"].transpose(2, 0, 1)).transpose(0, 2, 1, 3).reshape(P, E, -1)
    a["L1_cond2_mask"] = _rows(i["L1_cond2_mask"].T).reshape(P, -1)
    a["L1_cond2_bias"] = _column(i["L1_cond2_bias"])
    eps = np.full((P, 1), 1e-5, np.float32)
    for n in ("ln1", "ln2"):
        a[f"L1_ffn_{n}"] = np.concatenate([_column(i[f"L1_ffn_{n}_scale"]), _column(i[f"L1_ffn_{n}_shift"]), eps], 1)
    a["L1_qkv"] = _qkv(i["L1_ffn_wq"], i["L1_ffn_wk"], i["L1_ffn_wv"])
    a["L1_wo"] = _out_rows(i["L1_ffn_wo"])
    a["L1_bo"] = _column(i["L1_ffn_bo"])
    a["L1_ffn_gate_w"] = _rows(i["L1_ffn_gate_w"])
    a["L1_ffn_experts"] = parts(i["L1_ffn_w1"], i["L1_ffn_w2"], i["L1_ffn_w3"])
    return a


def kernel(**inputs):
    import concourse.bacc as bacc
    from concourse.bass_utils import run_bass_kernel_spmd

    host = {n: np.asarray(x) for n, x in inputs.items()}
    arrays = {n: np.ascontiguousarray(x) for n, x in _lay_out(host).items()}
    nc = bacc.Bacc("TRN2", target_bir_lowering=False, num_devices=1)
    A = {n: nc.dram_tensor(f"in_{n}", x.shape, mybir.dt.from_np(x.dtype), kind="ExternalInput").ap() for n, x in arrays.items()}
    out = nc.dram_tensor("out_features", (P, KD, N), F32, kind="ExternalOutput").ap()
    build(nc, A, out)
    r = run_bass_kernel_spmd(nc, [{f"in_{n}": x for n, x in arrays.items()}], core_ids=[0])
    got = np.asarray(r.results[0]["out_features"])
    return got.transpose(1, 0, 2).reshape(D, B, T).transpose(1, 2, 0)
```

```python
import numpy as np
import concourse.bass as bass
from concourse import mybir
from contextlib import ExitStack

F32 = mybir.dt.float32
U32 = mybir.dt.uint32
F32R = mybir.dt.float32r
ALU = mybir.AluOpType
ACT = mybir.ActivationFunctionType
AX = mybir.AxisListType.X

P = 128
B, T, D = 2, 1024, 256
N = B * T
KD = D // P
TT = 512
NT = N // TT
HEADS, HD = 16, 16
SLOT = 32
GH = P // SLOT
GROUPS = HEADS // GH
E = 8
SCALE = HD ** -0.5


class Chip:

    def __init__(self, nc, ctx):
        self.nc, self.ctx, self.sems = nc, ctx, []
        self.bank = [ctx.enter_context(nc.psum_tensor(f"bank{n}", [P, 512], F32)) for n in range(4, 8)]
        self.pair = [ctx.enter_context(nc.psum_tensor(f"pair{n}", [P, 1024], F32)) for n in range(2)]
        self.quad = [self.pair[n // 2][:, 512 * (n % 2):512 * (n % 2) + 512] for n in range(4)]
        self.x = self.sb("x_stream", [P, KD, N])
        self.h = self.sb("h_stream", [P, KD, N])
        self.ident = self.sb("ident", [P, P])
        self.neg_ident = self.sb("neg_ident", [P, P])
        self.mean_ones = self.sb("mean_ones", [P, P])
        self.sum_pick = self.sb("sum_pick", [P, GH])
        self.cond = self.sb("cond", [P, B, E])
        self.moe_w = self.sb("moe_w", [P, B, 3])
        self.moe_i = self.sb("moe_i", [P, B, 3], U32)

    def sb(self, name, shape, dt=F32, ctx=None):
        return (ctx or self.ctx).enter_context(self.nc.sbuf_tensor(name, shape, dt))

    def sem(self, name):
        self.sems.append(self.nc.alloc_semaphore(name=name))
        return self.sems[-1]

    def end_layer(self):
        self.nc.clear_and_free_semaphores(self.sems)
        self.nc.all_engine_barrier()
        self.sems = []


def setup(c, A):
    nc = c.nc
    loaded, picked, weighed = c.sem("su_loaded"), c.sem("su_picked"), c.sem("su_weighed")
    exp_done = c.sem("su_exp_done")
    with nc.Block() as block:
        @block.sync
        def _(sp):
            sp.dma_start(c.cond[:, :, :], A["cond_all"]).then_inc(loaded, 16)
            sp.dma_start(c.x[:, :, :], A["x"]).then_inc(loaded, 16)
            sp.dma_start(c.ident[:, :], A["ident"]).then_inc(loaded, 16)
            sp.dma_start(c.neg_ident[:, :], A["neg_ident"]).then_inc(loaded, 16)
            sp.dma_start(c.mean_ones[:, :], A["mean_ones"]).then_inc(loaded, 16)
            sp.dma_start(c.sum_pick[:, :], A["sum_pick"]).then_inc(loaded, 16)
            sp.wait_ge(loaded, 6 * 16)

        with ExitStack() as ctx:
            top = c.sb("su_top", [P, B, 8], ctx=ctx)
            idx = c.sb("su_idx", [P, B, 8], U32, ctx=ctx)
            gap = c.sb("su_gap", [P, B], ctx=ctx)
            den = c.sb("su_den", [P, B], ctx=ctx)

            @block.vector
            def _(dve):
                dve.wait_ge(loaded, 6 * 16)
                for b in range(B):
                    nc.vector.max(top[:, b, :], c.cond[:, b, :]).then_inc(picked, 1)
                dve.wait_ge(picked, B)
                for b in range(B):
                    nc.vector.max_index(idx[:, b, :], top[:, b, :], c.cond[:, b, :]).then_inc(picked, 1)
                nc.vector.tensor_tensor(gap[:, :], top[:, :, 1], top[:, :, 0], ALU.subtract).then_inc(picked, 1)
                nc.vector.memset(c.moe_i[:, :, 2:3], E).then_inc(weighed, 1)
                nc.vector.memset(c.moe_w[:, :, 2:3], 1.0).then_inc(weighed, 1)
                dve.wait_ge(picked, 2 * B + 1)
                nc.vector.tensor_copy(c.moe_i[:, :, 0:2], idx[:, :, 0:2]).then_inc(weighed, 1)
                dve.wait_ge(exp_done, 1)
                nc.vector.tensor_scalar(den[:, :], c.moe_w[:, :, 1], 1.0, None, ALU.add).then_inc(picked, 1)
                dve.wait_ge(picked, 2 * B + 2)
                nc.vector.reciprocal(c.moe_w[:, :, 0], den[:, :]).then_inc(picked, 1)
                dve.wait_ge(picked, 2 * B + 3)
                nc.vector.tensor_tensor(c.moe_w[:, :, 1], c.moe_w[:, :, 1], c.moe_w[:, :, 0], ALU.mult)\
                    .then_inc(weighed, 1)

            @block.scalar
            def _(act):
                act.wait_ge(picked, 2 * B + 1)
                nc.scalar.activation(c.moe_w[:, :, 1], gap[:, :], ACT.Exp).then_inc(exp_done, 1)


def merged_input(c, A):
    nc = c.nc
    loaded, scaled, merged, ready = c.sem("mi_loaded"), c.sem("mi_scaled"), c.sem("mi_merged"), c.sem("mi_ready")
    out_mm, out_ev = c.sem("mi_out_mm"), c.sem("mi_out_ev")
    with ExitStack() as ctx:
        lora_a = c.sb("mi_lora_a", [P, D], ctx=ctx)
        lora_b = c.sb("mi_lora_b", [P, D], ctx=ctx)
        cond_er = c.sb("mi_cond_er", [P, B], ctx=ctx)
        w_base = c.sb("mi_w_base", [P, KD, D], ctx=ctx)
        bias = c.sb("mi_bias", [P, KD], ctx=ctx)
        scaled_b = c.sb("mi_scaled_b", [P, B, D], ctx=ctx)
        w_eff = c.sb("mi_w_eff", [P, B, KD, D], ctx=ctx)
        with nc.Block() as block:
            @block.sync
            def _(sp):
                for dst, src in ((lora_a[:, :], "L0_cond_As"), (lora_b[:, :], "L0_cond_Bs"), (cond_er[:, :], "cond_er"),
                                 (w_base[:, :, :], "L0_cond_W_base"), (bias[:, :], "L0_cond_b_base")):
                    sp.dma_start(dst, A[src]).then_inc(loaded, 16)

            @block.vector
            def _(dve):
                dve.wait_ge(loaded, 5 * 16)
                for b in range(B):
                    nc.vector.tensor_scalar(scaled_b[:, b, :], lora_b[:, :], cond_er[:, b:b + 1], 2.0, ALU.mult, ALU.mult)\
                        .then_inc(scaled, 1)
                for b in range(B):
                    for k in range(KD):
                        dve.wait_ge(merged, b * KD + k + 1)
                        nc.vector.tensor_tensor(w_eff[:, b, k, :], c.quad[b * KD + k][:, 0:D], w_base[:, k, :], ALU.add)\
                            .then_inc(ready, 1)

            @block.tensor
            def _(pe):
                pe.wait_ge(loaded, 5 * 16)
                for b in range(B):
                    pe.wait_ge(scaled, b + 1)
                    for k in range(KD):
                        nc.tensor.matmul(c.quad[b * KD + k][:, 0:D], lora_a[:, k * P:(k + 1) * P], scaled_b[:, b, :],
                                         start=True, stop=True).then_inc(merged, 1)
                n = 0
                for b in range(B):
                    pe.wait_ge(ready, (b + 1) * KD)
                    for t in range(T // TT):
                        for m in range(KD):
                            if n >= 4:
                                pe.wait_ge(out_ev, n - 3)
                            for k in range(KD):
                                last = nc.tensor.matmul(c.bank[n % 4][:, :], w_eff[:, b, k, m * P:(m + 1) * P],
                                                        c.x[:, k, b * T + t * TT:b * T + (t + 1) * TT],
                                                        start=k == 0, stop=k == KD - 1)
                            last.then_inc(out_mm, 1)
                            n += 1

            @block.scalar
            def _(act):
                act.wait_ge(loaded, 5 * 16)
                n = 0
                for b in range(B):
                    for t in range(T // TT):
                        for m in range(KD):
                            act.wait_ge(out_mm, n + 1)
                            nc.scalar.activation(c.h[:, m, b * T + t * TT:b * T + (t + 1) * TT], c.bank[n % 4][:, :],
                                                 ACT.Identity, bias=bias[:, m:m + 1]).then_inc(out_ev, 1)
                            n += 1


NG = B * GROUPS
QT = T // P
HALF = T // TT
LOW = (1, 3, 0, 2)
QK_TILES = [(p, m, h) for p in range(2) for h in range(HALF) for m in range(2)]
FIRST = [(a, i, c_) for pair in ((0, 1), (2, 3)) for i in range(QT) for a in pair for c_ in range(i // 4 + 1)]
NF = len(FIRST)
MAX0 = FIRST.index((3, 3, 0)) + 1
STEPS = [(h, j) for h in range(HALF) for j in range(4 * (h + 1))]
NS = len(STEPS)
FR = 3


def cut(h, j):
    return max(0, j * P - h * TT)


SHARED = ("qk", "v", "max", "sums", "spread")


def front_order(previous, own, following):
    tiles = iter(range(NF if following else 0))
    order, waiting = [], []

    def some(n):
        for _, f in zip(range(n), tiles):
            a, i, chunk = FIRST[f]
            order.append((("first", f), 1.7 + min(512, (i + 1) * P - 512 * chunk) / 100))

    def use():
        if waiting:
            what, *which = waiting.pop()
            order.append(((what + "_use", *which), {"qk": 6.3, "v": 3, "max": 6.6, "sums": 1, "spread": 6}[what]))

    def shared(*entry, then=0):
        order.append((entry, {"qk": 17, "v": 23.8, "max": 4.5, "sums": 2, "spread": 4}[entry[0]]))
        use()
        waiting.append(entry)
        some(then)

    if previous:
        shared("sums", 1, -1)
    if following:
        shared("qk", 0)
    if previous:
        shared("spread", 1, -1)
    if following:
        shared("qk", 1)
    if own:
        shared("max", 1)
    if not following:
        use()
        return order
    shared("qk", 2, then=2)
    shared("qk", 3, then=2)
    shared("qk", 4, then=3)
    shared("qk", 5, then=1)
    shared("v", 0, then=2)
    shared("qk", 6, then=1)
    shared("v", 1, then=2)
    shared("qk", 7, then=2)
    if own:
        shared("sums", 0, 0, then=3)
        shared("spread", 0, 0)
    else:
        use()
    some(MAX0 - sum(e[0] == "first" for e, _ in order))
    order.append((("split", 0), 6))
    some(2)
    shared("max", 0, then=3)
    use()
    some(NF)
    order.append((("split", 1), 8))
    return order


def turn(opening, closing):
    front = front_order(not opening, True, not closing)
    total = sum(cost for _, cost in front)
    weights = [400 + TT - cut(h, j) for h, j in STEPS]
    order, spent, done = ([] if opening else [("copy", 1, -1)]), 0, 0
    for i in range(NS):
        for a in range(GH):
            order.append(("scores", i, a))
            done += weights[i] / GH
            while front and spent + front[0][1] / 2 <= total * done / sum(weights) * (5 if closing else 1.02):
                entry, cost = front.pop(0)
                assert entry[0] != "sums" or entry[1:] != (0, 0) or ("copy", 0, 0) in order
                order.append(entry)
                spent += cost
            if (i, a) == (5, 0):
                order.append(("copy", 0, 0))
            if closing and (i, a) in ((6, 0), (7, 0)):
                order += [("sums", 0, 0), ("sums_use", 0, 0)] if i == 6 else [("spread", 0, 0), ("spread_use", 0, 0)]
        if i:
            order.append(("values", i - 1))
        if i == 3:
            assert ("max_use", 1) in order
    order += [e for e, _ in front] + [("values", NS - 1)]
    if closing:
        order += [("copy", 1, 0), ("sums", 1, 0), ("sums_use", 1, 0), ("spread", 1, 0), ("spread_use", 1, 0)]
    return order


START = [e for e, _ in front_order(False, False, True)]
OPENING, STEADY, CLOSING = turn(True, False), turn(False, False), turn(False, True)


def banks_taken(order, until=None):
    return sum(e[0] in SHARED for e in (order if until is None else order[:order.index(until)]))


def taken_before(n):
    if isinstance(n, int) and n <= 0:
        return 0 if n < 0 else banks_taken(START)
    return (n - 1) * banks_taken(STEADY) + (banks_taken(START) + banks_taken(OPENING))


def all_turns(eng, body):
    assert banks_taken(STEADY) % 2 == 0
    body(START, -1, 1)
    body(OPENING, 0, 0)
    with eng.Fori(0, (NG - 2) // 2) as r:
        for x in range(2):
            body(STEADY, r * 2 + (1 + x), (1 + x) % 2)
    body(CLOSING, NG - 1, (NG - 1) % 2)


def attention(c, A, tag, w_qkv, w_out, b_out, dest):
    nc = c.nc
    s = {n: c.sem(f"{tag}_{n}") for n in (
        "mask", "passed", "seen", "wg", "hc", "hc_free", "proj", "hi", "used", "vp", "a_mm", "a_max", "m_hi", "m_lo",
        "t_mm", "b_mm", "b_exp", "b_cut", "pv", "o_sum", "o_cp", "o_spread", "o_done", "zero", "ow", "om", "oe")}
    ZEROS = 2 + 2 * GH
    banks = [*c.quad, c.bank[0][:, :]]
    first_bank, score_bank = banks[:FR], banks[FR:]
    SR = len(score_bank)
    value_bank = c.bank[1][:, :]
    shared_bank = [c.bank[2][:, :], c.bank[3][:, :]]

    def place(order, n, entry):
        before = banks_taken(order, entry)
        return shared_bank[(taken_before(n if isinstance(n, int) else 1) + before) % 2], taken_before(n) + (before + 1)

    with ExitStack() as octx:
        o_all = c.sb(f"{tag}_o_all", [P, NG * HALF, TT], ctx=octx)
        with ExitStack() as ctx:
            w = c.sb(f"{tag}_w", [P, 5, KD, P], ctx=ctx)
            hc = c.sb(f"{tag}_hc", [P, KD, T], ctx=ctx)
            hi = c.sb(f"{tag}_hi", [P, 2, TT], F32R, ctx=ctx)
            kx = c.sb(f"{tag}_kx", [P, 2, GH // 2, T], F32R, ctx=ctx)
            qx = c.sb(f"{tag}_qx", [P, 2, GH, T], F32R, ctx=ctx)
            v_sb = c.sb(f"{tag}_v", [P, 2, QT, P], ctx=ctx)
            mx_raw = c.sb(f"{tag}_mx_raw", [P, QT, 2, GH], ctx=ctx)
            mx_hi = c.sb(f"{tag}_mx_hi", [P, QT, GH], F32R, ctx=ctx)
            mx = c.sb(f"{tag}_mx", [P, QT, GH, SLOT], ctx=ctx)
            junk = c.sb(f"{tag}_junk", [P, 2, TT], ctx=ctx)
            mask = c.sb(f"{tag}_mask", [P, T], ctx=ctx)
            rows = c.sb(f"{tag}_rows", [P, GH // 2, 5], ctx=ctx)
            RING = 3
            prob = c.sb(f"{tag}_prob", [P, RING, GH, TT], ctx=ctx)
            o_raw = c.sb(f"{tag}_o_raw", [P, HALF, TT], ctx=ctx)
            o_rcp = c.sb(f"{tag}_o_rcp", [P, TT // P, GH], ctx=ctx)

            def quadrant(a):
                return slice(a * SLOT, (a + 1) * SLOT)

            def starts(n):
                return isinstance(n, int) and n <= 0

            with nc.Block() as block:
                @block.sync
                def _(sp):
                    sp.dma_start(mask[:, :], A["causal"]).then_inc(s["mask"], 16)
                    sp.dma_start(rows[:, :, :], A["split_rows"]).then_inc(s["mask"], 16)
                    with sp.Fori(0, B) as b:
                        sp.wait_ge(s["hc_free"], b * GROUPS + 1)
                        for k in range(KD):
                            sp.dma_start(hc[:, k, :], c.h[:, k, :].rearrange("p (b t) -> p b t", b=B)[:, b, :]).then_inc(s["hc"], 16)
                        sp.wait_ge(s["hc"], b * KD * 16 + KD * 16)
                        sp.sem_inc(s["passed"], 1)
                        with sp.Fori(0, GROUPS) as g:
                            sp.wait_ge(s["hc_free"], b * GROUPS + g + 1)
                            sp.dma_start(w[:, :, :, :], A[w_qkv][g, :, :, :, :]).then_inc(s["wg"], 16)

                @block.gpsimd
                def _(pool):
                    nc.gpsimd.memset(mx[:, :, :, :], 0.0).then_inc(s["zero"], 1)
                    nc.gpsimd.memset(v_sb[:, :, :, :].rearrange("p x t (a s) -> p (x t a) s", s=SLOT)[:, :, HD:HD + 1], 1.0)\
                        .then_inc(s["passed"], 1)
                    nc.gpsimd.memset(v_sb[:, :, :, :].rearrange("p x t (a s) -> p (x t a) s", s=SLOT)[:, :, HD + 1:SLOT], 0.0)\
                        .then_inc(s["zero"], 1)
                    with pool.Fori(0, NG) as n:
                        for i, (h, j) in enumerate(STEPS):
                            if j < 4 * h:
                                continue
                            pool.wait_ge(s["b_exp"], (n * NS + i + 1) * GH)
                            pool.sem_inc(s["passed"], 1)
                            q0 = cut(h, j)
                            block_ = prob[:, i % RING, :, q0:q0 + P]
                            nc.gpsimd.affine_select(out=block_, in_=block_, compare_op=ALU.is_ge, fill=0.0, base=0,
                                                    pattern=[[0, GH], [1, P]], channel_multiplier=-1)\
                                .then_inc(s["b_cut"], 1)

                @block.tensor
                def _(pe):
                    pe.wait_ge(s["zero"], ZEROS)

                    def body(order, n, buf):
                        m, next_buf = n + 1, 1 - buf

                        def take(*entry):
                            bank, count = place(order, n, entry)
                            if not isinstance(count, int) or count > 2:
                                pe.wait_ge(s["used"], count - 2)
                            return bank

                        def qk_projection(t):
                            p, which, h = QK_TILES[t]
                            if t == 0:
                                pe.wait_ge(s["wg"], m * 16 + 16)
                            bank = take("qk", t)
                            for k in range(KD):
                                last = nc.tensor.matmul(bank, w[:, 2 * which + p, k, :], hc[:, k, h * TT:(h + 1) * TT],
                                                        start=k == 0, stop=k == KD - 1)
                            last.then_inc(s["proj"], 1)

                        def v_projection(v):
                            bank = take("v", v)
                            for t in range(4):
                                for k in range(KD):
                                    last = nc.tensor.matmul(bank[:, t * P:(t + 1) * P],
                                                            hc[:, k, (4 * v + t) * P:(4 * v + t + 1) * P], w[:, 4, k, :],
                                                            start=k == 0, stop=k == KD - 1)
                            last.then_inc(s["vp"], 1)

                        def first(t):
                            a, i, chunk = FIRST[t]
                            if t >= FR or not starts(m):
                                pe.wait_ge(s["a_max"], m * NF + (t - FR + 1))
                            pe.wait_ge(s["used"], place(order, n, ("qk", 4 * (a // 2) + (1 if i < 4 else 3)))[1])
                            c0, c1 = 512 * chunk, min(512 * (chunk + 1), (i + 1) * P)
                            nc.tensor.matmul(first_bank[t % FR][:, 0:c1 - c0], qx[:, next_buf, a, i * P:(i + 1) * P],
                                             kx[:, next_buf, a // 2, c0:c1], start=True, stop=True).then_inc(s["a_mm"], 1)

                        def maxima(h):
                            x = m if h == 0 else n
                            pe.wait_ge(s["m_lo"], x * HALF + h + 1)
                            bank = take("max", h)
                            for i in range(4):
                                last = nc.tensor.matmul(bank[:, i * P:(i + 1) * P],
                                                        mx[:, 4 * h + i, :, :].rearrange("p a r -> p (a r)"),
                                                        c.neg_ident[:, :], start=True, stop=True)
                            last.then_inc(s["t_mm"], 1)

                        def scores(i, a):
                            h, j = STEPS[i]
                            q0 = cut(h, j)
                            t = i * GH + a
                            if j == 0 and a == 0:
                                pe.wait_ge(s["used"], place(order, n, ("max", 1))[1] if h else taken_before(n))
                            if t >= SR or not starts(n):
                                pe.wait_ge(s["b_exp"], n * NS * GH + (t - SR + 1))
                            nc.tensor.matmul(score_bank[t % SR][:, q0:TT], kx[:, buf, a // 2, j * P:(j + 1) * P],
                                             qx[:, buf, a, h * TT + q0:(h + 1) * TT], start=True, stop=True)\
                                .then_inc(s["b_mm"], 1)

                        def values(i):
                            h, j = STEPS[i]
                            q0 = cut(h, j)
                            pe.wait_ge(s["b_exp"], (n * NS + i + 1) * GH)
                            if j >= 4 * h:
                                pe.wait_ge(s["b_cut"], n * QT + j + 1)
                            if j == 0 and (h or not starts(n)):
                                pe.wait_ge(s["o_cp"], n * HALF + h)
                            for a in range(GH):
                                r = quadrant(a)
                                last = nc.tensor.matmul(value_bank[r, q0:TT], v_sb[:, buf, j, r], prob[:, i % RING, a, q0:TT],
                                                        start=j == 0, stop=j == 4 * h + 3)
                            last.then_inc(s["pv"], 1)

                        def sums(h, back):
                            pe.wait_ge(s["o_cp"], (n + back) * HALF + h + 1)
                            bank = take("sums", h, back)
                            for i in range(TT // P):
                                last = nc.tensor.matmul(bank[:, i * GH:(i + 1) * GH], o_raw[:, h, i * P:(i + 1) * P],
                                                        c.sum_pick[:, :], start=True, stop=True)
                            last.then_inc(s["o_sum"], 1)

                        def spread(h, back):
                            pe.wait_ge(s["used"], place(order, n, ("sums", h, back))[1])
                            bank = take("spread", h, back)
                            for i in range(TT // P):
                                for a in range(GH):
                                    last = nc.tensor.matmul(bank[quadrant(a), i * P:(i + 1) * P],
                                                            o_rcp[:, i, a:a + 1].broadcast_to([P, SLOT]),
                                                            c.ident[:, :], start=True, stop=True)
                            last.then_inc(s["o_spread"], 1)

                        does = {"qk": qk_projection, "v": v_projection, "first": first, "max": maxima, "scores": scores,
                                "values": values, "sums": sums, "spread": spread}
                        for what, *which in order:
                            if what in does:
                                does[what](*which)
                    all_turns(pe, body)

                @block.scalar
                def _(act):
                    act.wait_ge(s["mask"], 32)
                    act.wait_ge(s["zero"], ZEROS)

                    def body(order, n, buf):
                        m, next_buf = n + 1, 1 - buf

                        def upper(t):
                            p, which, h = QK_TILES[t]
                            bank = place(order, n, ("qk", t))[0]
                            act.wait_ge(s["proj"], m * len(QK_TILES) + t + 1)
                            if which == 0:
                                nc.scalar.activation(hi[:, t % 2, :], bank, ACT.Identity, scale=rows[:, p, 0:1], bias=rows[:, p, 1:2])\
                                    .then_inc(s["hi"], 1)
                            else:
                                nc.scalar.activation(hi[:, t % 2, :], bank, ACT.Identity, scale=rows[:, p, 3:4]).then_inc(s["hi"], 1)

                        def probabilities(i, a):
                            q0 = cut(*STEPS[i])
                            if a == 0 and (i >= RING or not starts(n)):
                                act.wait_ge(s["pv"], n * NS + i - RING + 1)
                            act.wait_ge(s["b_mm"], (n * NS + i) * GH + a + 1)
                            nc.scalar.activation(prob[:, i % RING, a, q0:TT], score_bank[(i * GH + a) % SR][:, q0:TT],
                                                 ACT.Exp, scale=SCALE).then_inc(s["b_exp"], 1)

                        def copy_result(h, back):
                            x = n + back
                            act.wait_ge(s["pv"], x * NS + (4 if h == 0 else NS))
                            act.wait_ge(s["o_done"], x * HALF + h + 1)
                            nc.scalar.activation(o_raw[:, h, :], value_bank, ACT.Copy).then_inc(s["o_cp"], 1)

                        does = {"qk": upper, "scores": probabilities, "copy": copy_result}
                        for what, *which in order:
                            if what in does:
                                does[what](*which)
                    all_turns(act, body)

                @block.vector
                def _(dve):
                    dve.wait_ge(s["mask"], 32)
                    for x in range(2):
                        for a in range(GH):
                            nc.vector.memset(qx[:, x, a, :].bitcast(F32), 0.0).then_inc(s["zero"], 1)
                    dve.wait_ge(s["zero"], ZEROS)
                    dve.sem_inc(s["hc_free"], 1)
                    dve.sem_inc(s["o_done"], HALF)

                    def body(order, n, buf):
                        m, next_buf = n + 1, 1 - buf

                        def split_rows(t):
                            p, which, h = QK_TILES[t]
                            bank, count = place(order, n, ("qk", t))
                            cols = slice(h * TT, (h + 1) * TT)
                            dve.wait_ge(s["hi"], m * len(QK_TILES) + t + 1)
                            if which == 0:
                                last = nc.vector.scalar_tensor_tensor(out=kx[:, next_buf, p, cols], in0=bank, scalar=rows[:, p, 2:3],
                                                                      in1=hi[:, t % 2, :].bitcast(F32), op0=ALU.mult, op1=ALU.add)
                            else:
                                for x in range(2):
                                    r = slice(x * 64, (x + 1) * 64)
                                    last = nc.vector.scalar_tensor_tensor(out=qx[r, next_buf, 2 * p + x, cols], in0=bank[r, :],
                                                                          scalar=rows[r, p, 4:5], in1=hi[r, t % 2, :].bitcast(F32),
                                                                          op0=ALU.mult, op1=ALU.add)
                            last.then_inc(s["used"], 1)
                            if t == len(QK_TILES) - 1:
                                dve.wait_ge(s["used"], count)
                                dve.sem_inc(s["hc_free"], 1)

                        def copy_values(v):
                            dve.wait_ge(s["vp"], m * 2 + v + 1)
                            nc.vector.tensor_copy(
                                v_sb[:, next_buf, 4 * v:4 * v + 4, :].rearrange("p t (a s) -> p (t a) s", s=SLOT)[:, :, 0:HD],
                                place(order, n, ("v", v))[0].rearrange("p (x s) -> p x s", s=SLOT)[:, :, 0:HD])\
                                .then_inc(s["used"], 1)

                        def maximum(t):
                            a, i, chunk = FIRST[t]
                            cols = min(512, (i + 1) * P - 512 * chunk)
                            m0 = 0 if (i + 1) * P - 512 * chunk > 512 else T - cols
                            dve.wait_ge(s["a_mm"], m * NF + t + 1)
                            if t >= 2 or not starts(m):
                                dve.wait_ge(s["a_max"], m * NF + t - 1)
                            dve.sem_inc(s["seen"], 1)
                            nc.vector.tensor_tensor_reduce(
                                out=junk[:, t % 2, 0:cols], in0=first_bank[t % FR][:, 0:cols], in1=mask[:, m0:m0 + cols],
                                scale=1.0, scalar=-3.0e38, op0=ALU.add, op1=ALU.max,
                                accum_out=mx_raw[:, i, chunk, LOW[a]:LOW[a] + 1]).then_inc(s["a_max"], 1)

                        def split_maxima(h):
                            part = slice(4 * h, 4 * h + 4)
                            small = m * 5 + 2 * h
                            dve.wait_ge(s["a_max"], m * NF + (FIRST.index((3, 3, 0)) + 1 if h == 0 else NF))
                            if h:
                                nc.vector.tensor_tensor(mx_raw[:, part, 0, :], mx_raw[:, part, 0, :], mx_raw[:, part, 1, :], ALU.max)\
                                    .then_inc(s["m_hi"], 1)
                                small = small + 1
                                dve.wait_ge(s["m_hi"], small)
                            nc.vector.tensor_copy(mx_hi[:, part, :], mx_raw[:, part, 0, :]).then_inc(s["m_hi"], 1)
                            dve.wait_ge(s["m_hi"], small + 1)
                            nc.vector.tensor_copy(mx[:, part, :, HD], mx_hi[:, part, :].bitcast(F32)).then_inc(s["m_hi"], 1)
                            dve.wait_ge(s["m_hi"], small + 2)
                            nc.vector.tensor_tensor(mx[:, part, :, HD + 1], mx_raw[:, part, 0, :], mx_hi[:, part, :].bitcast(F32),
                                                    ALU.subtract).then_inc(s["m_lo"], 1)

                        def add_max(h):
                            x, x_buf = (m, next_buf) if h == 0 else (n, buf)
                            bank = place(order, n, ("max", h))[0]
                            dve.wait_ge(s["t_mm"], x * HALF + h + 1)
                            for a in range(GH):
                                r = quadrant(LOW[a])
                                tile = qx[r, x_buf, a, h * TT:(h + 1) * TT]
                                last = nc.vector.tensor_tensor(tile, bank[r, :], tile.bitcast(F32), ALU.add)
                            last.then_inc(s["used"], 1)

                        def reciprocals(h, back):
                            bank = place(order, n, ("sums", h, back))[0]
                            dve.wait_ge(s["o_sum"], (n + back) * HALF + h + 1)
                            nc.vector.reciprocal(o_rcp[:, :, :].rearrange("p i a -> p (i a)"), bank[:, 0:TT // P * GH])\
                                .then_inc(s["used"], 1)

                        def divide(h, back):
                            x = n + back
                            bank = place(order, n, ("spread", h, back))[0]
                            out = o_all[:, x * HALF + h, :] if isinstance(x, int) else \
                                o_all[:, bass.ds(x * HALF + h, 1), :].rearrange("p x t -> p (x t)")
                            dve.wait_ge(s["o_spread"], x * HALF + h + 1)
                            nc.vector.tensor_tensor(out, bank, o_raw[:, h, :], ALU.mult).then_inc(s["used"], 1)
                            dve.wait_ge(s["used"], place(order, n, ("spread", h, back))[1])
                            dve.sem_inc(s["o_done"], 1)

                        does = {"qk_use": split_rows, "v_use": copy_values, "first": maximum, "split": split_maxima, "max_use": add_max,
                                "sums_use": reciprocals, "spread_use": divide}
                        for what, *which in order:
                            if what in does:
                                does[what](*which)
                    all_turns(dve, body)

        with ExitStack() as ctx:
            wo = c.sb(f"{tag}_wo", [P, GROUPS, D], ctx=ctx)
            bo = c.sb(f"{tag}_bo", [P, KD], ctx=ctx)
            with nc.Block() as block:
                @block.sync
                def _(sp):
                    sp.dma_start(wo[:, :, :], A[w_out]).then_inc(s["ow"], 16)
                    sp.dma_start(bo[:, :], A[b_out]).then_inc(s["ow"], 16)

                @block.tensor
                def _(pe):
                    pe.wait_ge(s["ow"], 32)
                    for t in range(NT):
                        for m in range(KD):
                            if t >= 2:
                                pe.wait_ge(s["oe"], (t - 2) * KD + m + 1)
                            for g in range(GROUPS):
                                last = nc.tensor.matmul(c.bank[t % 2 * KD + m][:, :], wo[:, g, m * P:(m + 1) * P],
                                                        o_all[:, (t // HALF * GROUPS + g) * HALF + t % HALF, :],
                                                        start=g == 0, stop=g == GROUPS - 1)
                            last.then_inc(s["om"], 1)

                @block.vector
                def _(dve):
                    dve.wait_ge(s["ow"], 32)
                    for t in range(NT):
                        for m in range(KD):
                            dve.wait_ge(s["om"], t * KD + m + 1)
                            tile = dest[:, m, t * TT:(t + 1) * TT]
                            nc.vector.scalar_tensor_tensor(out=tile, in0=c.bank[t % 2 * KD + m][:, :], scalar=bo[:, m:m + 1], in1=tile,
                                                           op0=ALU.add, op1=ALU.add).then_inc(s["oe"], 1)


def split(c, tag, src, hi, lo):
    nc = c.nc
    rounded, rest = c.sem(f"{tag}_sp_rounded"), c.sem(f"{tag}_sp_rest")
    with nc.Block() as block:
        @block.scalar
        def _(act):
            for k in range(KD):
                nc.scalar.activation(hi[:, k, :], src[:, k, :], ACT.Copy).then_inc(rounded, 1)

        @block.vector
        def _(dve):
            for k in range(KD):
                dve.wait_ge(rounded, k + 1)
                nc.vector.tensor_tensor(lo[:, k, :], src[:, k, :], hi[:, k, :].bitcast(F32), ALU.subtract).then_inc(rest, 1)


def product(nc, out, w_hi, w_lo, x_hi, x_lo, first, last):
    nc.tensor.matmul(out, w_lo, x_hi, start=first, stop=False)
    nc.tensor.matmul(out, w_hi, x_hi, start=False, stop=False)
    return nc.tensor.matmul(out, w_hi, x_lo, start=False, stop=last)


def gated_mlp(c, tag, hb, rounds, tiles, source, func, x_hi, x_lo, y, load_extra=None, bias=None, finish=None):
    nc = c.nc
    part = KD * hb * P
    steps = [(s, i, m) for s in range(2) for i in range(len(tiles[s])) for m in range(hb)]
    SB, TB = len(steps), len(tiles[0]) + len(tiles[1])
    LAG, RING = 3, 4
    q = {n: c.sem(f"{tag}_{n}") for n in (
        "passed", "raw0", "raw1", "raw_free", "w_hi", "w_ready", "unit_done", "up", "act", "prod", "hi", "lo",
        "down", "y_done", "y_part", "extra", "extra0", "extra1", "extra_free")}
    raw_ready = [q["raw0"], q["raw1"]]
    if bias:
        bias["sem"].append(q["extra"])
    with ExitStack() as ctx:
        raw = c.sb(f"{tag}_raw", [P, 2, part], ctx=ctx)
        w_hi = c.sb(f"{tag}_w_hi", [P, 2, 3, part], F32R, ctx=ctx)
        w_lo = c.sb(f"{tag}_w_lo", [P, 2, 3, part], F32R, ctx=ctx)
        g_sb = c.sb(f"{tag}_g", [P, 2, TT], ctx=ctx)
        h_sb = c.sb(f"{tag}_h", [P, 2, TT], ctx=ctx)
        h_hi = c.sb(f"{tag}_h_hi", [P, RING, TT], F32R, ctx=ctx)
        h_lo = c.sb(f"{tag}_h_lo", [P, RING, TT], F32R, ctx=ctx)

        def rolled(eng, body):
            if rounds == 1:
                body(0)
            else:
                with eng.Fori(0, rounds) as r:
                    body(r)

        with nc.Block() as block:
            @block.sync
            def _(sp):
                def body(r):
                    for s in range(2):
                        unit = source(sp, r, s)
                        if load_extra:
                            load_extra(sp, r, s, unit, q)
                        for p in range(3):
                            n = 3 * s + p
                            sp.wait_ge(q["raw_free"], r * 6 + n + 1)
                            sp.dma_start(raw[:, n % 2, :], unit(p)).then_inc(raw_ready[n % 2], 16)
                rolled(sp, body)

            @block.gpsimd
            def _(pool):
                pool.sem_inc(q["raw_free"], 2)

                def body(r):
                    for s in range(2):
                        for p in range(3):
                            n = 3 * s + p
                            pool.wait_ge(raw_ready[n % 2], (r * 3 + n // 2 + 1) * 16)
                            if p == 0:
                                pool.wait_ge(q["unit_done"], r * 2 + s + 1)
                            pool.sem_inc(q["passed"], 1)
                            nc.gpsimd.tensor_copy(w_hi[:, s, p, :], raw[:, n % 2, :]).then_inc(q["w_hi"], 1)
                            pool.wait_ge(q["w_hi"], r * 6 + n + 1)
                            nc.gpsimd.tensor_tensor(w_lo[:, s, p, :], raw[:, n % 2, :], w_hi[:, s, p, :].bitcast(F32),
                                                    ALU.subtract).then_inc(q["w_ready"], 1)
                            pool.wait_ge(q["w_ready"], r * 6 + n + 1)
                            pool.sem_inc(q["raw_free"], 1)
                rolled(pool, body)

            @block.tensor
            def _(pe):
                pe.sem_inc(q["unit_done"], 2)

                def body(r):
                    def w(arr, s, p, k, m):
                        wide = hb if p < 2 else KD
                        return arr[:, s, p, (k * wide + m) * P:(k * wide + m + 1) * P]

                    def up(n):
                        s, i, m = steps[n]
                        t0 = tiles[s][i]
                        if n >= 2:
                            pe.wait_ge(q["prod"], r * SB + n + 1)
                        for p in range(2):
                            if i == 0 and m == 0:
                                pe.wait_ge(q["w_ready"], r * 6 + 3 * s + p + 1)
                            for k in range(KD):
                                last = product(nc, c.quad[2 * (n % 2) + p], w(w_hi, s, p, k, m), w(w_lo, s, p, k, m),
                                               x_hi[:, k, t0:t0 + TT], x_lo[:, k, t0:t0 + TT], k == 0, k == KD - 1)
                            last.then_inc(q["up"], 1)

                    def down(n):
                        s, i, m = steps[n]
                        tile = n // hb
                        if i == 0 and m == 0:
                            pe.wait_ge(q["w_ready"], r * 6 + 3 * s + 3)
                        if m == 0:
                            pe.wait_ge(q["y_done"], r * TB + tile + 1)
                        pe.wait_ge(q["lo"], r * SB + n + 1)
                        for o in range(KD):
                            last = product(nc, c.bank[2 * (tile % 2) + o][:, :], w(w_hi, s, 2, m, o), w(w_lo, s, 2, m, o),
                                           h_hi[:, n % RING, :], h_lo[:, n % RING, :], m == 0, m == hb - 1)
                        last.then_inc(q["down"], 1)
                        if i == len(tiles[s]) - 1 and m == hb - 1:
                            pe.wait_ge(q["down"], RING + r * SB + n + 1)
                            pe.sem_inc(q["unit_done"], 1)

                    for n in range(SB):
                        up(n)
                        if n >= LAG:
                            down(n - LAG)
                    for n in range(SB - LAG, SB):
                        down(n)
                rolled(pe, body)

            @block.scalar
            def _(act):
                act.sem_inc(q["down"], RING)

                def body(r):
                    def rounded(n):
                        act.wait_ge(q["down"], r * SB + n + 1)
                        act.wait_ge(q["prod"], 2 + r * SB + n + 1)
                        nc.scalar.activation(h_hi[:, n % RING, :], h_sb[:, n % 2, :], ACT.Copy).then_inc(q["hi"], 1)

                    for n in range(SB):
                        s, i, m = steps[n]
                        act.wait_ge(q["prod"], r * SB + n + 1)
                        act.wait_ge(q["up"], 2 * (r * SB + n) + 1)
                        if bias:
                            if i == 0 and m == 0:
                                act.wait_ge(q["extra"], 16 * bias["loads"])
                            nc.scalar.activation(g_sb[:, n % 2, :], c.quad[2 * (n % 2)], func,
                                                 bias=bias["first"](s, m)).then_inc(q["act"], 1)
                        else:
                            nc.scalar.activation(g_sb[:, n % 2, :], c.quad[2 * (n % 2)], func).then_inc(q["act"], 1)
                        if n:
                            rounded(n - 1)
                    rounded(SB - 1)
                rolled(act, body)

            @block.vector
            def _(dve):
                dve.sem_inc(q["prod"], 2)
                dve.sem_inc(q["y_done"], 2)
                if load_extra:
                    dve.sem_inc(q["extra_free"], 2)
                    dve.sem_inc(q["y_part"], 1)
                if bias:
                    dve.wait_ge(q["extra"], 16 * bias["loads"])

                def body(r):
                    def rest(n):
                        dve.wait_ge(q["hi"], r * SB + n + 1)
                        nc.vector.tensor_tensor(h_lo[:, n % RING, :], h_sb[:, n % 2, :], h_hi[:, n % RING, :].bitcast(F32),
                                                ALU.subtract).then_inc(q["lo"], 1)

                    def add(tile):
                        s = tile // len(tiles[0])
                        t0 = tiles[s][tile % len(tiles[0])]
                        dve.wait_ge(q["down"], RING + r * SB + (tile + 1) * hb)
                        for o in range(KD):
                            last = finish(dve, r, s, o, t0, c.bank[2 * (tile % 2) + o][:, :], q)
                        if last is dve:
                            dve.sem_inc(q["y_done"], 1)
                        else:
                            last.then_inc(q["y_done"], 1)
                        if load_extra and (tile + 1) % len(tiles[0]) == 0:
                            dve.wait_ge(q["y_done"], 2 + r * TB + tile + 1)
                            dve.sem_inc(q["extra_free"], 1)

                    for n in range(SB):
                        s, i, m = steps[n]
                        dve.wait_ge(q["act"], r * SB + n + 1)
                        dve.wait_ge(q["up"], 2 * (r * SB + n) + 2)
                        if n >= 2:
                            dve.wait_ge(q["lo"], r * SB + n - 1)
                        if bias:
                            nc.vector.scalar_tensor_tensor(out=h_sb[:, n % 2, :], in0=c.quad[2 * (n % 2) + 1],
                                                           scalar=bias["second"](s, m), in1=g_sb[:, n % 2, :],
                                                           op0=ALU.add, op1=ALU.mult).then_inc(q["prod"], 1)
                        else:
                            nc.vector.tensor_tensor(h_sb[:, n % 2, :], c.quad[2 * (n % 2) + 1], g_sb[:, n % 2, :],
                                                    ALU.mult).then_inc(q["prod"], 1)
                        if n:
                            rest(n - 1)
                        if n >= hb + LAG and (n - LAG) % hb == 0:
                            add((n - LAG) // hb - 1)
                    rest(SB - 1)
                    add(TB - 1)
                rolled(dve, body)


def two_of_eight(c, A):
    nc = c.nc
    zeroed = c.sem("m2_zeroed")
    with ExitStack() as ctx:
        x_hi = c.sb("m2_x_hi", [P, KD, N], F32R, ctx=ctx)
        x_lo = c.sb("m2_x_lo", [P, KD, N], F32R, ctx=ctx)
        split(c, "m2", c.x, x_hi, x_lo)
        with nc.Block() as block:
            @block.vector
            def _(dve):
                for k in range(KD):
                    nc.vector.memset(c.h[:, k, :], 0.0).then_inc(zeroed, 1)

        def source(sp, r, s):
            e = sp.value_load(c.moe_i[0:1, s, :][:, bass.ds(r, 1)], min_val=0, max_val=E)
            return lambda p: A["L0_cond2_experts"][e, p, :, :]

        def finish(dve, r, s, o, t0, psum, q):
            y = c.h[:, o, t0:t0 + TT]
            return nc.vector.scalar_tensor_tensor(out=y, in0=psum, scalar=c.moe_w[:, s, :][:, bass.ds(r, 1)], in1=y,
                                                  op0=ALU.mult, op1=ALU.add)

        tiles = [[b * T + t * TT for t in range(T // TT)] for b in range(B)]
        gated_mlp(c, "m2", 8, 3, tiles, source, ACT.Gelu_apprx_tanh, x_hi, x_lo, c.h, finish=finish)


def spectral(c, A):
    nc = c.nc
    loaded, u_mm, u_ev, m_mm, m_ev = (c.sem(f"sp_{n}") for n in ("loaded", "u_mm", "u_ev", "m_mm", "m_ev"))
    mm, added = c.sem("sp_mm"), c.sem("sp_added")
    with ExitStack() as ctx:
        dft = c.sb("sp_dft", [P, 3, KD, D], ctx=ctx)
        wr = c.sb("sp_wr", [P, KD, D], ctx=ctx)
        wi = c.sb("sp_wi", [P, KD, D], ctx=ctx)
        bias = c.sb("sp_bias", [P, KD], ctx=ctx)
        u = c.sb("sp_u", [P, 2, KD, D], ctx=ctx)
        mat = c.sb("sp_mat", [P, KD, D], ctx=ctx)
        with nc.Block() as block:
            @block.sync
            def _(sp):
                for dst, src in ((dft[:, :, :, :], "dft"), (wr[:, :, :], "L0_ffn_wr"), (wi[:, :, :], "L0_ffn_wi"),
                                 (bias[:, :], "L0_ffn_bias")):
                    sp.dma_start(dst, A[src]).then_inc(loaded, 16)

            @block.tensor
            def _(pe):
                pe.wait_ge(loaded, 4 * 16)
                for part, terms in enumerate((((wr, 0), (wi, 1)), ((wi, 0), (wr, 2)))):
                    for f in range(KD):
                        n = 0
                        for w, d in terms:
                            for k in range(KD):
                                last = nc.tensor.matmul(c.quad[part * KD + f][:, 0:D], w[:, k, f * P:(f + 1) * P],
                                                        dft[:, d, k, :], start=n == 0, stop=n == 2 * KD - 1)
                                n += 1
                        last.then_inc(u_mm, 1)
                pe.wait_ge(u_ev, 2 * KD)
                for i in range(KD):
                    n = 0
                    for part, d in ((0, 0), (1, 2)):
                        for f in range(KD):
                            last = nc.tensor.matmul(c.bank[i][:, 0:D], u[:, part, f, i * P:(i + 1) * P], dft[:, d, f, :],
                                                    start=n == 0, stop=n == 2 * KD - 1)
                            n += 1
                    last.then_inc(m_mm, 1)
                pe.wait_ge(m_ev, KD)
                for t in range(NT):
                    for o in range(KD):
                        n = t * KD + o
                        if n >= 4:
                            pe.wait_ge(added, n - 3)
                        for k in range(KD):
                            last = nc.tensor.matmul(c.quad[n % 4], mat[:, k, o * P:(o + 1) * P],
                                                    c.h[:, k, t * TT:(t + 1) * TT], start=k == 0, stop=k == KD - 1)
                        last.then_inc(mm, 1)

            @block.scalar
            def _(act):
                for n in range(2 * KD):
                    act.wait_ge(u_mm, n + 1)
                    nc.scalar.activation(u[:, n // KD, n % KD, :], c.quad[n][:, 0:D], ACT.Copy).then_inc(u_ev, 1)
                for i in range(KD):
                    act.wait_ge(m_mm, i + 1)
                    nc.scalar.activation(mat[:, i, :], c.bank[i][:, 0:D], ACT.Copy, scale=1.0 / D).then_inc(m_ev, 1)

            @block.vector
            def _(dve):
                dve.wait_ge(loaded, 4 * 16)
                for t in range(NT):
                    for o in range(KD):
                        n = t * KD + o
                        dve.wait_ge(mm, n + 1)
                        x = c.x[:, o, t * TT:(t + 1) * TT]
                        nc.vector.scalar_tensor_tensor(out=x, in0=c.quad[n % 4], scalar=bias[:, o:o + 1], in1=x,
                                                       op0=ALU.add, op1=ALU.add).then_inc(added, 1)


def chosen_expert(c, A):
    nc = c.nc
    HB = 4
    with ExitStack() as ctx:
        x_hi = c.sb("m1_x_hi", [P, KD, N], F32R, ctx=ctx)
        x_lo = c.sb("m1_x_lo", [P, KD, N], F32R, ctx=ctx)
        biases = c.sb("m1_biases", [P, B, 2 * HB + KD], ctx=ctx)
        split(c, "m1", c.x, x_hi, x_lo)

        def source(sp, r, s):
            e = sp.value_load(c.moe_i[0:1, s, 0:1], min_val=0, max_val=E - 1)
            sp.dma_start(biases[:, s, :], A["L1_cond_biases"][e, :, :]).then_inc(extra[0], 16)
            return lambda p: A["L1_cond_experts"][e, p, :, :]

        extra = []

        def finish(dve, r, s, o, t0, psum, q):
            return nc.vector.tensor_scalar(c.h[:, o, t0:t0 + TT], psum, biases[:, s, 2 * HB + o:2 * HB + o + 1], None, ALU.add)

        bias = {"loads": B, "first": lambda s, m: biases[:, s, m:m + 1],
                "second": lambda s, m: biases[:, s, HB + m:HB + m + 1], "sem": extra}
        tiles = [[b * T + t * TT for t in range(T // TT)] for b in range(B)]
        gated_mlp(c, "m1", HB, 1, tiles, source, ACT.Silu, x_hi, x_lo, c.h, bias=bias, finish=finish)


H = 32
DI = 512
KI = DI // P
QW_ = T // 4
H_ALPHA, H_OMEGA1, H_OMEGA2, H_SELB0, H_SELB1, H_SELC0, H_SELC1, H_SELDT, H_BETA, H_RG, H_UG = range(11)
V_A11, V_A12, V_BETA, V_VF, V_SB0, V_SB1, V_SC0, V_SC1 = range(8)
L_STEP = 32
CHUNKS = T // L_STEP
NB = KI * CHUNKS
DVE_SHARE = (0.41, 0.82)


def recurrent(c, A):
    nc = c.nc
    names = ("rcp passed wload2 sq ms rt xn mm ev acc u hmm h1 h2 wload cb cd cp qload qmm d1 d2 d3 x1 xp p3 "
             "g1 g2 g3 g4 g5 oload omm oadd e1 win const").split()
    s = {n: c.sem(f"r_{n}") for n in names}
    with ExitStack() as ctx:
        z = c.sb("r_z", [P, KI, T], ctx=ctx)
        u = c.sb("r_u", [P, KI, T], ctx=ctx)
        coef = c.sb("r_coef", [P, 6, KI * T], ctx=ctx)
        weights = c.sb("r_weights", [P, 4096], ctx=ctx)
        scr = c.sb("r_scratch", [P, 4096], ctx=ctx)
        spread = c.sb("r_spread", [P, 4, KI, P], ctx=ctx)
        in_bias = c.sb("r_in_bias", [P, 16], ctx=ctx)
        vecs = c.sb("r_vecs", [P, KI, 9], ctx=ctx)
        hvecs = c.sb("r_hvecs", [P, 8], ctx=ctx)
        rms_w = c.sb("r_rms_w", [P, KD], ctx=ctx)
        group = c.sb("r_group", [P, P], ctx=ctx)
        dtc = c.sb("r_dtc", [P, 4], ctx=ctx)
        stat = c.sb("r_stat", [P, KI, 8], ctx=ctx)
        eps = c.sb("r_eps", [P, 2], ctx=ctx)
        flat = coef[:, :, :].rearrange("p a n -> p (a n)")
        pos = A["r_pos"]
        HALF = T // TT

        def tok(arr, b):
            return arr[:, :, :].rearrange("p k (b t) -> p k b t", b=B)[:, :, b, :]

        with nc.Block() as block:
            @block.sync
            def _(sp):
                for dst, src in ((spread[:, :, :, :], "r_spread"), (in_bias[:, :], "r_in_bias"), (vecs[:, :, :], "r_vecs"),
                                 (hvecs[:, :], "r_hvecs"), (rms_w[:, :], "r_rms_w"), (group[:, :], "r_group"),
                                 (eps[:, :], "r_eps")):
                    sp.dma_start(dst, A[src]).then_inc(s["const"], 16)

            @block.scalar
            def _(act):
                act.wait_ge(s["const"], 7 * 16)
                nc.scalar.activation(dtc[:, 1:2], hvecs[:, 3:4], ACT.Abs).then_inc(s["e1"], 1)
                act.wait_ge(s["e1"], 1)
                nc.scalar.activation(dtc[:, 2:3], dtc[:, 1:2], ACT.Exp, scale=-1.0).then_inc(s["e1"], 1)
                act.wait_ge(s["e1"], 2)
                nc.scalar.activation(dtc[:, 3:4], dtc[:, 2:3], ACT.Ln, bias=1.0).then_inc(s["e1"], 1)

            @block.vector
            def _(dve):
                dve.wait_ge(s["e1"], 3)
                nc.vector.scalar_tensor_tensor(out=dtc[:, 0:1], in0=hvecs[:, 3:4], scalar=0.0, in1=dtc[:, 3:4],
                                               op0=ALU.max, op1=ALU.add).then_inc(s["win"], 1)

        with nc.Fori(0, B) as b:
            xn = scr[:, 0:2 * T].rearrange("p (k t) -> p k t", k=KD)
            with nc.Block() as block:
                @block.sync
                def _(sp):
                    sp.dma_start(weights[:, :], A["r_in_proj"]).then_inc(s["wload"], 16)

                @block.scalar
                def _(act):
                    for k in range(KD):
                        nc.scalar.activation(xn[:, k, :], tok(c.h, b)[:, k, :], ACT.Square).then_inc(s["sq"], 1)
                    for h in range(HALF):
                        act.wait_ge(s["ms"], b * HALF + h + 1)
                        nc.scalar.activation(scr[:, 2 * T + h * TT:2 * T + (h + 1) * TT], c.quad[h], ACT.Sqrt,
                                             bias=eps[:, 0:1]).then_inc(s["rt"], 1)

                @block.tensor
                def _(pe):
                    pe.wait_ge(s["sq"], (b + 1) * KD)
                    for h in range(HALF):
                        for k in range(KD):
                            last = nc.tensor.matmul(c.quad[h], c.mean_ones[:, :], xn[:, k, h * TT:(h + 1) * TT],
                                                    start=k == 0, stop=k == KD - 1)
                        last.then_inc(s["ms"], 1)

                @block.vector
                def _(dve):
                    for h in range(HALF):
                        dve.wait_ge(s["rt"], b * HALF + h + 1)
                        nc.vector.reciprocal(scr[:, 3 * T + h * TT:3 * T + (h + 1) * TT],
                                             scr[:, 2 * T + h * TT:2 * T + (h + 1) * TT]).then_inc(s["rcp"], 1)
                    dve.wait_ge(s["rcp"], b * 2 + 2)
                    for k in range(KD):
                        nc.vector.scalar_tensor_tensor(out=xn[:, k, :], in0=tok(c.h, b)[:, k, :], scalar=rms_w[:, k:k + 1],
                                                       in1=scr[:, 3 * T:4 * T], op0=ALU.mult, op1=ALU.mult)\
                            .then_inc(s["xn"], 1)

            PADT = T + 3
            vpad = flat[:, 0:KI * PADT].rearrange("p (m t) -> p m t", m=KI)
            conv = coef[:, 2, :].rearrange("p (m t) -> p m t", m=KI)
            w_in = weights[:, :].rearrange("p (k m) -> p k m", k=KD)
            order = list(range(16))
            with nc.Block() as block:
                @block.tensor
                def _(pe):
                    pe.wait_ge(s["wload"], b * 16 + 16)
                    pe.wait_ge(s["xn"], b * KD + KD)
                    for n, m in enumerate(order):
                        for h in range(HALF):
                            t = n * HALF + h
                            if t >= 4:
                                pe.wait_ge(s["ev"], b * 32 + t - 3)
                            for k in range(KD):
                                last = nc.tensor.matmul(c.quad[t % 4], w_in[:, k, m * P:(m + 1) * P],
                                                        xn[:, k, h * TT:(h + 1) * TT], start=k == 0, stop=k == KD - 1)
                            last.then_inc(s["mm"], 1)

                @block.scalar
                def _(act):
                    for n, m in enumerate(order):
                        for h in range(HALF):
                            t = n * HALF + h
                            act.wait_ge(s["mm"], b * 32 + t + 1)
                            cols = slice(h * TT, (h + 1) * TT)
                            if m < 4:
                                dst, f = vpad[:, m, 3 + h * TT:3 + (h + 1) * TT], ACT.Identity
                            elif m < 12:
                                dst, f = coef[:, 4 + (m - 4) // 4, :].rearrange("p (m t) -> p m t", m=KI)[:, (m - 4) % 4, cols], ACT.Identity
                            else:
                                dst, f = z[:, m - 12, cols], ACT.Silu
                            nc.scalar.activation(dst, c.quad[t % 4], f, bias=in_bias[:, m:m + 1]).then_inc(s["ev"], 1)
                    for m in range(KI):
                        act.wait_ge(s["acc"], b * 4 * KI + (m + 1) * 4)
                        nc.scalar.activation(u[:, m, :], conv[:, m, :], ACT.Silu, bias=vecs[:, m, 4:5]).then_inc(s["u"], 1)

                @block.vector
                def _(dve):
                    nc.vector.memset(vpad[:, :, 0:3], 0.0).then_inc(s["e1"], 1)
                    dve.wait_ge(s["e1"], b + 4)
                    for m in range(KI):
                        dve.wait_ge(s["ev"], b * 32 + 2 * m + 2)
                        for j in range(4):
                            n = b * 4 * KI + 4 * m + j
                            src = vpad[:, m, j:j + T]
                            if j == 0:
                                op = nc.vector.tensor_scalar(conv[:, m, :], src, vecs[:, m, 0:1], None, ALU.mult)
                            else:
                                dve.wait_ge(s["acc"], n)
                                op = nc.vector.scalar_tensor_tensor(out=conv[:, m, :], in0=src, scalar=vecs[:, m, j:j + 1],
                                                                    in1=conv[:, m, :], op0=ALU.mult, op1=ALU.add)
                            op.then_inc(s["acc"], 1)

            w_h = weights[:, 0:KI * 11 * H].rearrange("p (k q h) -> p k q h", k=KI, q=11)
            hq = weights[:, 2048:4096].rearrange("p (v t) -> p v t", v=8)
            tmp = scr[:, :].rearrange("p (v t) -> p v t", t=QW_)
            places = [H_ALPHA, H_OMEGA1, H_SELDT, H_SELB0, H_SELB1, H_SELC0, H_SELC1, H_BETA, H_RG, H_UG]

            def head_psum(q):
                i = places.index(q)
                bank = [c.quad[0], c.quad[1], c.quad[2], c.quad[3], c.bank[0][:, :]][i // 2]
                return bank[:, (i % 2) * QW_:(i % 2 + 1) * QW_]

            with nc.Block() as block:
                @block.sync
                def _(sp):
                    sp.dma_start(weights[:, 0:KI * 11 * H], A["r_head_w"]).then_inc(s["wload2"], 16)
                    sp.dma_start(tmp[:, 15, :], pos).then_inc(s["wload2"], 16)

                @block.tensor
                def _(pe):
                    pe.wait_ge(s["wload2"], b * 32 + 32)
                    for q in places:
                        rows = [q, H_OMEGA2] if q == H_OMEGA1 else [q]
                        out = head_psum(q)
                        terms = [(r, k) for r in rows for k in range(KI)]
                        for n, (r, k) in enumerate(terms):
                            for t in range(4):
                                last = nc.tensor.matmul(out[t * H:(t + 1) * H, :], w_h[:, k, r, :],
                                                        u[:, k, t * QW_:(t + 1) * QW_], start=n == 0, stop=n == len(terms) - 1)
                        last.then_inc(s["hmm"], 1)

                (T_AL, T_OM, T_E1, T_E2, T_L1, T_L2, T_R, T_UG, T_A, T_W, T_DET, T_LAM, T_X, T_Y, T_Z) = range(15)

                @block.scalar
                def _(act):
                    count = [0]

                    def step(out, in_, f, **kw):
                        nc.scalar.activation(out, in_, f, **kw).then_inc(s["h1"], 1)
                        count[0] += 1
                        return count[0]

                    def own():
                        act.wait_ge(s["h1"], b * 22 + count[0])

                    act.wait_ge(s["hmm"], b * 10 + 10)
                    step(tmp[:, T_AL, :], head_psum(H_ALPHA), ACT.Identity, bias=hvecs[:, 0:1])
                    step(hq[:, V_SB0, :], head_psum(H_SELB0), ACT.Copy)
                    step(hq[:, V_SB1, :], head_psum(H_SELB1), ACT.Copy)
                    step(hq[:, V_SC0, :], head_psum(H_SELC0), ACT.Copy)
                    step(hq[:, V_SC1, :], head_psum(H_SELC1), ACT.Copy)
                    step(hq[:, V_BETA, :], head_psum(H_BETA), ACT.Sigmoid, bias=hvecs[:, 4:5])
                    step(tmp[:, T_R, :], head_psum(H_RG), ACT.Sigmoid, bias=hvecs[:, 5:6])
                    step(tmp[:, T_UG, :], head_psum(H_UG), ACT.Sigmoid, bias=hvecs[:, 6:7])
                    own()
                    step(tmp[:, T_E1, :], tmp[:, T_AL, :], ACT.Abs)
                    step(tmp[:, T_E2, :], head_psum(H_SELDT), ACT.Abs)
                    own()
                    step(tmp[:, T_X, :], tmp[:, T_E1, :], ACT.Exp, scale=-1.0)
                    step(tmp[:, T_Y, :], tmp[:, T_E2, :], ACT.Exp, scale=-1.0)
                    own()
                    step(tmp[:, T_L1, :], tmp[:, T_X, :], ACT.Ln, bias=1.0)
                    step(tmp[:, T_L2, :], tmp[:, T_Y, :], ACT.Ln, bias=1.0)
                    act.wait_ge(s["h2"], b * 23 + 2)
                    step(tmp[:, T_Z, :], tmp[:, T_OM, :], ACT.Abs)
                    act.wait_ge(s["h2"], b * 23 + 9)
                    step(tmp[:, T_X, :], tmp[:, T_A, :], ACT.Square, bias=1.0)
                    step(tmp[:, T_Y, :], tmp[:, T_A, :], ACT.Square, bias=1.0, scale=-1.0)
                    step(tmp[:, T_Z, :], tmp[:, T_W, :], ACT.Square)
                    step(tmp[:, T_E1, :], tmp[:, T_A, :], ACT.Square)
                    act.wait_ge(s["h2"], b * 23 + 18)
                    step(tmp[:, T_L1, :], tmp[:, T_E2, :], ACT.Ln)
                    act.wait_ge(s["h2"], b * 23 + 19)
                    step(tmp[:, T_L2, :], tmp[:, T_L1, :], ACT.Exp)
                    act.wait_ge(s["h2"], b * 23 + 22)
                    step(tmp[:, T_L1, :], tmp[:, T_L2, :], ACT.Sqrt)
                    assert count[0] == 22

                @block.vector
                def _(dve):
                    count = [0]

                    def did(op):
                        op.then_inc(s["h2"], 1)
                        count[0] += 1

                    def own():
                        dve.wait_ge(s["h2"], b * 23 + count[0])

                    def acts(n):
                        dve.wait_ge(s["h1"], b * 22 + n)

                    tt, ts, stt = nc.vector.tensor_tensor, nc.vector.tensor_scalar, nc.vector.scalar_tensor_tensor
                    t_ = lambda i: tmp[:, i, :]
                    dve.wait_ge(s["hmm"], b * 10 + 10)
                    dve.wait_ge(s["wload2"], b * 32 + 32)
                    acts(10)
                    did(stt(out=t_(T_OM), in0=head_psum(H_OMEGA1), scalar=hvecs[:, 1:2], in1=t_(15), op0=ALU.add, op1=ALU.add))
                    own()
                    did(ts(t_(T_OM), t_(T_OM), hvecs[:, 2:3], None, ALU.add))
                    acts(15)
                    did(stt(out=t_(T_AL), in0=t_(T_AL), scalar=0.0, in1=t_(T_L1), op0=ALU.max, op1=ALU.add))
                    did(stt(out=t_(T_L2), in0=head_psum(H_SELDT), scalar=0.0, in1=t_(T_L2), op0=ALU.max, op1=ALU.add))
                    own()
                    did(stt(out=t_(T_Z), in0=t_(T_AL), scalar=1.0e-4, in1=t_(T_Z), op0=ALU.add, op1=ALU.add))
                    own()
                    did(nc.vector.reciprocal(t_(T_L1), t_(T_Z)))
                    own()
                    did(stt(out=t_(T_L1), in0=t_(T_L1), scalar=dtc[:, 0:1], in1=t_(T_L2), op0=ALU.mult, op1=ALU.add))
                    own()
                    did(stt(out=t_(T_A), in0=t_(T_L1), scalar=0.5, in1=t_(T_AL), op0=ALU.mult, op1=ALU.mult))
                    did(stt(out=t_(T_W), in0=t_(T_L1), scalar=0.5, in1=t_(T_OM), op0=ALU.mult, op1=ALU.mult))
                    acts(19)
                    did(tt(t_(T_DET), t_(T_X), t_(T_Z), ALU.add))
                    did(tt(t_(T_LAM), t_(T_Y), t_(T_Z), ALU.add))
                    own()
                    did(nc.vector.reciprocal(t_(T_X), t_(T_DET)))
                    did(stt(out=t_(T_E1), in0=t_(T_E1), scalar=-1.0, in1=t_(T_Z), op0=ALU.mult, op1=ALU.subtract))
                    own()
                    did(stt(out=hq[:, V_A11, :], in0=t_(T_E1), scalar=1.0, in1=t_(T_X), op0=ALU.add, op1=ALU.mult))
                    did(stt(out=hq[:, V_A12, :], in0=t_(T_W), scalar=2.0, in1=t_(T_X), op0=ALU.mult, op1=ALU.mult))
                    did(tt(t_(T_LAM), t_(T_LAM), t_(T_X), ALU.mult))
                    own()
                    did(ts(t_(T_Y), t_(T_LAM), 0.0, None, ALU.is_gt))
                    did(ts(t_(T_E2), t_(T_LAM), 2.0 ** -63, None, ALU.max))
                    acts(20)
                    did(tt(t_(T_L1), t_(T_L1), t_(T_R), ALU.mult))
                    acts(21)
                    did(tt(t_(T_L2), t_(T_L2), t_(T_Y), ALU.mult))
                    own()
                    did(ts(t_(T_L2), t_(T_L2), -1.0, 1.0, ALU.mult, ALU.add))
                    own()
                    did(ts(t_(T_L2), t_(T_L2), 1.0e-6, None, ALU.max))
                    acts(22)
                    did(tt(hq[:, V_VF, :], t_(T_L1), t_(T_UG), ALU.mult))
                    assert count[0] == 23

            units = [(m, h) for m in range(KI) for h in range(HALF)]
            NU = len(units)
            d_order = []
            D1 = ["kh0", "kh1", "t1", "t2", "t3", "t4", "bk0", "bk1", "v"]
            D2 = ["m00", "m01", "m10", "m11"]
            PO = ["c0", "c1", "e00", "e01", "e10", "e11", "b0", "b1"]
            for n in range(NU + 1):
                d_order += [(n, o) for o in D1] if n < NU else []
                d_order += [(n - 1, o) for o in D2] if n else []
            ND, NP_ = len(d_order), NU * len(PO)
            d_at = {o: i + 1 for i, o in enumerate(d_order)}

            def p_at(n, o):
                return n * len(PO) + PO.index(o) + 1

            values = [V_SB0, V_SB1, V_A11, V_A12, V_BETA, V_VF]

            def vbank(n, v):
                return {V_SB0: c.bank[0][:, :], V_SB1: c.bank[1][:, :], V_BETA: c.bank[2][:, :], V_VF: c.bank[3][:, :],
                        V_A11: c.quad[n % 2], V_A12: c.quad[2 + n % 2]}[v]

            def vlast(n, v):
                return d_at[n, {V_SB0: "kh0", V_SB1: "kh1", V_A11: "m11", V_A12: "m10", V_BETA: "bk1", V_VF: "v"}[v]]

            def part(slot, n):
                m, h = units[n]
                return coef[:, slot, m * T + h * TT:m * T + (h + 1) * TT]

            def temp(n, i):
                return scr[:, ((n % 2) * 3 + i) * TT:((n % 2) * 3 + i + 1) * TT]

            with nc.Block() as block:
                @block.tensor
                def _(pe):
                    for n, (m, h) in enumerate(units):
                        for v in values:
                            back = 2 if v in (V_A11, V_A12) else 1
                            if n >= back:
                                pe.wait_ge(s["cd"], b * ND + vlast(n - back, v))
                            for t in range(2):
                                last = nc.tensor.matmul(vbank(n, v)[:, t * QW_:(t + 1) * QW_], spread[:, 2 * h + t, m, :],
                                                        hq[:, v, :], start=True, stop=True)
                            last.then_inc(s["cb"], 1)

                @block.vector
                def _(dve):
                    def cb(n, v):
                        dve.wait_ge(s["cb"], b * NU * 6 + n * 6 + values.index(v) + 1)

                    def own(n, o):
                        dve.wait_ge(s["cd"], b * ND + d_at[n, o])

                    def pool(n, o):
                        dve.wait_ge(s["cp"], b * NP_ + p_at(n, o))

                    mul = lambda out, a, bb: nc.vector.tensor_tensor(out, a, bb, ALU.mult)
                    for n, o in d_order:
                        m, h = units[n]
                        kh0, kh1, v_ = temp(n, 0), temp(n, 1), temp(n, 2)
                        if o == "kh0":
                            cb(n, V_SB0)
                            if n >= 2:
                                pool(n - 2, "b1")
                            op = mul(kh0, part(4, n), vbank(n, V_SB0))
                        elif o == "kh1":
                            cb(n, V_SB1)
                            op = mul(kh1, part(5, n), vbank(n, V_SB1))
                        elif o == "t1":
                            cb(n, V_A11)
                            own(n, "kh0")
                            op = mul(part(0, n), kh0, vbank(n, V_A11))
                        elif o == "t2":
                            cb(n, V_A12)
                            own(n, "kh1")
                            op = mul(part(1, n), kh1, vbank(n, V_A12))
                        elif o == "t3":
                            op = mul(part(2, n), kh0, vbank(n, V_A12))
                        elif o == "t4":
                            op = mul(part(3, n), kh1, vbank(n, V_A11))
                        elif o == "bk0":
                            cb(n, V_BETA)
                            own(n, "t3")
                            op = mul(kh0, kh0, vbank(n, V_BETA))
                        elif o == "bk1":
                            own(n, "t4")
                            op = mul(kh1, kh1, vbank(n, V_BETA))
                        elif o == "v":
                            cb(n, V_VF)
                            op = mul(v_, u[:, m, h * TT:(h + 1) * TT], vbank(n, V_VF))
                        else:
                            i = D2.index(o)
                            pool(n, "e" + o[1:])
                            a = vbank(n, V_A12 if o in ("m01", "m10") else V_A11)
                            if o == "m10":
                                op = nc.vector.scalar_tensor_tensor(out=part(i, n), in0=a, scalar=-1.0, in1=part(i, n),
                                                                    op0=ALU.mult, op1=ALU.subtract)
                            else:
                                op = nc.vector.tensor_tensor(part(i, n), a, part(i, n), ALU.subtract)
                        op.then_inc(s["cd"], 1)

                @block.gpsimd
                def _(pool):
                    def dve(n, o):
                        pool.wait_ge(s["cd"], b * ND + d_at[n, o])

                    def own(n, o):
                        pool.wait_ge(s["cp"], b * NP_ + p_at(n, o))

                    tt = nc.gpsimd.tensor_tensor
                    for n in range(NU):
                        bk0, bk1, v_ = temp(n, 0), temp(n, 1), temp(n, 2)
                        dve(n, "t3")
                        tt(part(4, n), part(0, n), part(1, n), ALU.subtract).then_inc(s["cp"], 1)
                        dve(n, "t4")
                        tt(part(5, n), part(2, n), part(3, n), ALU.add).then_inc(s["cp"], 1)
                        dve(n, "bk1")
                        own(n, "c1")
                        for i, (x_, y_) in enumerate(((bk0, 4), (bk0, 5), (bk1, 4), (bk1, 5))):
                            tt(part(i, n), x_, part(y_, n), ALU.mult).then_inc(s["cp"], 1)
                        dve(n, "v")
                        own(n, "e11")
                        tt(part(4, n), bk0, v_, ALU.mult).then_inc(s["cp"], 1)
                        tt(part(5, n), bk1, v_, ALU.mult).then_inc(s["cp"], 1)

            def at(slot, l):
                return coef[:, slot, :].rearrange("p (n l) -> p l n", l=L_STEP)[:, l, :]

            four = coef[:, 0:4, :].rearrange("p (i j) (n l) -> p l i j n", i=2, l=L_STEP)
            X = scr[:, 0:6 * NB].rearrange("p (i n q) -> p i n q", i=2, q=3)
            prod = scr[:, 1024:1024 + 12 * NB].rearrange("p (i n q j) -> p i n q j", i=2, q=3, j=2)
            starts = scr[:, 3072:3072 + (CHUNKS + 1) * KI * 3].rearrange("p (s m q) -> p s m q", m=KI, q=3)
            small = scr[:, 3600:3600 + KI * 6].rearrange("p (i m q) -> p i m q", i=2, q=3)
            sums = scr[:, 3840:3840 + 2 * NB].rearrange("p (i n) -> p i n", i=2)
            prev = scr[:, 768:768 + 2 * NB].rearrange("p (j n) -> p j n", j=2)
            cuts = [round(NB * x) for x in DVE_SHARE]
            dve_chains = [slice(x, y) for x, y in zip([0] + cuts[:-1], cuts)]
            pool_chains = [slice(cuts[-1], NB)]
            MATRIX, STATES = (L_STEP - 1) * 4, L_STEP * 4
            DVE_STEPS = 6 + len(dve_chains) * (MATRIX + STATES) + 2 + 2 * CHUNKS + 2
            POOL_STEPS = MATRIX + STATES
            offsets = coef[:, 4:6, :].rearrange("p i (n l) -> p l i n", l=L_STEP)
            p3 = scr[:, 1024:1024 + 4 * NB].rearrange("p (i n j) -> p i n j", i=2, j=2)
            w_q = weights[:, 0:2048]
            ybuf = coef[:, 0, :].rearrange("p (m t) -> p m t", m=KI)

            def matrix_step(tt, l, r, stage):
                if stage == 0:
                    x_t = X[:, :, r, :].rearrange("p j n q -> p n q j")
                    for i in range(2):
                        m_t = four[:, l, i, :, r].rearrange("p j n -> p n j").unsqueeze(2).broadcast_to([P, r.stop - r.start, 3, 2])
                        yield tt(prod[:, i, r, :, :], m_t, x_t, ALU.mult)
                elif stage == 1:
                    yield tt(X[:, :, r, :].rearrange("p i n q -> p i (n q)"), prod[:, :, r, :, 0].rearrange("p i n q -> p i (n q)"),
                             prod[:, :, r, :, 1].rearrange("p i n q -> p i (n q)"), ALU.add)
                else:
                    yield tt(X[:, :, r, 2], X[:, :, r, 2], offsets[:, l, :, r], ALU.add)

            def state_step(tt, l, r, stage):
                if stage == 0:
                    before = prev[:, :, r] if l == 0 else offsets[:, l - 1, :, r]
                    for i in range(2):
                        yield tt(p3[:, i, r, :].rearrange("p n j -> p j n"), four[:, l, i, :, r], before, ALU.mult)
                elif stage == 1:
                    yield tt(sums[:, :, r], p3[:, :, r, 0], p3[:, :, r, 1], ALU.add)
                else:
                    yield tt(offsets[:, l, :, r], sums[:, :, r], offsets[:, l, :, r], ALU.add)

            with nc.Block() as block:
                @block.sync
                def _(sp):
                    sp.dma_start(weights[:, 0:2048], A["r_q_w"][:, 0:2048]).then_inc(s["qload"], 16)
                    sp.wait_ge(s["d3"], b + 1)
                    sp.dma_start(weights[:, 0:2048], A["r_q_w"][:, 2048:4096]).then_inc(s["qload"], 16)

                @block.vector
                def _(dve):
                    tt = nc.vector.tensor_tensor
                    count = [0]

                    def did(op):
                        op.then_inc(s["x1"], 1)
                        count[0] += 1
                        return count[0]

                    def own(behind=None):
                        dve.wait_ge(s["x1"], b * DVE_STEPS + (count[0] if behind is None else behind))

                    for i in range(2):
                        for j in range(2):
                            did(nc.vector.tensor_copy(X[:, i, :, j], at(2 * i + j, 0)))
                        did(nc.vector.tensor_copy(X[:, i, :, 2], at(4 + i, 0)))
                    behind = [count[0]] * len(dve_chains)
                    for l in range(1, L_STEP):
                        for stage in range(3):
                            for x, r in enumerate(dve_chains):
                                own(behind[x])
                                for op in matrix_step(tt, l, r, stage):
                                    behind[x] = did(op)
                    did(nc.vector.memset(starts[:, :, :, :], 0.0))
                    own()
                    dve.wait_ge(s["xp"], b * POOL_STEPS + MATRIX)
                    for k in range(CHUNKS):
                        xs = X[:, :, :, :].rearrange("p i (m s) q -> p s i m q", m=KI)[:, k, :, :, :]
                        st = starts[:, k, :, :].unsqueeze(1).broadcast_to([P, 2, KI, 3])
                        if k == 0:
                            did(nc.vector.memset(starts[:, :, :, 2:3], 1.0))
                            own()
                        did(tt(small[:, :, :, :], xs, st, ALU.mult))
                        own()
                        did(nc.vector.tensor_reduce(starts[:, k + 1, :, 0:2].rearrange("p m i -> p i m"), small[:, :, :, :],
                                                    AX, ALU.add))
                        own()
                    for j in range(2):
                        did(nc.vector.tensor_copy(prev[:, j, :].rearrange("p (m s) -> p m s", m=KI),
                                                  starts[:, 0:CHUNKS, :, j].rearrange("p s m -> p m s")))
                    behind = [count[0]] * len(dve_chains)
                    for l in range(L_STEP):
                        for stage in range(3):
                            for x, r in enumerate(dve_chains):
                                own(behind[x])
                                for op in state_step(tt, l, r, stage):
                                    behind[x] = did(op)
                    assert count[0] == DVE_STEPS
                    own()
                    dve.wait_ge(s["xp"], (b + 1) * POOL_STEPS)
                    for n, (m, h) in enumerate(units):
                        dve.wait_ge(s["qmm"], b * NU + n + 1)
                        for j in range(2):
                            nc.vector.tensor_tensor(part(4 + j, n), part(4 + j, n), c.bank[2 * (n % 2) + j][:, :], ALU.mult)\
                                .then_inc(s["d1"], 1)
                        for j in range(2):
                            dve.wait_ge(s["d1"], b * NU * 4 + 4 * n + j + 1)
                            nc.vector.tensor_tensor(part(4 + j, n), part(4 + j, n), c.quad[2 * (n % 2) + j], ALU.mult)\
                                .then_inc(s["d1"], 1)

                @block.gpsimd
                def _(pool):
                    tt = nc.gpsimd.tensor_tensor
                    count = [0]

                    def own():
                        pool.wait_ge(s["xp"], b * POOL_STEPS + count[0])

                    pool.wait_ge(s["x1"], b * DVE_STEPS + 6)
                    for l in range(1, L_STEP):
                        for stage in range(3):
                            if count[0]:
                                own()
                            for op in matrix_step(tt, l, pool_chains[0], stage):
                                op.then_inc(s["xp"], 1)
                                count[0] += 1
                    pool.wait_ge(s["x1"], b * DVE_STEPS + (DVE_STEPS - len(dve_chains) * STATES))
                    for l in range(L_STEP):
                        for stage in range(3):
                            own()
                            for op in state_step(tt, l, pool_chains[0], stage):
                                op.then_inc(s["xp"], 1)
                                count[0] += 1
                    for n in range(NU):
                        pool.wait_ge(s["d1"], b * NU * 4 + 4 * n + 4)
                        nc.gpsimd.tensor_tensor(part(0, n), part(4, n), part(5, n), ALU.add).then_inc(s["d2"], 1)
                        if n == 0:
                            pool.sem_inc(s["passed"], 1)

                @block.tensor
                def _(pe):
                    for n, (m, h) in enumerate(units):
                        if n == 0:
                            pe.wait_ge(s["qload"], b * 32 + 16)
                        if n == NU // 2:
                            pe.wait_ge(s["qload"], b * 32 + 32)
                        if n >= 2:
                            pe.wait_ge(s["d1"], b * NU * 4 + 4 * (n - 2) + 4)
                        for j in range(2):
                            bank = c.quad[2 * (n % 2) + j]
                            for k in range(KI):
                                w_ = w_q.rearrange("p (m j k o) -> p m j k o", m=2, j=2, k=KI)[:, m % 2, j, k, :]
                                last = nc.tensor.matmul(bank, w_, u[:, k, h * TT:(h + 1) * TT], start=k == 0, stop=k == KI - 1)
                            bank = c.bank[2 * (n % 2) + j]
                            for t in range(2):
                                last = nc.tensor.matmul(bank[:, t * QW_:(t + 1) * QW_], spread[:, 2 * h + t, m, :],
                                                        hq[:, V_SC0 + j, :], start=True, stop=True)
                        last.then_inc(s["qmm"], 1)
                        if n == NU // 2 - 1:
                            pe.wait_ge(s["qmm"], b * NU + n + 1)
                            pe.sem_inc(s["d3"], 1)

            with nc.Block() as block:
                @block.scalar
                def _(act):
                    for m in range(KI):
                        nc.scalar.activation(scr[:, 0:T], ybuf[:, m, :], ACT.Copy, accum_out=stat[:, m, 0:1]).then_inc(s["g1"], 1)
                        act.wait_ge(s["g1"], b * 2 * KI + m + 1)
                    act.wait_ge(s["g2"], b * 2 + 1)
                    for m in range(KI):
                        nc.scalar.activation(scr[:, 0:T], ybuf[:, m, :], ACT.Square, bias=stat[:, m, 1:2],
                                             accum_out=stat[:, m, 2:3]).then_inc(s["g1"], 1)
                        act.wait_ge(s["g1"], b * 2 * KI + KI + m + 1)
                    act.wait_ge(s["g3"], b * 2 + 2)
                    nc.scalar.activation(stat[:, :, 3], c.quad[1][:, 0:KI], ACT.Sqrt, bias=eps[:, 1:2]).then_inc(s["g4"], 1)
                    act.wait_ge(s["g2"], b * 2 + 2)
                    for m in range(KI):
                        nc.scalar.activation(ybuf[:, m, :], ybuf[:, m, :], ACT.Identity, bias=stat[:, m, 6:7],
                                             scale=stat[:, m, 5:6]).then_inc(s["g5"], 1)

                @block.tensor
                def _(pe):
                    for i in range(2):
                        pe.wait_ge(s["g1"], b * 2 * KI + (i + 1) * KI)
                        nc.tensor.matmul(c.quad[i][:, 0:KI], group[:, :], stat[:, :, 2 * i], start=True, stop=True)\
                            .then_inc(s["g3"], 1)

                @block.vector
                def _(dve):
                    dve.wait_ge(s["g3"], b * 2 + 1)
                    nc.vector.tensor_scalar(stat[:, :, 1], c.quad[0][:, 0:KI], -1.0, None, ALU.mult).then_inc(s["g2"], 1)
                    dve.wait_ge(s["g4"], b + 1)
                    nc.vector.reciprocal(stat[:, :, 4], stat[:, :, 3]).then_inc(s["p3"], 1)
                    dve.wait_ge(s["p3"], b * (3 + 2 * KI) + 1)
                    nc.vector.tensor_tensor(stat[:, :, 5], stat[:, :, 4], vecs[:, :, 5], ALU.mult).then_inc(s["p3"], 1)
                    dve.wait_ge(s["p3"], b * (3 + 2 * KI) + 2)
                    nc.vector.tensor_tensor(stat[:, :, 7], stat[:, :, 5], stat[:, :, 1], ALU.mult).then_inc(s["p3"], 1)
                    dve.wait_ge(s["p3"], b * (3 + 2 * KI) + 3)
                    nc.vector.tensor_tensor(stat[:, :, 6], stat[:, :, 7], vecs[:, :, 6], ALU.add).then_inc(s["g2"], 1)
                    for m in range(KI):
                        dve.wait_ge(s["g5"], b * KI + m + 1)
                        nc.vector.tensor_tensor(ybuf[:, m, :], ybuf[:, m, :], z[:, m, :], ALU.mult).then_inc(s["p3"], 1)
                        dve.wait_ge(s["p3"], b * (3 + 2 * KI) + 3 + 2 * m + 1)
                        nc.vector.scalar_tensor_tensor(out=ybuf[:, m, :], in0=u[:, m, :], scalar=vecs[:, m, 7:8], in1=ybuf[:, m, :],
                                                       op0=ALU.mult, op1=ALU.add).then_inc(s["p3"], 1)
                    dve.wait_ge(s["p3"], (b + 1) * (3 + 2 * KI))
                    dve.sem_inc(s["passed"], 1)

                @block.sync
                def _(sp):
                    sp.dma_start(weights[:, 0:KI * D], A["r_out_w"]).then_inc(s["oload"], 16)

            w_o = weights[:, 0:KI * D].rearrange("p (k m) -> p k m", k=KI)
            with nc.Block() as block:
                @block.tensor
                def _(pe):
                    pe.wait_ge(s["oload"], b * 16 + 16)
                    for m in range(KD):
                        for h in range(HALF):
                            for k in range(KI):
                                last = nc.tensor.matmul(c.quad[m * HALF + h], w_o[:, k, m * P:(m + 1) * P],
                                                        ybuf[:, k, h * TT:(h + 1) * TT], start=k == 0, stop=k == KI - 1)
                            last.then_inc(s["omm"], 1)

                @block.vector
                def _(dve):
                    for m in range(KD):
                        x = tok(c.x, b)[:, m, :]
                        nc.vector.tensor_tensor(x, x, tok(c.h, b)[:, m, :], ALU.add).then_inc(s["oadd"], 1)
                    dve.wait_ge(s["oadd"], b * (KD + KD * HALF) + KD)
                    for m in range(KD):
                        for h in range(HALF):
                            dve.wait_ge(s["omm"], b * KD * HALF + m * HALF + h + 1)
                            x = tok(c.x, b)[:, m, h * TT:(h + 1) * TT]
                            nc.vector.tensor_tensor(x, c.quad[m * HALF + h], x, ALU.add).then_inc(s["oadd"], 1)


def gated_weight(c, A, v):
    nc = c.nc
    loaded, step, made, mm, ev = (c.sem(f"gw_{n}") for n in ("loaded", "step", "made", "mm", "ev"))
    with ExitStack() as ctx:
        w = c.sb("gw_w", [P, E, KD * D], ctx=ctx)
        mask = c.sb("gw_mask", [P, KD * D], ctx=ctx)
        bias = c.sb("gw_bias", [P, KD], ctx=ctx)
        w_b = c.sb("gw_w_b", [P, B, KD * D], ctx=ctx)
        with nc.Block() as block:
            @block.sync
            def _(sp):
                for dst, src in ((w[:, :, :], "L1_cond2_weight"), (mask[:, :], "L1_cond2_mask"), (bias[:, :], "L1_cond2_bias")):
                    sp.dma_start(dst, A[src]).then_inc(loaded, 16)

            @block.vector
            def _(dve):
                dve.wait_ge(loaded, 3 * 16)
                n = 0
                for g in range(E + 1):
                    for b in range(B):
                        if g:
                            dve.wait_ge(step, n - 1)
                        if g == 0:
                            op = nc.vector.tensor_scalar(w_b[:, b, :], w[:, 0, :], c.cond[:, b, 0:1], None, ALU.mult)
                        elif g < E:
                            op = nc.vector.scalar_tensor_tensor(out=w_b[:, b, :], in0=w[:, g, :], scalar=c.cond[:, b, g:g + 1],
                                                                in1=w_b[:, b, :], op0=ALU.mult, op1=ALU.add)
                        else:
                            op = nc.vector.tensor_tensor(w_b[:, b, :], w_b[:, b, :], mask[:, :], ALU.mult)
                        op.then_inc(step, 1)
                        n += 1

            @block.tensor
            def _(pe):
                n = 0
                for b in range(B):
                    pe.wait_ge(step, B * E + b + 1)
                    for t in range(T // TT):
                        for m in range(KD):
                            if n >= 4:
                                pe.wait_ge(ev, n - 3)
                            for k in range(KD):
                                last = nc.tensor.matmul(c.quad[n % 4], w_b[:, b, k * D + m * P:k * D + (m + 1) * P],
                                                        c.x[:, k, b * T + t * TT:b * T + (t + 1) * TT],
                                                        start=k == 0, stop=k == KD - 1)
                            last.then_inc(mm, 1)
                            n += 1

            @block.scalar
            def _(act):
                n = 0
                for b in range(B):
                    for t in range(T // TT):
                        for m in range(KD):
                            act.wait_ge(mm, n + 1)
                            nc.scalar.activation(v[:, m, b * T + t * TT:b * T + (t + 1) * TT], c.quad[n % 4],
                                                 ACT.Identity, bias=bias[:, m:m + 1]).then_inc(ev, 1)
                            n += 1


def layer_norm(c, A, tag, src, dst, params):
    nc = c.nc
    s = {n: c.sem(f"{tag}_{n}") for n in "loaded mm1 cen sq mm2 root rcp mul out".split()}
    with ExitStack() as ctx:
        vec = c.sb(f"{tag}_vec", [P, 2 * KD + 1], ctx=ctx)
        cen = c.sb(f"{tag}_cen", [P, NT, KD, TT], ctx=ctx)
        sq = c.sb(f"{tag}_sq", [P, NT, KD, TT], ctx=ctx)
        root = c.sb(f"{tag}_root", [P, NT, TT], ctx=ctx)
        rcp = c.sb(f"{tag}_rcp", [P, NT, TT], ctx=ctx)
        with nc.Block() as block:
            @block.sync
            def _(sp):
                sp.dma_start(vec[:, :], A[params]).then_inc(s["loaded"], 16)

            @block.tensor
            def _(pe):
                for t in range(NT):
                    for k in range(KD):
                        last = nc.tensor.matmul(c.quad[t], c.mean_ones[:, :], src[:, k, t * TT:(t + 1) * TT],
                                                start=k == 0, stop=k == KD - 1)
                    last.then_inc(s["mm1"], 1)
                for t in range(NT):
                    for k in range(KD):
                        pe.wait_ge(s["sq"], t * KD + k + 1)
                        last = nc.tensor.matmul(c.bank[t][:, :], c.mean_ones[:, :], sq[:, t, k, :],
                                                start=k == 0, stop=k == KD - 1)
                    last.then_inc(s["mm2"], 1)

            @block.vector
            def _(dve):
                dve.wait_ge(s["loaded"], 16)
                for t in range(NT):
                    dve.wait_ge(s["mm1"], t + 1)
                    for k in range(KD):
                        nc.vector.tensor_tensor(cen[:, t, k, :], src[:, k, t * TT:(t + 1) * TT], c.quad[t], ALU.subtract)\
                            .then_inc(s["cen"], 1)
                for t in range(NT):
                    dve.wait_ge(s["root"], t + 1)
                    nc.vector.reciprocal(rcp[:, t, :], root[:, t, :]).then_inc(s["rcp"], 1)
                    dve.wait_ge(s["rcp"], t + 1)
                    for k in range(KD):
                        nc.vector.scalar_tensor_tensor(out=cen[:, t, k, :], in0=cen[:, t, k, :], scalar=vec[:, k:k + 1],
                                                       in1=rcp[:, t, :], op0=ALU.mult, op1=ALU.mult).then_inc(s["mul"], 1)

            @block.scalar
            def _(act):
                act.wait_ge(s["loaded"], 16)
                for t in range(NT):
                    for k in range(KD):
                        act.wait_ge(s["cen"], t * KD + k + 1)
                        nc.scalar.activation(sq[:, t, k, :], cen[:, t, k, :], ACT.Square).then_inc(s["sq"], 1)
                for t in range(NT):
                    act.wait_ge(s["mm2"], t + 1)
                    nc.scalar.activation(root[:, t, :], c.bank[t][:, :], ACT.Sqrt, bias=vec[:, 2 * KD:2 * KD + 1])\
                        .then_inc(s["root"], 1)
                for t in range(NT):
                    for k in range(KD):
                        act.wait_ge(s["mul"], t * KD + k + 1)
                        nc.scalar.activation(dst[:, k, t * TT:(t + 1) * TT], cen[:, t, k, :], ACT.Identity,
                                             bias=vec[:, KD + k:KD + k + 1]).then_inc(s["out"], 1)


def router(c, A, v, table):
    nc = c.nc
    TL = N // P
    s = {n: c.sem(f"ro_{n}") for n in "loaded mm sc top idx gap exp den p1 p2 oh w tr cp out add".split()}
    with ExitStack() as ctx:
        gate = c.sb("ro_gate", [P, KD, E], ctx=ctx)
        number = c.sb("ro_number", [P, TL, E], ctx=ctx)
        score = c.sb("ro_score", [P, TL, E], ctx=ctx)
        top = c.sb("ro_top", [P, TL, 8], ctx=ctx)
        idx = c.sb("ro_idx", [P, TL, 8], U32, ctx=ctx)
        idx_f = c.sb("ro_idx_f", [P, TL, 2], ctx=ctx)
        prob = c.sb("ro_prob", [P, 4, TL], ctx=ctx)
        hot = c.sb("ro_hot", [P, 2, TL, E], ctx=ctx)
        w_t = c.sb("ro_w_t", [E, N], ctx=ctx)
        with nc.Block() as block:
            @block.sync
            def _(sp):
                sp.dma_start(gate[:, :, :], A["L1_ffn_gate_w"]).then_inc(s["loaded"], 16)
                sp.dma_start(number[:, :, :], A["number"]).then_inc(s["loaded"], 16)
                sp.wait_ge(s["cp"], 4)
                sp.dma_start(table, w_t[:, :]).then_inc(s["out"], 16)
                sp.wait_ge(s["out"], 16)

            @block.tensor
            def _(pe):
                pe.wait_ge(s["loaded"], 32)
                for t in range(TL):
                    for k in range(KD):
                        last = nc.tensor.matmul(c.quad[0][:, t * E:(t + 1) * E], c.h[:, k, t * P:(t + 1) * P], gate[:, k, :],
                                                start=k == 0, stop=k == KD - 1)
                last.then_inc(s["mm"], 1)
                pe.wait_ge(s["w"], 1)
                for q in range(4):
                    for t in range(4):
                        last = nc.tensor.transpose(c.bank[q][0:E, t * P:(t + 1) * P], hot[:, 0, 4 * q + t, :], c.ident[:, :])
                    last.then_inc(s["tr"], 1)

            @block.scalar
            def _(act):
                act.wait_ge(s["gap"], 1)
                nc.scalar.activation(prob[:, 1, :], prob[:, 0, :], ACT.Exp).then_inc(s["exp"], 1)
                for q in range(4):
                    act.wait_ge(s["tr"], q + 1)
                    nc.scalar.activation(w_t[:, q * 512:(q + 1) * 512], c.bank[q][0:E, :], ACT.Copy).then_inc(s["cp"], 1)

            @block.gpsimd
            def _(pool):
                for k in range(KD):
                    nc.gpsimd.tensor_tensor(c.x[:, k, :], c.x[:, k, :], v[:, k, :], ALU.add).then_inc(s["add"], 1)

            @block.vector
            def _(dve):
                dve.wait_ge(s["mm"], 1)
                nc.vector.tensor_copy(score[:, :, :].rearrange("p t e -> p (t e)"), c.quad[0][:, 0:TL * E]).then_inc(s["sc"], 1)
                dve.wait_ge(s["sc"], 1)
                for t in range(TL):
                    nc.vector.max(top[:, t, :], score[:, t, :]).then_inc(s["top"], 1)
                for t in range(TL):
                    dve.wait_ge(s["top"], t + 1)
                    nc.vector.max_index(idx[:, t, :], top[:, t, :], score[:, t, :]).then_inc(s["idx"], 1)
                nc.vector.tensor_tensor(prob[:, 0, :], top[:, :, 1], top[:, :, 0], ALU.subtract).then_inc(s["gap"], 1)
                dve.wait_ge(s["idx"], TL)
                nc.vector.tensor_copy(idx_f[:, :, :], idx[:, :, 0:2]).then_inc(s["idx"], 1)
                dve.wait_ge(s["exp"], 1)
                nc.vector.tensor_scalar(prob[:, 3, :], prob[:, 1, :], 1.0, None, ALU.add).then_inc(s["den"], 1)
                dve.wait_ge(s["den"], 1)
                nc.vector.reciprocal(prob[:, 2, :], prob[:, 3, :]).then_inc(s["p1"], 1)
                dve.wait_ge(s["p1"], 1)
                nc.vector.tensor_tensor(prob[:, 3, :], prob[:, 1, :], prob[:, 2, :], ALU.mult).then_inc(s["p2"], 1)
                dve.wait_ge(s["idx"], TL + 1)
                for i in range(2):
                    nc.vector.tensor_tensor(hot[:, i, :, :], number[:, :, :], idx_f[:, :, i:i + 1].broadcast_to([P, TL, E]),
                                            ALU.is_equal).then_inc(s["oh"], 1)
                dve.wait_ge(s["p2"], 1)
                for i in range(2):
                    dve.wait_ge(s["oh"], i + 1)
                    nc.vector.tensor_tensor(hot[:, i, :, :], hot[:, i, :, :],
                                            prob[:, 2 + i, :].unsqueeze(2).broadcast_to([P, TL, E]), ALU.mult)\
                        .then_inc(s["oh"], 1)
                dve.wait_ge(s["oh"], 4)
                nc.vector.tensor_tensor(hot[:, 0, :, :], hot[:, 0, :, :], hot[:, 1, :, :], ALU.add).then_inc(s["w"], 1)


def mixture(c, A, table):
    nc = c.nc
    part_done = c.sem("mx_part_done")
    with ExitStack() as ctx:
        x_hi = c.sb("mx_x_hi", [P, KD, N], F32R, ctx=ctx)
        x_lo = c.sb("mx_x_lo", [P, KD, N], F32R, ctx=ctx)
        wt = c.sb("mx_wt", [P, 2, N], ctx=ctx)
        part = c.sb("mx_part", [P, KD, TT], ctx=ctx)
        split(c, "mx", c.h, x_hi, x_lo)
        tiles = [[t * TT for t in range(NT)] for _ in range(2)]

        def source(sp, r, s):
            e = r * 2 + s
            return lambda p: A["L1_ffn_experts"][e, p, :, :]

        def load_extra(sp, r, s, unit, q):
            sp.wait_ge(q["extra_free"], r * 2 + s + 1)
            sp.dma_start(wt[:, s, :], table[bass.ds(r * 2 + s, 1), :].broadcast_to([P, N])).then_inc(q[f"extra{s}"], 16)

        def finish(dve, r, s, o, t0, psum, q):
            n = s * NT + t0 // TT
            if o == 0:
                dve.wait_ge(q[f"extra{s}"], r * 16 + 16)
            dve.wait_ge(q["y_part"], r * 2 * NT * KD + n * KD + o + 1)
            nc.vector.tensor_tensor(part[:, o, :], psum, wt[:, s, t0:t0 + TT], ALU.mult).then_inc(part_done, 1)
            dve.wait_ge(part_done, r * 2 * NT * KD + n * KD + o + 1)
            y = c.x[:, o, t0:t0 + TT]
            nc.vector.tensor_tensor(y, y, part[:, o, :], ALU.add).then_inc(q["y_part"], 1)
            if o == KD - 1:
                dve.wait_ge(q["y_part"], 1 + r * 2 * NT * KD + n * KD + o + 1)
                return dve
            return None

        gated_mlp(c, "mx", 4, 4, tiles, source, ACT.Silu, x_hi, x_lo, c.x, load_extra=load_extra, finish=finish)


def build(nc, A, out):
    table = nc.dram_tensor("expert_weights", [E, N], F32, kind="Internal").ap()
    with ExitStack() as ctx:
        c = Chip(nc, ctx)
        setup(c, A)
        merged_input(c, A)
        attention(c, A, "a0", "L0_qkv", "L0_wo", "zero_bias", c.x)
        two_of_eight(c, A)
        spectral(c, A)
        c.end_layer()
        chosen_expert(c, A)
        recurrent(c, A)
        last_branch(c, A, table)
        stored = c.sem("stored")
        with nc.Block() as block:
            @block.sync
            def _(sp):
                sp.dma_start(out, c.x[:, :, :]).then_inc(stored, 16)
                sp.wait_ge(stored, 16)


def last_branch(c, A, table):
    with ExitStack() as ctx:
        v = c.sb("branch", [P, KD, N], ctx=ctx)
        gated_weight(c, A, v)
        layer_norm(c, A, "n1", v, c.h, "L1_ffn_ln1")
        attention(c, A, "a1", "L1_qkv", "L1_wo", "L1_bo", v)
        layer_norm(c, A, "n2", v, c.h, "L1_ffn_ln2")
        router(c, A, v, table)
    mixture(c, A, table)



def _rows(w):
    return w.reshape(w.shape[0] // P, P, *w.shape[1:]).swapaxes(0, 1)


def _features(x):
    return _rows(x.transpose(2, 0, 1).reshape(x.shape[2], -1))


def _column(v):
    return v.reshape(-1, P).T


def _slots(w):
    out = np.zeros((w.shape[0], GROUPS, GH, SLOT), w.dtype)
    out[..., :HD] = w.reshape(w.shape[0], GROUPS, GH, HD)
    return out


def _split_places():
    place = np.full((2, P, 2), -1)
    for pair in range(2):
        for x in range(2):
            high, low = x * 64 + (32 if pair else 0), x * 64 + (0 if pair else 32)
            place[pair, high:high + HD] = (x, 0)
            place[pair, high + HD:high + 2 * HD] = (x, 1)
            place[pair, low:low + HD] = (x, 2)
            place[pair, low + HD:low + HD + 2] = (x, 3)
    return place


def _qkv(wq, wk, wv):
    place = _split_places()
    parts = []
    for w in (wk, wq):
        heads = w.reshape(D, GROUPS, 2, 2, HD)
        for pair in range(2):
            out = np.zeros((D, GROUPS, P), w.dtype)
            for r0 in range(0, P, HD):
                x, part = place[pair, r0]
                if part in (0, 1, 2):
                    out[:, :, r0:r0 + HD] = heads[:, :, pair, x, :]
            parts.append(out.reshape(KD, P, GROUPS, P).transpose(2, 1, 0, 3))
    parts.append(_slots(wv).reshape(KD, P, GROUPS, P).transpose(2, 1, 0, 3))
    return np.stack(parts, 2)


def _split_rows():
    part = _split_places()[:, :, 1]
    k_low, q_low = part == 1, part == 2
    cols = [1 - 2 * k_low, part == 3, k_low, 1 - 2 * q_low, q_low]
    return np.stack(cols, 2).transpose(1, 0, 2).astype(np.float32)


def _out_rows(w):
    out = np.zeros((GROUPS, GH, SLOT, D), w.dtype)
    out[:, :, :HD] = w.reshape(GROUPS, GH, HD, D)
    return out.reshape(GROUPS, P, D).transpose(1, 0, 2)


def _constants():
    f = np.float32
    ident = np.eye(P, dtype=f)
    row = np.arange(P)
    extra = (row % SLOT == HD)
    pick = (extra[:, None] & (row[:, None] // SLOT == np.arange(GH)[None, :])).astype(f)
    causal = np.zeros((P, T), f)
    causal[:, T - P:] = np.where(row[None, :] > row[:, None], -1.0e30, 0.0)
    freq = np.arange(D)
    angle = 2 * np.pi * ((freq[:, None] * freq[None, :]) % D) / D
    return {
        "ident": ident, "neg_ident": -ident, "mean_ones": np.full((P, P), 1.0 / D, f), "sum_pick": pick,
        "split_rows": _split_rows(), "causal": causal,
        "zero_bias": np.zeros((P, KD), f),
        "dft": np.stack([_rows(np.cos(angle).astype(f)), _rows(np.sin(angle).astype(f)), _rows(-np.sin(angle).astype(f))], 1),
    }


def _recurrent(i):
    f = np.float32
    a = {}
    w, bias = i["L1_attn_in_proj_W"], i["L1_attn_in_proj_b"]
    rows = np.concatenate([np.arange(3 * DI, 4 * DI), np.arange(DI, 3 * DI, 2), np.arange(DI + 1, 3 * DI, 2), np.arange(DI)])
    a["r_in_proj"] = _rows(w[rows].T).reshape(P, -1)
    a["r_in_bias"] = _column(bias[rows])
    cols = [*i["L1_attn_conv_w"].T, i["L1_attn_conv_b"], i["L1_attn_gn_w"], i["L1_attn_gn_b"], i["L1_attn_D"], i["L1_attn_D"]]
    a["r_vecs"] = np.stack([_column(v) for v in cols], 2)
    a["r_rms_w"] = _column(i["L1_attn_rms_w"])
    dyn, selb, selc = i["L1_attn_dyn_W"], i["L1_attn_selB_W"], i["L1_attn_selC_W"]
    heads = [dyn[:H], dyn[H:2 * H], dyn[2 * H:], selb[0::2], selb[1::2], selc[0::2], selc[1::2],
             i["L1_attn_seldt_W"], i["L1_attn_beta_W"], i["L1_attn_rg_W"], i["L1_attn_ug_W"]]
    a["r_head_w"] = _rows(np.concatenate(heads).T).reshape(P, -1)
    db = i["L1_attn_dyn_b"]
    hv = [db[:H], db[H:2 * H], db[2 * H:], i["L1_attn_dt_c"], i["L1_attn_beta_b"], i["L1_attn_rg_b"], i["L1_attn_ug_b"],
          i["L1_attn_ug_b"]]
    a["r_hvecs"] = np.tile(np.stack(hv, 1), (4, 1))
    q = i["L1_attn_Q_W"].reshape(KI, P, 2, KI, P).transpose(4, 0, 2, 3, 1)
    a["r_q_w"] = q.reshape(P, -1)
    a["r_out_w"] = _rows(i["L1_attn_out_W"].T).reshape(P, -1)
    row, ch = np.arange(P), np.arange(DI)
    spread = np.zeros((P, 4, KI, P), f)
    for t in range(4):
        for m in range(KI):
            spread[:, t, m, :] = row[:, None] == t * H + (ch[None, m * P:(m + 1) * P] // 16)
    a["r_spread"] = spread
    a["r_group"] = (row[:, None] // 16 == row[None, :] // 16).astype(f) / f(16 * T)
    rope = (f(1.0) / (f(10000.0) ** (np.arange(H, dtype=f) / f(H)))).astype(f)
    a["r_pos"] = (np.arange(T, dtype=f).reshape(4, 1, QW_) * rope[None, :, None]).reshape(P, QW_)
    a["r_eps"] = np.tile(np.array([[1e-6, 1e-5]], f), (P, 1))
    return a


def _lay_out(i):
    a = _constants()
    a["x"] = _features(i["x"])
    a["cond_all"] = np.broadcast_to(i["cond_8"][None], (P, B, E))
    a["cond_er"] = np.repeat(i["cond_8"].T, P // E, axis=0)
    a["L0_cond_As"] = i["L0_cond_As"].reshape(P, D)
    a["L0_cond_Bs"] = i["L0_cond_Bs"].transpose(0, 2, 1).reshape(P, D)
    a["L0_cond_W_base"] = _rows(i["L0_cond_W_base"].T)
    a["L0_cond_b_base"] = _column(i["L0_cond_b_base"])
    a["L0_qkv"] = _qkv(i["L0_attn_Wq"].T, i["L0_attn_Wk"].T, i["L0_attn_Wv"].T)
    a["L0_wo"] = _out_rows(i["L0_attn_Wo"].T)

    def parts(gate, up, down):
        def rows(w):
            return w.reshape(w.shape[0], -1, P, w.shape[2]).swapaxes(1, 2).reshape(w.shape[0], P, -1)
        return np.stack([rows(gate), rows(up), rows(down)], 1)

    a["L0_cond2_experts"] = np.concatenate([
        parts(i["L0_cond2_skill_gate"], i["L0_cond2_skill_up"], i["L0_cond2_skill_down"]),
        parts(i["L0_cond2_shared_gate"][None], i["L0_cond2_shared_up"][None], i["L0_cond2_shared_down"][None])])
    a["L0_ffn_wr"] = _rows(i["L0_ffn_w_freq_real"])
    a["L0_ffn_wi"] = _rows(i["L0_ffn_w_freq_imag"])
    a["L0_ffn_bias"] = _column(i["L0_ffn_bias"])
    a["L1_cond_experts"] = parts(*(i[f"L1_cond_W_{n}"].transpose(0, 2, 1) for n in ("up", "gate", "down")))
    a["L1_cond_biases"] = np.concatenate([i[f"L1_cond_b_{n}"].reshape(E, -1, P).swapaxes(1, 2)
                                          for n in ("up", "gate", "down")], 2)
    a.update(_recurrent(i))
    a["number"] = np.tile(np.arange(E, dtype=np.float32), (P, N // P, 1))
    a["L1_cond2_weight"] = _rows(i["L1_cond2_weight"].transpose(2, 0, 1)).transpose(0, 2, 1, 3).reshape(P, E, -1)
    a["L1_cond2_mask"] = _rows(i["L1_cond2_mask"].T).reshape(P, -1)
    a["L1_cond2_bias"] = _column(i["L1_cond2_bias"])
    eps = np.full((P, 1), 1e-5, np.float32)
    for n in ("ln1", "ln2"):
        a[f"L1_ffn_{n}"] = np.concatenate([_column(i[f"L1_ffn_{n}_scale"]), _column(i[f"L1_ffn_{n}_shift"]), eps], 1)
    a["L1_qkv"] = _qkv(i["L1_ffn_wq"], i["L1_ffn_wk"], i["L1_ffn_wv"])
    a["L1_wo"] = _out_rows(i["L1_ffn_wo"])
    a["L1_bo"] = _column(i["L1_ffn_bo"])
    a["L1_ffn_gate_w"] = _rows(i["L1_ffn_gate_w"])
    a["L1_ffn_experts"] = parts(i["L1_ffn_w1"], i["L1_ffn_w2"], i["L1_ffn_w3"])
    return a


def kernel(**inputs):
    import concourse.bacc as bacc
    from concourse.bass_utils import run_bass_kernel_spmd

    host = {n: np.asarray(x) for n, x in inputs.items()}
    arrays = {n: np.ascontiguousarray(x) for n, x in _lay_out(host).items()}
    nc = bacc.Bacc("TRN2", target_bir_lowering=False, num_devices=1)
    A = {n: nc.dram_tensor(f"in_{n}", x.shape, mybir.dt.from_np(x.dtype), kind="ExternalInput").ap() for n, x in arrays.items()}
    out = nc.dram_tensor("out_features", (P, KD, N), F32, kind="ExternalOutput").ap()
    build(nc, A, out)
    r = run_bass_kernel_spmd(nc, [{f"in_{n}": x for n, x in arrays.items()}], core_ids=[0])
    got = np.asarray(r.results[0]["out_features"])
    return got.transpose(1, 0, 2).reshape(D, B, T).transpose(1, 2, 0)
```
